# Optimizing a Trainium2 kernel written in Bass

```python
import numpy as np
import jax
import jax.numpy as jnp

def _softmax(x, axis=-1):
    return jax.nn.softmax(x, axis=axis)

def _gelu(x):
    return jax.nn.gelu(x, approximate=True)

def _silu(x):
    return jax.nn.silu(x)

def _sigmoid(x):
    return jax.nn.sigmoid(x)

def _layernorm(x, axis=-1, eps=1e-05):
    m = jnp.mean(x, axis=axis, keepdims=True)
    v = jnp.var(x, axis=axis, keepdims=True)
    return (x - m) / jnp.sqrt(v + eps)

def _scatter_add(tgt, idx, src, axis=0):
    return tgt.at[idx].add(src)

def _segment_sum(src, seg, n):
    return jax.ops.segment_sum(src, seg, n)
kernel_name = 'mk_gnn_resnorm_d4_gnn_r32_683e55'

def setup_inputs(seed: int=0):
    np.random.seed(seed)
    _w = jnp.asarray

    def _rec_inputs():
        import jax
        import jax.numpy as jnp
        _gk = jax.random.key(seed)
        x = -6.415e-05 + 1 * jax.random.normal(jax.random.fold_in(_gk, 1), (10000, 512), jnp.float32)
        src = jax.random.randint(jax.random.fold_in(_gk, 2), (10000,), 0, 10000, jnp.int32)
        dst = jax.random.randint(jax.random.fold_in(_gk, 3), (10000,), 0, 10000, jnp.int32)
        _o = jnp.argsort(dst, stable=True)
        src = src[_o]
        dst = dst[_o]
        edge_attr_64 = 0.000279952 + 1.00013 * jax.random.normal(jax.random.fold_in(_gk, 13), (10000, 64), jnp.float32)
        return (x, src, dst, edge_attr_64)
    x, src, dst, edge_attr_64 = _rec_inputs()

    def _L0_gnn_setup():
        import jax, jax.numpy as jnp
        import numpy as np
        N_NODES = 625
        N_EDGES = 10000
        HIDDEN = 512
        EDGE_DIM = 64
        LN_EPS = 1e-05

        def mish(x):
            return x * jnp.tanh(jax.nn.softplus(x))
        key = jax.random.key(seed)
        ks = jax.random.split(key, 8)
        s = lambda fan_in: 1.0 / np.sqrt(fan_in)
        return {'x': jax.random.normal(ks[0], (N_NODES, HIDDEN), dtype=jnp.float32), 'edge_index': jax.random.randint(ks[1], (2, N_EDGES), 0, N_NODES, dtype=jnp.int64), 'edge_attr': jax.random.normal(ks[2], (N_EDGES, EDGE_DIM), dtype=jnp.float32), 'W1': jax.random.normal(ks[3], (2 * HIDDEN + EDGE_DIM, HIDDEN), dtype=jnp.float32) * s(2 * HIDDEN + EDGE_DIM), 'b1': jnp.zeros((HIDDEN,), dtype=jnp.float32), 'W2': jax.random.normal(ks[4], (HIDDEN, HIDDEN), dtype=jnp.float32) * s(HIDDEN), 'b2': jnp.zeros((HIDDEN,), dtype=jnp.float32), 'W3': jax.random.normal(ks[5], (2 * HIDDEN, HIDDEN), dtype=jnp.float32) * s(2 * HIDDEN), 'b3': jnp.zeros((HIDDEN,), dtype=jnp.float32), 'W4': jax.random.normal(ks[6], (HIDDEN, HIDDEN), dtype=jnp.float32) * s(HIDDEN), 'b4': jnp.zeros((HIDDEN,), dtype=jnp.float32), 'gamma': jnp.ones((HIDDEN,), dtype=jnp.float32), 'beta': jnp.zeros((HIDDEN,), dtype=jnp.float32)}
    _L0_gnn_all = _L0_gnn_setup()
    _L0_gnn_in = {k: v for k, v in _L0_gnn_all.items() if k in ('W1', 'b1', 'W2', 'b2', 'W3', 'b3', 'W4', 'b4', 'gamma', 'beta')}
    del _L0_gnn_all

    def _L1_gnn_setup():
        import jax, jax.numpy as jnp
        import numpy as np
        B = 32
        MAXN = 64
        HEADS = 8
        DH = 64
        M = 256
        D = 512
        EPS = 1e-05
        KEPS = 1e-06

        def _batchnorm(x, g, b):
            mu = jnp.mean(x, axis=0)
            var = jnp.mean((x - mu) ** 2, axis=0)
            return (x - mu) * jax.lax.rsqrt(var + EPS) * g + b

        def _forward(x, batch, edge_index, norm1_g, norm1_b, norm2_g, norm2_b, W_conv, b_conv, Wq, Wk, Wv, Wo, proj):
            N = x.shape[0]
            E = edge_index.shape[1]
            h = x
            xn = _batchnorm(x, norm1_g, norm1_b)
            msg = xn[edge_index[0]]
            agg = jax.ops.segment_sum(msg, edge_index[1], num_segments=N)
            deg = jax.ops.segment_sum(jnp.ones((E,), x.dtype), edge_index[1], num_segments=N)
            agg = agg / jnp.maximum(deg, 1.0)[:, None]
            conv_out = jax.nn.relu(agg @ W_conv + b_conv)
            counts = jax.ops.segment_sum(jnp.ones((N,), jnp.int32), batch, num_segments=B)
            offsets = jnp.concatenate([jnp.zeros((1,), jnp.int32), jnp.cumsum(counts)[:-1]])
            pos = jnp.arange(N, dtype=jnp.int32) - offsets[batch]
            h_dense = jnp.zeros((B, MAXN, D), x.dtype).at[batch, pos].set(h)
            mask = jnp.zeros((B, MAXN), bool).at[batch, pos].set(True)

            def heads(t, W):
                return (t @ W).reshape(B, MAXN, HEADS, DH).transpose(0, 2, 1, 3)
            q, k, v = (heads(h_dense, Wq), heads(h_dense, Wk), heads(h_dense, Wv))
            scale = DH ** (-0.25)

            def phi(t, is_query):
                t = t * scale
                u = jnp.einsum('bhnd,md->bhnm', t, proj)
                diag = 0.5 * jnp.sum(t * t, axis=-1, keepdims=True)
                if is_query:
                    m_ = jnp.max(u, axis=-1, keepdims=True)
                else:
                    m_ = jnp.max(u, axis=(-2, -1), keepdims=True)
                return jnp.exp(u - diag - jax.lax.stop_gradient(m_)) / np.sqrt(M) + KEPS
            qf = phi(q, True)
            kf = phi(k, False) * mask[:, None, :, None]
            vm = v * mask[:, None, :, None]
            kv = jnp.einsum('bhnm,bhnd->bhmd', kf, vm)
            z = 1.0 / (jnp.einsum('bhnm,bhm->bhn', qf, kf.sum(axis=2)) + KEPS)
            attn = jnp.einsum('bhnm,bhmd->bhnd', qf, kv) * z[..., None]
            attn = attn.transpose(0, 2, 1, 3).reshape(B, MAXN, D) @ Wo
            h_attn = attn[batch, pos]
            return _batchnorm(conv_out + h_attn + h, norm2_g, norm2_b)
        key = jax.random.key(seed)
        ks = jax.random.split(key, 10)
        sizes = 1024 + np.arange(B) * 131 % 1025
        N = int(sizes.sum())
        E = N * 8
        batch = jnp.asarray(np.repeat(np.arange(B), sizes), dtype=jnp.int32)
        edge_index = jax.random.randint(ks[0], (2, E), 0, N, dtype=jnp.int32)
        s = 1.0 / np.sqrt(D)
        return {'x': jax.random.normal(ks[1], (N, D), jnp.float32), 'batch': batch, 'edge_index': edge_index, 'norm1_g': jnp.ones((D,), jnp.float32), 'norm1_b': jnp.zeros((D,), jnp.float32), 'norm2_g': jnp.ones((D,), jnp.float32), 'norm2_b': jnp.zeros((D,), jnp.float32), 'W_conv': jax.random.normal(ks[2], (D, D), jnp.float32) * s, 'b_conv': jnp.zeros((D,), jnp.float32), 'Wq': jax.random.normal(ks[3], (D, D), jnp.float32) * s, 'Wk': jax.random.normal(ks[4], (D, D), jnp.float32) * s, 'Wv': jax.random.normal(ks[5], (D, D), jnp.float32) * s, 'Wo': jax.random.normal(ks[6], (D, D), jnp.float32) * s, 'proj': jax.random.normal(ks[7], (M, DH), jnp.float32)}
    _L1_gnn_all = _L1_gnn_setup()
    _L1_gnn_in = {k: v for k, v in _L1_gnn_all.items() if k in ('norm1_g', 'norm1_b', 'norm2_g', 'norm2_b', 'W_conv', 'b_conv', 'Wq', 'Wk', 'Wv', 'Wo', 'proj')}
    del _L1_gnn_all

    def _L2_gnn_setup():
        import jax, jax.numpy as jnp
        import numpy as np
        N, E, H, D_IN, D_PRIME = (50000, 25000, 8, 512, 64)

        def _segment_softmax(scores, seg, num_segments):
            smax = jax.ops.segment_max(scores, seg, num_segments=num_segments)
            ex = jnp.exp(scores - smax[seg])
            denom = jax.ops.segment_sum(ex, seg, num_segments=num_segments)
            return ex / denom[seg]
        key = jax.random.key(seed)
        ks = jax.random.split(key, 6)
        x = jax.random.normal(ks[0], (N, D_IN), dtype=jnp.float32)
        edge_index = jax.random.randint(ks[1], (2, E), 0, N)
        Ws = jax.random.normal(ks[2], (H, D_IN, D_PRIME), dtype=jnp.float32) * 0.05
        Wb = jax.random.normal(ks[3], (H, D_PRIME), dtype=jnp.float32) * 0.05
        a_w = jax.random.normal(ks[4], (H, 2 * D_PRIME), dtype=jnp.float32) * 0.05
        a_b = jax.random.normal(ks[5], (H,), dtype=jnp.float32) * 0.05
        return dict(x=x, edge_index=edge_index, Ws=Ws, Wb=Wb, a_w=a_w, a_b=a_b)
    _L2_gnn_all = _L2_gnn_setup()
    _L2_gnn_in = {k: v for k, v in _L2_gnn_all.items() if k in ('Ws', 'Wb', 'a_w', 'a_b')}
    del _L2_gnn_all

    def _L3_gnn_setup():
        import jax, jax.numpy as jnp
        import numpy as np
        N_NODES = 50000
        N_EDGES = 25000
        D_IN = 512
        D_OUT = 512
        key = jax.random.key(seed)
        k1, k2, k3, k4, k5 = jax.random.split(key, 5)
        local_feats = jax.random.normal(k1, (N_NODES, D_IN), dtype=jnp.float32)
        src = jax.random.randint(k2, (N_EDGES,), 0, N_NODES, dtype=jnp.int64)
        dst = jax.random.randint(k3, (N_EDGES,), 0, N_NODES, dtype=jnp.int64)
        lim = (6.0 / (D_IN + D_OUT)) ** 0.5
        W_self = jax.random.uniform(k4, (D_OUT, D_IN), minval=-lim, maxval=lim, dtype=jnp.float32)
        W_neigh = jax.random.uniform(k5, (D_OUT, D_IN), minval=-lim, maxval=lim, dtype=jnp.float32)
        b = jnp.zeros((D_OUT,), dtype=jnp.float32)
        return {'local_feats': local_feats, 'src': src, 'dst': dst, 'layer': 0, 'W_self': W_self, 'W_neigh': W_neigh, 'b': b}
    _L3_gnn_all = _L3_gnn_setup()
    _L3_gnn_in = {k: v for k, v in _L3_gnn_all.items() if k in ('W_self', 'W_neigh', 'b')}
    del _L3_gnn_all
    return {'x': x, 'src': src, 'dst': dst, 'edge_attr_64': edge_attr_64, 'L0_gnn_W1': _L0_gnn_in['W1'], 'L0_gnn_b1': _L0_gnn_in['b1'], 'L0_gnn_W2': _L0_gnn_in['W2'], 'L0_gnn_b2': _L0_gnn_in['b2'], 'L0_gnn_W3': _L0_gnn_in['W3'], 'L0_gnn_b3': _L0_gnn_in['b3'], 'L0_gnn_W4': _L0_gnn_in['W4'], 'L0_gnn_b4': _L0_gnn_in['b4'], 'L0_gnn_gamma': _L0_gnn_in['gamma'], 'L0_gnn_beta': _L0_gnn_in['beta'], 'L1_gnn_norm1_g': _L1_gnn_in['norm1_g'], 'L1_gnn_norm1_b': _L1_gnn_in['norm1_b'], 'L1_gnn_norm2_g': _L1_gnn_in['norm2_g'], 'L1_gnn_norm2_b': _L1_gnn_in['norm2_b'], 'L1_gnn_W_conv': _L1_gnn_in['W_conv'], 'L1_gnn_b_conv': _L1_gnn_in['b_conv'], 'L1_gnn_Wq': _L1_gnn_in['Wq'], 'L1_gnn_Wk': _L1_gnn_in['Wk'], 'L1_gnn_Wv': _L1_gnn_in['Wv'], 'L1_gnn_Wo': _L1_gnn_in['Wo'], 'L1_gnn_proj': _L1_gnn_in['proj'], 'L2_gnn_Ws': _L2_gnn_in['Ws'], 'L2_gnn_Wb': _L2_gnn_in['Wb'], 'L2_gnn_a_w': _L2_gnn_in['a_w'], 'L2_gnn_a_b': _L2_gnn_in['a_b'], 'L3_gnn_W_self': _L3_gnn_in['W_self'], 'L3_gnn_W_neigh': _L3_gnn_in['W_neigh'], 'L3_gnn_b': _L3_gnn_in['b']}

def reference(x, src, dst, edge_attr_64, L0_gnn_W1, L0_gnn_b1, L0_gnn_W2, L0_gnn_b2, L0_gnn_W3, L0_gnn_b3, L0_gnn_W4, L0_gnn_b4, L0_gnn_gamma, L0_gnn_beta, L1_gnn_norm1_g, L1_gnn_norm1_b, L1_gnn_norm2_g, L1_gnn_norm2_b, L1_gnn_W_conv, L1_gnn_b_conv, L1_gnn_Wq, L1_gnn_Wk, L1_gnn_Wv, L1_gnn_Wo, L1_gnn_proj, L2_gnn_Ws, L2_gnn_Wb, L2_gnn_a_w, L2_gnn_a_b, L3_gnn_W_self, L3_gnn_W_neigh, L3_gnn_b):
    import jax
    import jax.numpy as jnp

    def _L0_gnn_ref(x, edge_index, edge_attr, W1, b1, W2, b2, W3, b3, W4, b4, gamma, beta):
        import jax, jax.numpy as jnp
        import numpy as np
        N_NODES = 625
        N_EDGES = 10000
        HIDDEN = 512
        EDGE_DIM = 64
        LN_EPS = 1e-05

        def mish(x):
            return x * jnp.tanh(jax.nn.softplus(x))
        src, dst = (edge_index[0], edge_index[1])
        edge_feat = jnp.concatenate([x[src], x[dst], edge_attr], axis=-1)
        h = mish(edge_feat @ W1 + b1)
        messages = mish(h @ W2 + b2)
        agg = jax.ops.segment_sum(messages, dst, num_segments=x.shape[0])
        u = mish(jnp.concatenate([x, agg], axis=-1) @ W3 + b3)
        out = u @ W4 + b4
        y = x + out
        mu = jnp.mean(y, axis=-1, keepdims=True)
        var = jnp.mean(jnp.square(y - mu), axis=-1, keepdims=True)
        return (y - mu) * jax.lax.rsqrt(var + LN_EPS) * gamma + beta

    def _L1_gnn_ref(x, batch, edge_index, norm1_g, norm1_b, norm2_g, norm2_b, W_conv, b_conv, Wq, Wk, Wv, Wo, proj):
        import jax, jax.numpy as jnp
        import numpy as np
        B = 32
        MAXN = 64
        HEADS = 8
        DH = 64
        M = 256
        D = 512
        EPS = 1e-05
        KEPS = 1e-06

        def _batchnorm(x, g, b):
            mu = jnp.mean(x, axis=0)
            var = jnp.mean((x - mu) ** 2, axis=0)
            return (x - mu) * jax.lax.rsqrt(var + EPS) * g + b

        def _forward(x, batch, edge_index, norm1_g, norm1_b, norm2_g, norm2_b, W_conv, b_conv, Wq, Wk, Wv, Wo, proj):
            N = x.shape[0]
            E = edge_index.shape[1]
            h = x
            xn = _batchnorm(x, norm1_g, norm1_b)
            msg = xn[edge_index[0]]
            agg = jax.ops.segment_sum(msg, edge_index[1], num_segments=N)
            deg = jax.ops.segment_sum(jnp.ones((E,), x.dtype), edge_index[1], num_segments=N)
            agg = agg / jnp.maximum(deg, 1.0)[:, None]
            conv_out = jax.nn.relu(agg @ W_conv + b_conv)
            counts = jax.ops.segment_sum(jnp.ones((N,), jnp.int32), batch, num_segments=B)
            offsets = jnp.concatenate([jnp.zeros((1,), jnp.int32), jnp.cumsum(counts)[:-1]])
            pos = jnp.arange(N, dtype=jnp.int32) - offsets[batch]
            h_dense = jnp.zeros((B, MAXN, D), x.dtype).at[batch, pos].set(h)
            mask = jnp.zeros((B, MAXN), bool).at[batch, pos].set(True)

            def heads(t, W):
                return (t @ W).reshape(B, MAXN, HEADS, DH).transpose(0, 2, 1, 3)
            q, k, v = (heads(h_dense, Wq), heads(h_dense, Wk), heads(h_dense, Wv))
            scale = DH ** (-0.25)

            def phi(t, is_query):
                t = t * scale
                u = jnp.einsum('bhnd,md->bhnm', t, proj)
                diag = 0.5 * jnp.sum(t * t, axis=-1, keepdims=True)
                if is_query:
                    m_ = jnp.max(u, axis=-1, keepdims=True)
                else:
                    m_ = jnp.max(u, axis=(-2, -1), keepdims=True)
                return jnp.exp(u - diag - jax.lax.stop_gradient(m_)) / np.sqrt(M) + KEPS
            qf = phi(q, True)
            kf = phi(k, False) * mask[:, None, :, None]
            vm = v * mask[:, None, :, None]
            kv = jnp.einsum('bhnm,bhnd->bhmd', kf, vm)
            z = 1.0 / (jnp.einsum('bhnm,bhm->bhn', qf, kf.sum(axis=2)) + KEPS)
            attn = jnp.einsum('bhnm,bhmd->bhnd', qf, kv) * z[..., None]
            attn = attn.transpose(0, 2, 1, 3).reshape(B, MAXN, D) @ Wo
            h_attn = attn[batch, pos]
            return _batchnorm(conv_out + h_attn + h, norm2_g, norm2_b)
        return _forward(x, batch, edge_index, norm1_g, norm1_b, norm2_g, norm2_b, W_conv, b_conv, Wq, Wk, Wv, Wo, proj)

    def _L2_gnn_ref(x, edge_index, Ws, Wb, a_w, a_b):
        import jax, jax.numpy as jnp
        import numpy as np
        N, E, H, D_IN, D_PRIME = (50000, 25000, 8, 512, 64)

        def _segment_softmax(scores, seg, num_segments):
            smax = jax.ops.segment_max(scores, seg, num_segments=num_segments)
            ex = jnp.exp(scores - smax[seg])
            denom = jax.ops.segment_sum(ex, seg, num_segments=num_segments)
            return ex / denom[seg]
        v_src, v_tgt = (edge_index[0], edge_index[1])
        n = x.shape[0]
        outs = []
        for h in range(Ws.shape[0]):
            Wx = x @ Ws[h] + Wb[h]
            d = Wx.shape[-1]
            s = Wx[v_tgt] @ a_w[h, :d] + Wx[v_src] @ a_w[h, d:] + a_b[h]
            s = jax.nn.leaky_relu(s, negative_slope=0.2)
            alpha = _segment_softmax(s, v_tgt, n)
            outs.append(jax.ops.segment_sum(alpha[:, None] * Wx[v_src], v_tgt, num_segments=n))
        return jnp.stack(outs, axis=1).reshape(n, -1)

    def _L3_gnn_ref(local_feats, src, dst, layer, W_self, W_neigh, b):
        import jax, jax.numpy as jnp
        import numpy as np
        N_NODES = 50000
        N_EDGES = 25000
        D_IN = 512
        D_OUT = 512
        'DistSAGEConv forward: mean neighbor aggregation + fc_self + fc_neigh + bias + ReLU.\n            `layer` only selects which hop in the distributed impl; aggregation math is identical.\n            '
        n = local_feats.shape[0]
        msg = local_feats[src]
        agg = jax.ops.segment_sum(msg, dst, num_segments=n)
        deg = jax.ops.segment_sum(jnp.ones((src.shape[0],), local_feats.dtype), dst, num_segments=n)
        h_neigh = agg / jnp.maximum(deg, 1.0)[:, None]
        rst = local_feats @ W_self.T + h_neigh @ W_neigh.T + b
        return jax.nn.relu(rst)
    edge_index = jnp.stack([src, dst])
    batch0 = jnp.zeros((10000,), jnp.int32)
    x = _layernorm(x + _L0_gnn_ref(x, edge_index, edge_attr_64, L0_gnn_W1, L0_gnn_b1, L0_gnn_W2, L0_gnn_b2, L0_gnn_W3, L0_gnn_b3, L0_gnn_W4, L0_gnn_b4, L0_gnn_gamma, L0_gnn_beta), axis=-1)
    x = _layernorm(x + _L1_gnn_ref(x, batch0, edge_index, L1_gnn_norm1_g, L1_gnn_norm1_b, L1_gnn_norm2_g, L1_gnn_norm2_b, L1_gnn_W_conv, L1_gnn_b_conv, L1_gnn_Wq, L1_gnn_Wk, L1_gnn_Wv, L1_gnn_Wo, L1_gnn_proj), axis=-1)
    x = _layernorm(x + _L2_gnn_ref(x, edge_index, L2_gnn_Ws, L2_gnn_Wb, L2_gnn_a_w, L2_gnn_a_b), axis=-1)
    x = _layernorm(x + _L3_gnn_ref(x, src, dst, 0, L3_gnn_W_self, L3_gnn_W_neigh, L3_gnn_b), axis=-1)
    return x

_drawn_inputs = setup_inputs


def setup_inputs(seed=0):
    import zlib

    import numpy as np

    out = dict(_drawn_inputs(seed))
    spreads = {'L0_gnn_b1': (0.0, 0.617),
     'L0_gnn_b2': (0.0, 0.446),
     'L0_gnn_b3': (0.0, 0.336),
     'L0_gnn_b4': (0.0, 0.304),
     'L0_gnn_gamma': (1.0, 0.2),
     'L0_gnn_beta': (0.0, 0.1),
     'L1_gnn_norm1_g': (1.0, 0.2),
     'L1_gnn_norm1_b': (0.0, 0.343),
     'L1_gnn_norm2_g': (1.0, 0.2),
     'L1_gnn_norm2_b': (0.0, 0.1),
     'L1_gnn_b_conv': (0.0, 0.446),
     'L3_gnn_b': (0.0, 0.1)}
    factors = {'L1_gnn_Wq': 8.0,
     'L1_gnn_Wk': 8.0,
     'L1_gnn_Wv': 64.0,
     'L1_gnn_Wo': 64.0,
     'L1_gnn_proj': 8.0,
     'L2_gnn_a_b': 22.482}
    for name, (base, spread) in spreads.items():
        noise = np.random.default_rng([zlib.crc32(name.encode()), seed]).standard_normal(out[name].shape)
        drawn = base * np.exp(spread * noise) if base else spread * noise
        out[name] = jnp.asarray(drawn.astype(out[name].dtype))
    for name, factor in factors.items():
        out[name] = (out[name] * factor).astype(out[name].dtype)
    return out
```

```python
from contextlib import ExitStack

import concourse.bass as bass
from concourse import mybir

F32 = mybir.dt.float32
BF16 = mybir.dt.bfloat16
F32R = mybir.dt.float32r
I32 = mybir.dt.int32
ALU = mybir.AluOpType
ACT = mybir.ActivationFunctionType

P = 128
N = 10000
E = 10000
D = 512
KC = D // P
DE = 64
NT = -(-N // P)
LAST = N - (NT - 1) * P
NP = NT * P
ET = P - 1
NET = -(-(E + 1) // ET)
NSORT = NET * ET + 1
NOKEY = NP - 1
ZROW = NET * P
SC = 80
SR = E // SC
HEADS = 8
DH = D // HEADS
GROUPS = P // HEADS
GT = -(-NET // GROUPS)
GE = GT * ET
EPS = 1e-5
EXP_AND_LN = 6
BIG = 1e30


def wait(eng, signal, value):
    if isinstance(value, int) and value <= 0:
        return
    eng.wait_ge(signal, value)


def over_tiles(eng, tiles, unroll, *stages):
    depth = max(lag for lag, _ in stages)
    first = min(-(-(depth + unroll + 1) // unroll) * unroll, tiles)
    last = first + max(tiles - 1 - first, 0) // unroll * unroll

    def peeled(t):
        for lag, fn in stages:
            if 0 <= t - lag < tiles:
                fn(t - lag, (t - lag) % unroll)

    for t in range(first):
        peeled(t)
    if last > first:
        with eng.Fori(0, (last - first) // unroll, 1) as turn:
            step = turn * unroll + first
            for u in range(unroll):
                for lag, fn in stages:
                    fn(step + (u - lag), (u - lag) % unroll)
    for t in range(last, tiles + depth):
        peeled(t)


def landed(t, slot, slots):
    if isinstance(t, int):
        return 16 * (t // slots + 1)
    return (t - slot) * (16 // slots) + 16


DMA_SIGNALS, SIGNALS = 8, 80


class Stage:

    def __init__(self, nc, name):
        self.nc, self.name, self.used, self.dmas = nc, name, 0, 0

    def __enter__(self):
        self.ctx = ExitStack()
        self.ctx.__enter__()
        return self

    def sb(self, name, shape, dt=F32):
        return self.ctx.enter_context(self.nc.sbuf_tensor(f"{self.name}_{name}", shape, dt))

    def ps(self, name, shape=(P, D), dt=F32):
        return self.ctx.enter_context(self.nc.psum_tensor(f"{self.name}_{name}", list(shape), dt))

    def sem(self, name):
        self.used += 1
        return SEMS[self.used - 1]

    def dma_sem(self, name):
        self.dmas += 1
        return DMA_SEMS[self.dmas - 1]

    def slots(self, make, name, n, *a):
        return [make(f"{name}{i}", *a) for i in range(n)]

    def __exit__(self, *exc):
        if exc[0] is None:
            ids = [s.num for s in DMA_SEMS[:self.dmas] + SEMS[:self.used]]
            if self.dmas:
                first = min(s.num for s in DMA_SEMS[:self.dmas])
                self.nc.gpsimd.dma_reset(range(first, first + self.dmas))
            self.nc.all_engine_barrier(sems_to_clear=range(min(ids), max(ids) + 1))
        return self.ctx.__exit__(*exc)


DMA_SEMS, SEMS = [], []


def row_of_all(v, parts=P):
    return bass.AP(tensor=v.tensor, offset=v.offset, ap=[[0, parts], [1, v.shape[-1]]])


def make_constants(nc, c):
    with Stage(nc, "constants") as st:
        done, copied = st.sem("const_made"), st.sem("const_copied")
        counts = st.sb("counts_i", [P, P], I32)
        with nc.Block() as block:
            @block.scalar
            def _(act):
                nc.scalar.add_instruction(mybir.InstLoadActFuncSet(name=nc.get_next_instruction_name(),
                                                                   act_func_set_id=EXP_AND_LN))

            @block.gpsimd
            def _(pool):
                nc.gpsimd.memset(c["ident"][:, :], 0.0).then_inc(done, 1)
                nc.gpsimd.memset(c["ones"][:, :], 1.0).then_inc(done, 1)
                nc.gpsimd.memset(c["below"][:, :], 1.0).then_inc(done, 1)
                nc.gpsimd.memset(c["upto"][:, :], 1.0).then_inc(done, 1)
                nc.gpsimd.memset(c["two"][:, :], 2.0)
                nc.gpsimd.memset(c["eps"][:, :], EPS)
                nc.gpsimd.iota(counts[:, :], [[1, P]], base=0, channel_multiplier=0).then_inc(done, 1)
                pool.wait_ge(done, 5)
                nc.gpsimd.affine_select(out=c["ident"][:, :], in_=c["ident"][:, :], compare_op=ALU.not_equal,
                                        fill=1.0, base=0, pattern=[[-1, P]], channel_multiplier=1)
                nc.gpsimd.affine_select(out=c["below"][:, :], in_=c["below"][:, :], compare_op=ALU.is_gt,
                                        fill=0.0, base=0, pattern=[[-1, P]], channel_multiplier=1)
                nc.gpsimd.affine_select(out=c["upto"][:, :], in_=c["upto"][:, :], compare_op=ALU.is_ge,
                                        fill=0.0, base=0, pattern=[[1, P]], channel_multiplier=-1)

            @block.vector
            def _(dve):
                dve.wait_ge(done, 5)
                nc.vector.tensor_copy(c["count"][:, :], counts[:, :]).then_inc(copied, 1)


def sort_edges(nc, c, src, dst, sorted_edges, edge_keys):
    with Stage(nc, "count") as st:
        dst_i, src_i = st.sb("dst_i", [SR, SC], I32), st.sb("src_i", [SR, SC], I32)
        hi_i, lo_i = st.sb("hi_i", [SR, SC], I32), st.sb("lo_i", [SR, SC], I32)
        dst_f, hi_f, lo_f = (st.sb(n, [SR, SC]) for n in ("dst_f", "hi_f", "lo_f"))
        rec = st.sb("rec", [SR, SC, 3], I32)
        hi_all = st.sb("hi_all", [SR, SC, NT], BF16)
        lo_all = st.sb("lo_all", [SR, SC, P], BF16)
        deg, ends, excl = st.sb("deg", [P, NT]), st.sb("ends", [P, NT]), st.sb("excl", [P, NT])
        first_pos = st.sb("first_pos", [P, NT])
        tmp = [st.sb(f"tmp{i}", [P, NT]) for i in range(3)]
        count = [st.sb(f"count{i}", [NT, P]) for i in range(2)]
        oh = [st.sb(f"oh{i}", [SR, NT]) for i in range(2)]
        ol = [st.sb(f"ol{i}", [SR, P]) for i in range(2)]
        dg = [st.sb(f"dg{i}", [SR, SR]) for i in range(2)]
        oht = [st.sb(f"oht{i}", [NT, SR]) for i in range(2)]
        junk = [st.sb(f"junk{i}", [SR, P]) for i in range(2)]
        before = [st.sb(f"before{i}", [SR, 2]) for i in range(2)]
        rank = st.sb("rank", [SR, SC])
        pos_i = [st.sb(f"pos_i{i}", [SR, 1], I32) for i in range(4)]
        rec_s = [st.sb(f"rec_s{i}", [SR, 3], I32) for i in range(4)]
        padding = st.sb("padding", [NSORT - 1 - E, 3], I32)
        p_hist, p_end = st.ps("p_hist"), st.ps("p_end")
        p_turn = [st.ps(f"p_turn{i}") for i in range(2)]
        p_tile = [st.ps(f"p_tile{i}") for i in range(2)]
        p_look = [st.ps(f"p_look{i}") for i in range(2)]
        loaded, split, hot, hist, prefix = (st.sem(n) for n in ("loaded", "split", "hot", "hist", "prefix"))
        end_sum, based, first_t = (st.sem(n) for n in ("end_sum", "based", "first_t"))
        hots, tile_hist, oht_made, g_done = (st.sem(n) for n in ("hots", "tile_hist", "oht_made", "g_done"))
        counted, picked, ranked = (st.sem(n) for n in ("counted", "picked", "ranked"))
        packed, staged = st.sem("packed"), st.sem("staged")
        scattered = [st.dma_sem(f"scattered{i}") for i in range(4)]
        padded = st.sem("padded")
        assert NT <= P and SR * SC == E

        with nc.Block() as block:
            @block.sync
            def _(sp):
                sp.dma_start(dst_i[:, :], dst.rearrange("(p t) -> p t", t=SC)).then_inc(loaded, 16)
                sp.dma_start(src_i[:, :], src.rearrange("(p t) -> p t", t=SC)).then_inc(loaded, 16)
                sp.wait_ge(packed, 5)
                sp.dma_start(sorted_edges[0:1, :], padding[0:1, :]).then_inc(padded, 16)
                sp.dma_start(sorted_edges[E + 1:NSORT, :], padding[:, :]).then_inc(padded, 16)
                sp.wait_ge(padded, 32)

            @block.vector
            def _(dve):
                dve.wait_ge(loaded, 32)
                nc.vector.tensor_scalar(hi_i[:, :], dst_i[:, :], 7, None, ALU.logical_shift_right).then_inc(split, 1)
                nc.vector.tensor_scalar(lo_i[:, :], dst_i[:, :], P - 1, None, ALU.bitwise_and).then_inc(split, 1)
                nc.vector.tensor_copy(dst_f[:, :], dst_i[:, :]).then_inc(split, 1)
                dve.wait_ge(split, 2)
                nc.vector.tensor_copy(hi_f[:, :], hi_i[:, :]).then_inc(split, 1)
                nc.vector.tensor_copy(lo_f[:, :], lo_i[:, :]).then_inc(split, 1)
                dve.wait_ge(split, 5)
                nc.vector.tensor_tensor(hi_all[:, :, :], hi_f[:, :].unsqueeze(2).to_broadcast([SR, SC, NT]),
                                        c["count"][0:SR, 0:NT].unsqueeze(1).to_broadcast([SR, SC, NT]),
                                        ALU.is_equal).then_inc(hot, 1)
                nc.vector.tensor_tensor(lo_all[:, :, :], lo_f[:, :].unsqueeze(2).to_broadcast([SR, SC, P]),
                                        c["count"][0:SR, :].unsqueeze(1).to_broadcast([SR, SC, P]),
                                        ALU.is_equal).then_inc(hot, 1)
                dve.wait_ge(hist, 1)
                nc.vector.tensor_copy(deg[:, :], p_hist[:, 0:NT]).then_inc(prefix, 1)
                dve.wait_ge(prefix, 1)
                nc.vector.tensor_tensor_scan(tmp[0][:, :], c["ones"][:, 0:NT], deg[:, :], 0.0,
                                             ALU.mult, ALU.add).then_inc(prefix, 1)
                dve.wait_ge(prefix, 2)
                nc.vector.tensor_tensor(excl[:, :], tmp[0][:, :], deg[:, :], ALU.subtract).then_inc(prefix, 1)
                dve.wait_ge(end_sum, 1)
                nc.vector.tensor_copy(ends[:, :], p_end[:, 0:NT]).then_inc(based, 1)
                dve.wait_ge(based, 1)
                nc.vector.scalar_tensor_tensor(first_pos[:, :], ends[:, :], 1.0, deg[:, :],
                                               ALU.add, ALU.subtract).then_inc(based, 1)
                nc.vector.tensor_scalar(tmp[1][:, :], ends[:, :], -64.0, 1.0 / ET, ALU.add, ALU.mult).then_inc(based, 1)
                dve.wait_ge(based, 3)
                nc.vector.tensor_scalar(tmp[0][:, :], tmp[1][:, :], 12582912.0, None, ALU.add).then_inc(based, 1)
                dve.wait_ge(based, 4)
                nc.vector.tensor_scalar(tmp[1][:, :], tmp[0][:, :], -12582912.0, None, ALU.add).then_inc(based, 1)
                dve.wait_ge(based, 5)
                nc.vector.scalar_tensor_tensor(tmp[2][:, :], tmp[1][:, :], float(-ZROW), ends[:, :],
                                               ALU.add, ALU.add).then_inc(based, 1)
                nc.vector.tensor_scalar(c["has_edges"][:, :], deg[:, :], 0.0, None, ALU.is_gt).then_inc(based, 1)
                nc.vector.tensor_scalar(tmp[0][:, :], deg[:, :], 1.0, None, ALU.max).then_inc(based, 1)
                dve.wait_ge(based, 8)
                nc.vector.reciprocal(c["inv_deg"][:, :], tmp[0][:, :]).then_inc(based, 1)
                nc.vector.tensor_tensor(tmp[1][:, :], tmp[2][:, :], c["has_edges"][:, :], ALU.mult).then_inc(based, 1)
                dve.wait_ge(based, 10)
                nc.vector.tensor_scalar(c["sum_row"][:, :], tmp[1][:, :], float(ZROW), None, ALU.add).then_inc(based, 1)
                dve.wait_ge(first_t, 1)
                nc.vector.tensor_copy(count[0][:, :], p_hist[0:NT, P:2 * P]).then_inc(counted, 1)

                def one_hots(t, s):
                    wait(dve, tile_hist, t - 1)
                    nc.vector.tensor_scalar(oh[s][:, :], c["count"][0:SR, 0:NT], hi_f[:, bass.ds(t, 1)], None,
                                            ALU.is_equal).then_inc(hots, 1)
                    nc.vector.tensor_scalar(ol[s][:, :], c["count"][0:SR, :], lo_f[:, bass.ds(t, 1)], None,
                                            ALU.is_equal).then_inc(hots, 1)
                    nc.vector.tensor_scalar(dg[s][:, :], c["ident"][0:SR, 0:SR], dst_f[:, bass.ds(t, 1)], None,
                                            ALU.mult).then_inc(hots, 1)

                def ranks(t, s):
                    wait(dve, tile_hist, t + 1)
                    wait(dve, g_done, t)
                    wait(dve, counted, t + 1)
                    nc.vector.tensor_tensor(count[1 - s][:, :], count[s][:, :], p_tile[s][0:NT, P:2 * P],
                                            ALU.add).then_inc(counted, 1)
                    wait(dve, g_done, t + 1)
                    nc.vector.tensor_tensor_reduce(out=junk[0][:, :], in0=p_look[s][0:SR, 0:P], in1=ol[s][:, :],
                                                   scale=1.0, scalar=0.0, op0=ALU.mult, op1=ALU.add,
                                                   accum_out=before[s][:, 0:1]).then_inc(picked, 1)
                    nc.vector.scalar_tensor_tensor(junk[1][:, 0:SR], p_tile[s][0:SR, 2 * P:2 * P + SR],
                                                   dst_f[:, bass.ds(t, 1)], c["below"][0:SR, 0:SR],
                                                   ALU.is_equal, ALU.mult,
                                                   accum_out=before[s][:, 1:2]).then_inc(picked, 1)
                    wait(dve, picked, 2 * t + 2)
                    nc.vector.tensor_tensor(rank[:, bass.ds(t, 1)], before[s][:, 0:1], before[s][:, 1:2],
                                            ALU.add).then_inc(ranked, 1)

                over_tiles(dve, SC, 2, (0, one_hots), (1, ranks))

            @block.tensor
            def _(pe):
                pe.wait_ge(hot, 2)
                nc.tensor.matmul(p_hist[:, 0:NT], lo_all[:, 0, :], hi_all[:, 0, :], start=True, stop=False)
                with pe.Fori(1, SC - 1, 1) as t:
                    nc.tensor.matmul(p_hist[:, 0:NT], lo_all[:, bass.ds(t, 1), :].rearrange("p o l -> p (o l)"),
                                     hi_all[:, bass.ds(t, 1), :].rearrange("p o l -> p (o l)"), start=False, stop=False)
                nc.tensor.matmul(p_hist[:, 0:NT], lo_all[:, SC - 1, :], hi_all[:, SC - 1, :],
                                 start=False, stop=True).then_inc(hist, 1)
                pe.wait_ge(prefix, 3)
                nc.tensor.matmul(p_end[:, 0:NT], c["upto"][:, :], deg[:, :], start=True, stop=False)
                nc.tensor.matmul(p_end[:, 0:NT], c["ones"][:, :], excl[:, :], start=False, stop=True).then_inc(end_sum, 1)
                pe.wait_ge(based, 2)
                nc.tensor.transpose(p_hist[0:NT, P:2 * P], first_pos[:, :], c["ident"][:, :]).then_inc(first_t, 1)

                def tile_histogram(t, s):
                    wait(pe, hots, 3 * t + 3)
                    wait(pe, ranked, t - 1)
                    wait(pe, oht_made, t - 1)
                    nc.tensor.transpose(p_turn[s][0:NT, 0:SR], oh[s][:, :], c["ident"][0:SR, 0:SR])
                    nc.tensor.matmul(p_tile[s][0:NT, P:2 * P], oh[s][:, :], ol[s][:, :], start=True, stop=True)
                    nc.tensor.matmul(p_tile[s][0:SR, 2 * P:2 * P + SR], c["ones"][0:SR, 0:SR], dg[s][:, :],
                                     start=True, stop=True).then_inc(tile_hist, 1)

                def look_up(t, s):
                    wait(pe, oht_made, t + 1)
                    wait(pe, counted, t + 1)
                    nc.tensor.matmul(p_look[s][0:SR, 0:P], oht[s][:, :], count[s][:, :],
                                     start=True, stop=True).then_inc(g_done, 1)

                over_tiles(pe, SC, 2, (0, tile_histogram), (1, look_up))

            @block.scalar
            def _(act):
                def copy_turned(t, s):
                    wait(act, tile_hist, t + 1)
                    wait(act, g_done, t - 1)
                    nc.scalar.copy(oht[s][:, :], p_turn[s][0:NT, 0:SR]).then_inc(oht_made, 1)

                over_tiles(act, SC, 2, (0, copy_turned))

            @block.gpsimd
            def _(pool):
                nc.gpsimd.iota(rec[:, :, 2], [[1, SC]], base=0, channel_multiplier=SC).then_inc(packed, 1)
                nc.gpsimd.memset(padding[:, 0:1], 0).then_inc(packed, 1)
                nc.gpsimd.memset(padding[:, 1:2], NOKEY).then_inc(packed, 1)
                nc.gpsimd.memset(padding[:, 2:3], 0).then_inc(packed, 1)
                pool.wait_ge(loaded, 32)
                pool.wait_ge(packed, 4)
                nc.gpsimd.tensor_copy(rec[:, :, 0], src_i[:, :]).then_inc(packed, 1)
                nc.gpsimd.tensor_copy(rec[:, :, 1], dst_i[:, :]).then_inc(packed, 1)
                pool.wait_ge(based, 11)
                nc.gpsimd.tensor_copy(c["sum_row_i"][:, :], c["sum_row"][:, :]).then_inc(packed, 1)
                pool.wait_ge(packed, 7)

                def send(t, s):
                    nc.gpsimd.indirect_dma_start(out=sorted_edges[:, :], in_=rec_s[s][:, :],
                                                 out_offset=bass.IndirectOffsetOnAxis(ap=pos_i[s][:, 0:1], axis=0),
                                                 in_offset=None).then_inc(scattered[s], 16)

                def stage_and_scatter(t, s):
                    wait(pool, staged, 2 * t)
                    wait(pool, ranked, t + 1)
                    wait(pool, scattered[s], landed(t, s, 4) - 16)
                    nc.gpsimd.tensor_copy(pos_i[s][:, :], rank[:, bass.ds(t, 1)]).then_inc(staged, 1)
                    nc.gpsimd.tensor_copy(rec_s[s][:, :], rec[:, bass.ds(t, 1), :].rearrange("p o c -> p (o c)"))\
                        .then_inc(staged, 1)
                    if not isinstance(t, int) or t > 0:
                        send(t - 1, (s - 1) % 4)

                over_tiles(pool, SC, 4, (0, stage_and_scatter))
                pool.wait_ge(staged, 2 * SC)
                send(SC - 1, (SC - 1) % 4)
                for s in range(4):
                    pool.wait_ge(scattered[s], 16 * SC // 4)

    with Stage(nc, "list") as st:
        lst = st.sb("lst", [P, NET, 3], I32)
        keys = c["keys"][:, 0:NET]
        key_rows = st.sb("key_rows", [NET, P])
        key_all = st.sb("key_all", [P, NET, P])
        p_key = st.ps("p_key")
        read, keyed, turned, rows, stored, spread = (st.sem(n) for n in
                                                     ("read", "keyed", "turned", "rows", "stored", "spread"))
        same = st.sem("same")
        body = sorted_edges[0:ET * NET, :].rearrange("(t p) c -> p t c", p=ET)
        tail = bass.AP(tensor=sorted_edges.tensor, offset=3 * ET, ap=[[3, 1], [3 * ET, NET], [1, 3]])

        with nc.Block() as block:
            @block.sync
            def _(sp):
                sp.dma_start(lst[0:ET, :, :], body).then_inc(read, 16)
                sp.dma_start(lst[ET:P, :, :], tail).then_inc(read, 16)
                sp.wait_ge(rows, 2)
                sp.dma_start(edge_keys, key_rows[:, :]).then_inc(stored, 16)
                sp.wait_ge(stored, 16)
                sp.dma_start(key_all[:, :, :], bass.AP(tensor=edge_keys.tensor, offset=edge_keys.offset,
                                                       ap=[[0, P], [P, NET], [1, P]])).then_inc(spread, 16)
                sp.wait_ge(spread, 16)

            @block.vector
            def _(dve):
                dve.wait_ge(read, 32)
                for n, name in enumerate(("src_list", "dst_list", "edge_list")):
                    nc.vector.tensor_copy(c[name][:, :], lst[:, :, n])
                nc.vector.memset(c["keys"][:, NET:], float(NOKEY))
                nc.vector.tensor_copy(keys, lst[:, :, 1]).then_inc(keyed, 1)
                dve.wait_ge(turned, 1)
                nc.vector.tensor_copy(key_rows[:, 1:P], p_key[0:NET, 1:P]).then_inc(rows, 1)
                nc.vector.tensor_copy(key_rows[:, 0:1], p_key[0:NET, P - 1:P]).then_inc(rows, 1)
                dve.wait_ge(spread, 16)
                nc.vector.tensor_tensor(c["same"][:, :, :], key_all[:, :, :],
                                        keys.unsqueeze(2).to_broadcast([P, NET, P]),
                                        ALU.is_equal).then_inc(same, 1)

            @block.tensor
            def _(pe):
                pe.wait_ge(keyed, 1)
                nc.tensor.transpose(p_key[0:NET, 0:P], keys, c["ident"][:, :]).then_inc(turned, 1)


def load_weights(eng, sem, pairs):
    for tile, w in pairs:
        eng.dma_start(tile, w.rearrange("(k p) n -> p k n", p=P)).then_inc(sem, 16)


class Halves:

    def __init__(self, st, name, shape, slots=2):
        self.hi = st.slots(st.sb, name + "_hi", slots, shape, F32R)
        self.lo = st.slots(st.sb, name + "_lo", slots, shape, F32R)
        self.hi_made, self.made = st.sem(name + "_hi_made"), st.sem(name + "_made")


def split_weights(nc, st, name, w):
    halves = Halves(st, name, w.shape, 1)

    def fill(dve):
        for k in range(w.shape[1]):
            nc.vector.tensor_copy(halves.hi[0][:, k, :], w[:, k, :]).then_inc(halves.hi_made, 1)
            dve.wait_ge(halves.hi_made, k + 1)
            nc.vector.tensor_tensor(halves.lo[0][:, k, :], w[:, k, :], halves.hi[0][:, k, :], ALU.subtract)\
                .then_inc(halves.made, 1)

    return halves, fill


def multiply_halves(nc, out, x, s, x_blocks, w, w_blocks):
    pairs = list(zip(x_blocks, w_blocks))
    products = [(x.lo[s], w.hi[0], pair) for pair in pairs]
    products += [(x.hi[s], half, pair) for pair in pairs for half in (w.lo[0], w.hi[0])]
    for n, (x_half, w_half, (i, j)) in enumerate(products):
        ins = nc.tensor.matmul(out, x_half[:, i, :], w_half[:, j, :], start=n == 0, stop=n == len(products) - 1)
    return ins


def copy_blocks(nc, dest, bank):
    return nc.scalar.copy(dest, bank[:, :].rearrange("p (k m) -> p k m", k=KC))


def rest_of_blocks(nc, lo, bank, hi):
    return nc.vector.tensor_tensor(lo, bank[:, :].rearrange("p (k m) -> p k m", k=KC), hi, ALU.subtract)


def rows(dram, t):
    return dram[bass.ds(t * P, P), :]


def node_products(nc, c, x, attr, W1, b1, from_src, from_dst, attrT):
    with Stage(nc, "products") as st:
        w = st.sb("w", [P, 2 * KC, D])
        bias = st.sb("bias", [P, D])
        xt = st.slots(st.sb, "xt", 2, [P, D])
        xT = Halves(st, "xT", [P, KC, P])
        w_halves, fill_w = split_weights(nc, st, "w", w)
        res = [st.slots(st.sb, f"res{n}_", 2, [P, D]) for n in range(2)]
        p_turn = st.slots(st.ps, "p_turn", 2)
        p_out = [st.slots(st.ps, f"p_out{n}_", 2) for n in range(2)]
        weights, zeroed = st.sem("weights"), st.sem("zeroed")
        idx = st.slots(st.sb, "idx", 4, [P, 1], I32)
        attr_rows = st.slots(st.sb, "attr", 4, [P, DE])
        p_attr = st.slots(st.ps, "p_attr", 2)
        staged, attr_turned, attrT_made = (st.sem(n) for n in ("staged", "attr_turned", "attrT_made"))
        attr_in = st.slots(st.dma_sem, "attr_in", 4)
        x_in = st.slots(st.sem, "x_in", 2)
        turned = st.sem("turned")
        product, evacuated = st.slots(st.sem, "product", 2), st.slots(st.sem, "evacuated", 2)
        stored = [st.slots(st.sem, f"stored{n}_", 2) for n in range(2)]

        with nc.Block() as block:
            @block.sync
            def _(sp):
                load_weights(sp, weights, [(w[:, :, :], W1[0:2 * D, :])])
                sp.dma_start(bias[:, :], row_of_all(b1)).then_inc(weights, 16)
                sp.wait_ge(zeroed, 2)

                def load(t, s):
                    wait(sp, turned, t - 1)
                    if isinstance(t, int) and t == NT - 1:
                        sp.dma_start(xt[s][0:LAST, :], x[t * P:N, :]).then_inc(x_in[s], 16)
                    else:
                        sp.dma_start(xt[s][:, :], rows(x, t)).then_inc(x_in[s], 16)

                def store(t, s):
                    for n, dram in enumerate((from_src, from_dst)):
                        wait(sp, evacuated[n], t + 1)
                        sp.dma_start(rows(dram, t), res[n][s][:, :]).then_inc(stored[n][s], 16)

                over_tiles(sp, NT, 2, (0, load), (2, store))
                for s in range(2):
                    for n in range(2):
                        sp.wait_ge(stored[n][s], 16 * len(range(s, NT, 2)))

            @block.gpsimd
            def _(pool):
                for s in range(2):
                    nc.gpsimd.memset(xt[s][:, :], 0.0).then_inc(zeroed, 1)

                def gather(t, s):
                    nc.gpsimd.indirect_dma_start(out=attr_rows[s][:, :], in_=attr[:, :], out_offset=None,
                                                 in_offset=bass.IndirectOffsetOnAxis(ap=idx[s][:, 0:1], axis=0))\
                        .then_inc(attr_in[s], 16)

                def stage_and_gather(t, s):
                    wait(pool, staged, t)
                    wait(pool, attr_turned, t - 4)
                    wait(pool, attr_in[s], landed(t, s, 4) - 16)
                    nc.gpsimd.tensor_copy(idx[s][:, :], c["edge_list"][:, bass.ds(t, 1)]).then_inc(staged, 1)
                    if not isinstance(t, int) or t > 0:
                        gather(t - 1, (s - 1) % 4)

                over_tiles(pool, NET, 4, (0, stage_and_gather))
                pool.wait_ge(staged, NET)
                pool.wait_ge(attr_turned, NET - 4)
                gather(NET - 1, (NET - 1) % 4)

            @block.tensor
            def _(pe):
                pe.wait_ge(w_halves.made, 2 * KC)

                def turn(t, s):
                    wait(pe, x_in[s], landed(t, s, 2))
                    wait(pe, xT.made, t - 1)
                    for k in range(KC):
                        ins = nc.tensor.transpose(p_turn[s][:, k * P:(k + 1) * P], xt[s][:, k * P:(k + 1) * P],
                                                  c["ident"][:, :])
                    ins.then_inc(turned, 1)

                def multiply(t, s):
                    wait(pe, xT.made, t + 1)
                    for n in range(2):
                        wait(pe, evacuated[n], t - 1)
                        multiply_halves(nc, p_out[n][s][:, :], xT, s, range(KC), w_halves,
                                        range(n * KC, (n + 1) * KC)).then_inc(product[n], 1)

                def turn_attr(t, s):
                    wait(pe, attr_in[s], landed(t, s, 4))
                    wait(pe, attrT_made, t - 1)
                    nc.tensor.matmul(p_attr[s % 2][0:DE, 0:P], attr_rows[s][:, :], c["ident"][:, :],
                                     start=True, stop=True)\
                        .then_inc(attr_turned, 1)

                over_tiles(pe, NT, 4, (0, lambda t, s: turn(t, s % 2)), (1, lambda t, s: multiply(t, s % 2)),
                           (4, turn_attr))

            @block.scalar
            def _(act):
                def copy_turned(t, s):
                    wait(act, turned, t + 1)
                    wait(act, product[1], t - 1)
                    copy_blocks(nc, xT.hi[s][:, :, :], p_turn[s]).then_inc(xT.hi_made, 1)

                def evacuate(t, s):
                    wait(act, product[1], t + 1)
                    wait(act, stored[1][s], landed(t, s, 2) - 16)
                    nc.scalar.copy(res[1][s][:, :], p_out[1][s][:, :]).then_inc(evacuated[1], 1)

                def copy_attr(t, s):
                    wait(act, attr_turned, t + 1)
                    nc.scalar.copy(attrT[:, bass.ds(t, 1), :].rearrange("p o m -> p (o m)"), p_attr[s][0:DE, 0:P])\
                        .then_inc(attrT_made, 1)

                over_tiles(act, NT, 2, (0, copy_turned), (1, evacuate), (5, copy_attr))

            @block.vector
            def _(dve):
                dve.wait_ge(weights, 32)
                fill_w(dve)

                def rest(t, s):
                    wait(dve, xT.hi_made, t + 1)
                    wait(dve, product[1], t - 1)
                    rest_of_blocks(nc, xT.lo[s][:, :, :], p_turn[s], xT.hi[s][:, :, :]).then_inc(xT.made, 1)

                def evacuate(t, s):
                    wait(dve, product[0], t + 1)
                    wait(dve, stored[0][s], landed(t, s, 2) - 16)
                    nc.vector.tensor_tensor(res[0][s][:, :], p_out[0][s][:, :], bias[:, :], ALU.add)\
                        .then_inc(evacuated[0], 1)

                over_tiles(dve, NT, 2, (0, rest), (1, evacuate))


class Mish:

    def __init__(self, nc, st, name, slots=2):
        self.nc, self.n = nc, slots
        self.z = st.slots(st.sb, name + "_z", slots, [P, D])
        self.w = st.slots(st.sb, name + "_w", slots, [P, D])
        self.z_made, self.exp_made, self.d_made = (st.sem(f"{name}_{n}") for n in ("z_made", "exp_made", "d_made"))
        self.log_made, self.inv_made, self.share_made = (st.sem(f"{name}_{n}")
                                                         for n in ("log_made", "inv_made", "share_made"))
        self.made = st.sem(name + "_made")

    def exp(self, act, t, s):
        wait(act, self.z_made, t + 1)
        wait(act, self.made, t - self.n + 1)
        self.nc.scalar.activation(self.w[s][:, :], self.z[s][:, :], ACT.Exp).then_inc(self.exp_made, 1)

    def product(self, dve, t, s):
        wait(dve, self.exp_made, t + 1)
        self.nc.vector.scalar_tensor_tensor(self.w[s][:, :], self.w[s][:, :], 2.0, self.w[s][:, :],
                                            ALU.add, ALU.mult).then_inc(self.d_made, 1)

    def log(self, act, t, s):
        wait(act, self.d_made, t + 1)
        self.nc.scalar.activation(self.w[s][:, :], self.w[s][:, :], ACT.Ln, bias=self.two[:, 0:1])\
            .then_inc(self.log_made, 1)

    def inverse(self, act, t, s):
        wait(act, self.log_made, t + 1)
        self.nc.scalar.activation(self.w[s][:, :], self.w[s][:, :], ACT.Exp, scale=-1.0).then_inc(self.inv_made, 1)

    def share(self, dve, t, s):
        wait(dve, self.inv_made, t + 1)
        self.nc.vector.scalar_tensor_tensor(self.w[s][:, :], self.w[s][:, :], -2.0, self.z[s][:, :],
                                            ALU.mult, ALU.mult).then_inc(self.share_made, 1)

    def finish(self, eng, engine, out, t, s):
        wait(eng, self.share_made, t + 1)
        engine.tensor_tensor(out, self.w[s][:, :], self.z[s][:, :], ALU.add).then_inc(self.made, 1)


def edge_messages(nc, c, from_src, from_dst, attrT, W1, W2, b2, sums):
    with Stage(nc, "messages") as st:
        w1 = st.sb("w1", [DE, D])
        w2 = st.sb("w2", [P, KC, D])
        bias = st.sb("bias", [P, D])
        idx = [st.slots(st.sb, f"idx{n}_", 4, [P, 1], I32) for n in range(2)]
        part = [st.slots(st.sb, f"part{n}_", 4, [P, D]) for n in range(2)]
        at = st.slots(st.sb, "at", 2, [DE, P])
        first, second = Mish(nc, st, "first"), Mish(nc, st, "second")
        first.two = second.two = c["two"]
        h = st.slots(st.sb, "h", 2, [P, D])
        hT = Halves(st, "hT", [P, KC, P])
        w2_halves, fill_w2 = split_weights(nc, st, "w2", w2)
        msg = st.slots(st.sb, "msg", 2, [P, D])
        same = st.slots(st.sb, "same", 2, [P, P])
        res = st.slots(st.sb, "res", 2, [P, D])
        zeros = st.sb("zeros", [1, D])
        p_z, p_turn = st.slots(st.ps, "p_z", 2), st.slots(st.ps, "p_turn", 2)
        p_m, p_sum = st.slots(st.ps, "p_m", 2), st.slots(st.ps, "p_sum", 2)
        weights, zeroed, zero_row = st.sem("weights"), st.sem("zeroed"), st.sem("zero_row")
        staged, at_made, z_product, parts_added = (st.sem(n) for n in
                                                   ("staged", "at_made", "z_product", "parts_added"))
        gathered = [st.slots(st.dma_sem, f"gathered{n}_", 4) for n in range(2)]
        turned, m_product, same_made = (st.sem(n) for n in ("turned", "m_product", "same_made"))
        carried, summed, evacuated = st.sem("carried"), st.sem("summed"), st.sem("evacuated")
        stored = st.slots(st.sem, "stored", 2)

        with nc.Block() as block:
            @block.sync
            def _(sp):
                sp.dma_start(w1[:, :], W1[2 * D:2 * D + DE, :]).then_inc(weights, 16)
                load_weights(sp, weights, [(w2[:, :, :], W2)])
                sp.dma_start(bias[:, :], row_of_all(b2)).then_inc(weights, 16)
                sp.wait_ge(zeroed, 1)
                sp.dma_start(sums[ZROW:ZROW + 1, :], zeros[:, :]).then_inc(zero_row, 16)
                sp.wait_ge(zero_row, 16)

                def store(t, s):
                    wait(sp, evacuated, t + 1)
                    sp.dma_start(rows(sums, t), res[s][:, :]).then_inc(stored[s], 16)

                over_tiles(sp, NET, 2, (8, store))
                for s in range(2):
                    sp.wait_ge(stored[s], 16 * len(range(s, NET, 2)))

            @block.gpsimd
            def _(pool):
                nc.gpsimd.memset(zeros[:, :], 0.0).then_inc(zeroed, 1)

                def gather(t, s):
                    for n, table in enumerate((from_src, from_dst)):
                        nc.gpsimd.indirect_dma_start(out=part[n][s][:, :], in_=table[:, :], out_offset=None,
                                                     in_offset=bass.IndirectOffsetOnAxis(ap=idx[n][s][:, 0:1], axis=0))\
                            .then_inc(gathered[n][s], 16)

                def stage_and_gather(t, s):
                    wait(pool, staged, 2 * t)
                    wait(pool, first.z_made, t - 4)
                    for n, lst in enumerate(("src_list", "dst_list")):
                        wait(pool, gathered[n][s], landed(t, s, 4) - 16)
                        nc.gpsimd.tensor_copy(idx[n][s][:, :], c[lst][:, bass.ds(t, 1)]).then_inc(staged, 1)
                    if not isinstance(t, int) or t > 0:
                        gather(t - 1, (s - 1) % 4)

                def last_gather():
                    pool.wait_ge(staged, 2 * NET)
                    pool.wait_ge(first.z_made, NET - 4)
                    gather(NET - 1, (NET - 1) % 4)

                def copy_attr(t, s):
                    if isinstance(t, int) and t == NET - 1:
                        last_gather()
                    wait(pool, z_product, t - 1)
                    nc.gpsimd.tensor_copy(at[s % 2][:, :], attrT[:, bass.ds(t, 1), :].rearrange("p o m -> p (o m)"))\
                        .then_inc(at_made, 1)

                def add_parts(t, s):
                    for n in range(2):
                        wait(pool, gathered[n][s], landed(t, s, 4))
                    nc.gpsimd.tensor_tensor(part[0][s][:, :], part[0][s][:, :], part[1][s][:, :], ALU.add)\
                        .then_inc(parts_added, 1)

                def finish_first(t, s):
                    wait(pool, turned, t - 1)
                    first.finish(pool, nc.gpsimd, h[s % 2][:, :], t, s % 2)

                over_tiles(pool, NET, 4, (0, stage_and_gather), (1, copy_attr), (3, add_parts), (4, finish_first))

            @block.vector
            def _(dve):
                dve.wait_ge(weights, 48)
                fill_w2(dve)

                def rest_of_h(t, s):
                    wait(dve, hT.hi_made, t + 1)
                    wait(dve, m_product, t - 1)
                    rest_of_blocks(nc, hT.lo[s % 2][:, :, :], p_turn[s % 2], hT.hi[s % 2][:, :, :]).then_inc(hT.made, 1)

                def first_z(t, s):
                    wait(dve, z_product, t + 1)
                    wait(dve, parts_added, t + 1)
                    wait(dve, first.made, t - 1)
                    nc.vector.tensor_tensor(first.z[s % 2][:, :], p_z[s % 2][:, :], part[0][s][:, :], ALU.add)\
                        .then_inc(first.z_made, 1)

                def second_z(t, s):
                    wait(dve, m_product, t + 1)
                    wait(dve, second.made, t - 1)
                    nc.vector.tensor_tensor(second.z[s % 2][:, :], p_m[s % 2][:, :], bias[:, :], ALU.add)\
                        .then_inc(second.z_made, 1)

                def spread_same(t, s):
                    wait(dve, summed, t - 1)
                    nc.vector.tensor_copy(same[s % 2][:, :], c["same"][:, bass.ds(t, 1), :]
                                          .rearrange("p o m -> p (o m)")).then_inc(same_made, 1)

                def finish_second(t, s):
                    wait(dve, summed, t - 1)
                    second.finish(dve, nc.vector, msg[s % 2][:, :], t, s % 2)

                over_tiles(dve, NET, 4, (4, first_z), (7, second_z), (5, rest_of_h), (7, spread_same),
                           (4, lambda t, s: first.product(dve, t, s % 2)),
                           (7, lambda t, s: second.product(dve, t, s % 2)),
                           (4, lambda t, s: first.share(dve, t, s % 2)),
                           (7, lambda t, s: second.share(dve, t, s % 2)), (7, finish_second))

            @block.scalar
            def _(act):
                def copy_turned(t, s):
                    wait(act, turned, t + 1)
                    wait(act, m_product, t - 1)
                    copy_blocks(nc, hT.hi[s % 2][:, :, :], p_turn[s % 2]).then_inc(hT.hi_made, 1)

                def carry(t, s):
                    wait(act, second.made, t + 1)
                    wait(act, summed, t)
                    source = zeros[0:1, :] if isinstance(t, int) and t == 0 else p_sum[(s - 1) % 2][0:1, :]
                    nc.scalar.copy(msg[s % 2][0:1, :], source).then_inc(carried, 1)

                def evacuate(t, s):
                    wait(act, summed, t + 1)
                    wait(act, stored[s % 2], landed(t, s % 2, 2) - 16)
                    nc.scalar.copy(res[s % 2][:, :], p_sum[s % 2][:, :]).then_inc(evacuated, 1)

                act.wait_ge(zeroed, 1)
                over_tiles(act, NET, 4, (8, carry), (5, copy_turned),
                           (4, lambda t, s: first.exp(act, t, s % 2)), (7, lambda t, s: second.exp(act, t, s % 2)),
                           (4, lambda t, s: first.log(act, t, s % 2)), (4, lambda t, s: first.inverse(act, t, s % 2)),
                           (7, lambda t, s: second.log(act, t, s % 2)), (7, lambda t, s: second.inverse(act, t, s % 2)),
                           (9, evacuate))

            @block.tensor
            def _(pe):
                pe.wait_ge(weights, 48)
                pe.wait_ge(w2_halves.made, KC)

                def attr_product(t, s):
                    wait(pe, at_made, t + 1)
                    wait(pe, first.z_made, t - 1)
                    nc.tensor.matmul(p_z[s % 2][:, :], at[s % 2][:, :], w1[:, :], start=True, stop=True)\
                        .then_inc(z_product, 1)

                def turn(t, s):
                    wait(pe, first.made, t + 1)
                    wait(pe, hT.made, t - 1)
                    for k in range(KC):
                        ins = nc.tensor.transpose(p_turn[s % 2][:, k * P:(k + 1) * P], h[s % 2][:, k * P:(k + 1) * P],
                                                  c["ident"][:, :])
                    ins.then_inc(turned, 1)

                def multiply(t, s):
                    wait(pe, hT.made, t + 1)
                    wait(pe, second.z_made, t - 1)
                    multiply_halves(nc, p_m[s % 2][:, :], hT, s % 2, range(KC), w2_halves, range(KC))\
                        .then_inc(m_product, 1)

                def add_up(t, s):
                    wait(pe, same_made, t + 1)
                    wait(pe, carried, t + 1)
                    wait(pe, evacuated, t - 1)
                    nc.tensor.matmul(p_sum[s % 2][:, :], same[s % 2][:, :], msg[s % 2][:, :], start=True, stop=True)\
                        .then_inc(summed, 1)

                over_tiles(pe, NET, 4, (3, attr_product), (5, turn), (8, add_up), (6, multiply))


def segment_sums(nc, c, name, table, sums, weights=None):
    with Stage(nc, name) as st:
        U = 4
        idx = st.slots(st.sb, "idx", U, [P, 1], I32)
        msg = st.slots(st.sb, "msg", U, [P, D])
        same = st.slots(st.sb, "same", U, [P, P])
        res = st.slots(st.sb, "res", U, [P, D])
        p_sum = st.slots(st.ps, "p_sum", U)
        zeros = st.sb("zeros", [1, D])
        staged, same_made, summed = st.sem("staged"), st.sem("same_made"), st.sem("summed")
        carried, evacuated, weighted, zeroed = (st.sem(n) for n in ("carried", "evacuated", "weighted", "zeroed"))
        zero_row = st.sem("zero_row")
        gathered, stored = st.slots(st.dma_sem, "gathered", U), st.slots(st.sem, "stored", U)
        if weights is not None:
            msg_in = st.slots(st.sb, "msg_in", U, [P, D])

        with nc.Block() as block:
            @block.gpsimd
            def _(pool):
                dest = msg if weights is None else msg_in
                nc.gpsimd.memset(zeros[:, :], 0.0).then_inc(zeroed, 1)

                def gather(t, s):
                    nc.gpsimd.indirect_dma_start(out=dest[s][:, :], in_=table[:, :], out_offset=None,
                                                 in_offset=bass.IndirectOffsetOnAxis(ap=idx[s][:, 0:1], axis=0))\
                        .then_inc(gathered[s], 16)

                def stage_and_gather(t, s):
                    wait(pool, staged, t)
                    if weights is None:
                        wait(pool, summed, t - U)
                    else:
                        wait(pool, weighted, t - U)
                    wait(pool, gathered[s], landed(t, s, U) - 16)
                    nc.gpsimd.tensor_copy(idx[s][:, :], c["src_list"][:, bass.ds(t, 1)]).then_inc(staged, 1)
                    if not isinstance(t, int) or t > 0:
                        gather(t - 1, (s - 1) % U)

                over_tiles(pool, NET, U, (0, stage_and_gather))
                pool.wait_ge(staged, NET)
                wait(pool, summed if weights is None else weighted, NET - U)
                gather(NET - 1, (NET - 1) % U)

            @block.vector
            def _(dve):
                def spread_same(t, s):
                    wait(dve, summed, t - U + 1)
                    nc.vector.tensor_copy(same[s][:, :], c["same"][:, bass.ds(t, 1), :]
                                          .rearrange("p o m -> p (o m)")).then_inc(same_made, 1)

                def evacuate(t, s):
                    wait(dve, summed, t + 1)
                    wait(dve, carried, min(t + 2, NET) if isinstance(t, int) else t + 2)
                    wait(dve, stored[s], landed(t, s, U) - 16)
                    nc.vector.tensor_copy(res[s][:, :], p_sum[s][:, :]).then_inc(evacuated, 1)

                def weigh(t, s):
                    wait(dve, gathered[s], landed(t, s, U))
                    wait(dve, summed, t - U + 1)
                    nc.vector.tensor_tensor(msg[s][:, :].rearrange("p (h d) -> p h d", h=HEADS),
                                            msg_in[s][:, :].rearrange("p (h d) -> p h d", h=HEADS),
                                            weights[:, bass.ds(t, 1), :].rearrange("p o h -> p (o h)")
                                            .unsqueeze(2).to_broadcast([P, HEADS, DH]),
                                            ALU.mult).then_inc(weighted, 1)

                if weights is None:
                    over_tiles(dve, NET, U, (0, spread_same), (1, evacuate))
                else:
                    over_tiles(dve, NET, U, (0, spread_same), (0, weigh), (1, evacuate))

            @block.tensor
            def _(pe):
                def add_up(t, s):
                    wait(pe, same_made, t + 1)
                    wait(pe, carried, t + 1)
                    wait(pe, evacuated, t - U + 1)
                    nc.tensor.matmul(p_sum[s][:, :], same[s][:, :], msg[s][:, :], start=True, stop=True)\
                        .then_inc(summed, 1)

                over_tiles(pe, NET, U, (0, add_up))

            @block.scalar
            def _(act):
                act.wait_ge(zeroed, 1)

                def carry(t, s):
                    if weights is None:
                        wait(act, gathered[s], landed(t, s, U))
                    else:
                        wait(act, weighted, t + 1)
                    wait(act, summed, t)
                    source = zeros[0:1, :] if isinstance(t, int) and t == 0 else p_sum[(s - 1) % U][0:1, :]
                    nc.scalar.copy(msg[s][0:1, :], source).then_inc(carried, 1)

                over_tiles(act, NET, U, (0, carry))

            @block.sync
            def _(sp):
                sp.wait_ge(zeroed, 1)
                sp.dma_start(sums[ZROW:ZROW + 1, :], zeros[:, :]).then_inc(zero_row, 16)
                sp.wait_ge(zero_row, 16)

                def store(t, s):
                    wait(sp, evacuated, t + 1)
                    sp.dma_start(rows(sums, t), res[s][:, :]).then_inc(stored[s], 16)

                over_tiles(sp, NET, U, (0, store))
                for s in range(U):
                    sp.wait_ge(stored[s], 16 * len(range(s, NET, U)))


class LayerNorm:

    def __init__(self, nc, st, c, name, slots=2):
        self.nc, self.n, self.eps = nc, slots, c["eps"]
        self.spare = st.sb(name + "_spare", [P, 1])
        self.stats = st.slots(st.sb, name + "_stats", slots, [P, 6])
        self.moments = st.slots(st.sb, name + "_moments", slots, [P, 2])
        self.inv = st.slots(st.sb, name + "_inv", slots, [P, 1])
        self.stats_made, self.moments_made, self.log_made = (st.sem(f"{name}_{n}") for n in
                                                             ("stats_made", "moments_made", "log_made"))
        self.inv_made, self.made = st.sem(name + "_inv_made"), st.sem(name + "_made")

    def sums(self, dve, v, t, s):
        self.nc.vector.bn_stats(self.stats[s][:, :], v).then_inc(self.stats_made, 1)
        wait(dve, self.stats_made, t + 1)
        self.nc.vector.memset(self.spare[:, :], 0.0)
        self.nc.vector.bn_aggr(self.moments[s][:, :], self.stats[s][:, :]).then_inc(self.moments_made, 1)

    def root(self, act, t, s):
        wait(act, self.moments_made, t + 1)
        wait(act, self.made, t - self.n + 1)
        self.nc.scalar.activation(self.inv[s][:, :], self.moments[s][:, 1:2], ACT.Ln, bias=self.eps[:, 0:1])\
            .then_inc(self.log_made, 1)
        wait(act, self.log_made, t + 1)
        self.nc.scalar.activation(self.inv[s][:, :], self.inv[s][:, :], ACT.Exp, scale=-0.5).then_inc(self.inv_made, 1)

    def scale(self, dve, out, v, t, s):
        wait(dve, self.inv_made, t + 1)
        self.nc.vector.tensor_scalar(out, v, self.moments[s][:, 0:1], self.inv[s][:, 0:1],
                                     ALU.subtract, ALU.mult).then_inc(self.made, 1)


class NodeGather:

    def __init__(self, nc, st, c, sums, used, name="agg"):
        self.nc, self.c, self.sums, self.used = nc, c, sums, used
        self.idx = st.slots(st.sb, name + "_idx", 4, [P, 1], I32)
        self.rows = st.slots(st.sb, name, 4, [P, D])
        self.staged = st.sem(name + "_staged")
        self.landed = st.slots(st.dma_sem, name + "_landed", 4)

    def _gather(self, t, s):
        self.nc.gpsimd.indirect_dma_start(out=self.rows[s][:, :], in_=self.sums[:, :], out_offset=None,
                                          in_offset=bass.IndirectOffsetOnAxis(ap=self.idx[s][:, 0:1], axis=0))\
            .then_inc(self.landed[s], 16)

    def stage_and_gather(self, pool, t, s):
        wait(pool, self.staged, t)
        wait(pool, self.used, t - 4)
        wait(pool, self.landed[s], landed(t, s, 4) - 16)
        self.nc.gpsimd.tensor_copy(self.idx[s][:, :], self.c["sum_row_i"][:, bass.ds(t, 1)]).then_inc(self.staged, 1)
        if not isinstance(t, int) or t > 0:
            self._gather(t - 1, (s - 1) % 4)
        if isinstance(t, int) and t == NT - 1:
            pool.wait_ge(self.staged, NT)
            pool.wait_ge(self.used, NT - 4)
            self._gather(t, s)


def turn_blocks(nc, c, p_turn, v):
    for k in range(KC):
        ins = nc.tensor.transpose(p_turn[:, k * P:(k + 1) * P], v[:, k * P:(k + 1) * P], c["ident"][:, :])
    return ins


def column_stats(nc, c, stats, p_turn, t):
    count = LAST if isinstance(t, int) and t == NT - 1 else P
    for k in range(KC):
        ins = nc.vector.bn_stats(stats[:, k, bass.ds(t, 1), :].rearrange("p o f -> p (o f)"),
                                 p_turn[:, k * P:k * P + count])
    return ins


def update_nodes(nc, c, x, sums, W3, b3, W4, b4, gamma, beta, x1, stats):
    with Stage(nc, "update") as st:
        w3, w4 = st.sb("w3", [P, 2 * KC, D]), st.sb("w4", [P, KC, D])
        vecs = {n: st.sb(n, [P, D]) for n in ("b3", "b4", "gamma", "beta")}
        xt, again = st.slots(st.sb, "xt", 2, [P, D]), st.slots(st.sb, "again", 4, [P, D])
        xaT = Halves(st, "xaT", [P, 2 * KC, P])
        w3_halves, fill_w3 = split_weights(nc, st, "w3", w3)
        w4_halves, fill_w4 = split_weights(nc, st, "w4", w4)
        mish = Mish(nc, st, "mish")
        mish.two = c["two"]
        u, uT = st.slots(st.sb, "u", 2, [P, D]), Halves(st, "uT", [P, KC, P])
        y, y_norm = st.slots(st.sb, "y", 2, [P, D]), st.slots(st.sb, "y_norm", 2, [P, D])
        res = st.slots(st.sb, "res", 2, [P, D])
        p_x, p_agg, p_uT, p_res = (st.ps(n) for n in ("p_x", "p_agg", "p_uT", "p_res"))
        p_u, p_out = st.slots(st.ps, "p_u", 2), st.slots(st.ps, "p_out", 2)
        weights, zeroed = st.sem("weights"), st.sem("zeroed")
        x_in, again_in = st.slots(st.sem, "x_in", 2), st.slots(st.sem, "again_in", 4)
        stored = st.slots(st.sem, "stored", 2)
        turned, u_product, u_turned, out_product = (
            st.sem(n) for n in ("turned", "u_product", "u_turned", "out_product"))
        y_step, scaled, shifted, summed = (st.sem(n) for n in ("y_step", "scaled", "shifted", "summed"))
        res_turned, counted = st.sem("res_turned"), st.sem("counted")
        agg = NodeGather(nc, st, c, sums, turned)
        norm_y, norm_x = LayerNorm(nc, st, c, "norm_y"), LayerNorm(nc, st, c, "norm_x")

        with nc.Block() as block:
            @block.sync
            def _(sp):
                load_weights(sp, weights, [(w3[:, :, :], W3), (w4[:, :, :], W4)])
                for n, v in (("b3", b3), ("b4", b4), ("gamma", gamma), ("beta", beta)):
                    sp.dma_start(vecs[n][:, :], row_of_all(v)).then_inc(weights, 16)
                sp.wait_ge(zeroed, 6)

                def load_rows(dest, done, t, s):
                    if isinstance(t, int) and t == NT - 1:
                        sp.dma_start(dest[s][0:LAST, :], x[t * P:N, :]).then_inc(done[s], 16)
                    else:
                        sp.dma_start(dest[s][:, :], rows(x, t)).then_inc(done[s], 16)

                def load(t, s):
                    wait(sp, turned, t - 1)
                    load_rows(xt, x_in, t, s % 2)

                def load_again(t, s):
                    wait(sp, summed, t - 3)
                    load_rows(again, again_in, t, s)

                def store(t, s):
                    wait(sp, norm_x.made, t + 1)
                    sp.dma_start(rows(x1, t), res[s % 2][:, :]).then_inc(stored[s % 2], 16)

                over_tiles(sp, NT, 4, (1, load), (5, load_again), (8, store))
                for s in range(2):
                    sp.wait_ge(stored[s], 16 * len(range(s, NT, 2)))

            @block.gpsimd
            def _(pool):
                for v in xt + again:
                    nc.gpsimd.memset(v[:, :], 0.0).then_inc(zeroed, 1)
                pool.wait_ge(weights, 96)

                def scale_and_shift(t, s):
                    wait(pool, norm_y.made, t + 1)
                    nc.gpsimd.tensor_tensor(y_norm[s % 2][:, :], y_norm[s % 2][:, :], vecs["gamma"][:, :], ALU.mult)\
                        .then_inc(scaled, 1)
                    wait(pool, scaled, t + 1)
                    nc.gpsimd.tensor_tensor(y_norm[s % 2][:, :], y_norm[s % 2][:, :], vecs["beta"][:, :], ALU.add)\
                        .then_inc(shifted, 1)
                    wait(pool, shifted, t + 1)
                    nc.gpsimd.tensor_tensor(y_norm[s % 2][:, :], y_norm[s % 2][:, :], again[s][:, :], ALU.add)\
                        .then_inc(summed, 1)

                over_tiles(pool, NT, 4, (0, lambda t, s: agg.stage_and_gather(pool, t, s)), (7, scale_and_shift))

            @block.vector
            def _(dve):
                dve.wait_ge(weights, 96)
                fill_w3(dve)
                fill_w4(dve)

                def rest_of_xa(t, s):
                    wait(dve, xaT.hi_made, 2 * t + 2)
                    wait(dve, u_product, t - 1)
                    for n, bank in enumerate((p_x, p_agg)):
                        ins = rest_of_blocks(nc, xaT.lo[s % 2][:, n * KC:(n + 1) * KC, :], bank,
                                             xaT.hi[s % 2][:, n * KC:(n + 1) * KC, :])
                    ins.then_inc(xaT.made, 1)

                def rest_of_u(t, s):
                    wait(dve, uT.hi_made, t + 1)
                    wait(dve, out_product, t - 1)
                    rest_of_blocks(nc, uT.lo[s % 2][:, :, :], p_uT, uT.hi[s % 2][:, :, :]).then_inc(uT.made, 1)

                def make_z(t, s):
                    wait(dve, u_product, t + 1)
                    wait(dve, mish.made, t - 1)
                    nc.vector.tensor_tensor(mish.z[s % 2][:, :], p_u[s % 2][:, :], vecs["b3"][:, :], ALU.add)\
                        .then_inc(mish.z_made, 1)

                def make_y(t, s):
                    wait(dve, out_product, t + 1)
                    wait(dve, again_in[s], landed(t, s, 4))
                    nc.vector.tensor_tensor(y[s % 2][:, :], p_out[s % 2][:, :], vecs["b4"][:, :], ALU.add)\
                        .then_inc(y_step, 1)
                    wait(dve, y_step, 2 * t + 1)
                    nc.vector.tensor_tensor(y[s % 2][:, :], y[s % 2][:, :], again[s][:, :], ALU.add)\
                        .then_inc(y_step, 1)
                    wait(dve, y_step, 2 * t + 2)
                    norm_y.sums(dve, y[s % 2][:, :], t, s % 2)

                def scale_y(t, s):
                    wait(dve, summed, t - 1)
                    norm_y.scale(dve, y_norm[s % 2][:, :], y[s % 2][:, :], t, s % 2)

                def norm_sums(t, s):
                    wait(dve, summed, t + 1)
                    norm_x.sums(dve, y_norm[s % 2][:, :], t, s % 2)

                def scale_x(t, s):
                    wait(dve, res_turned, t - 1)
                    wait(dve, stored[s % 2], landed(t, s % 2, 2) - 16)
                    norm_x.scale(dve, res[s % 2][:, :], y_norm[s % 2][:, :], t, s % 2)

                def count(t, s):
                    wait(dve, res_turned, t + 1)
                    column_stats(nc, c, stats, p_res, t).then_inc(counted, 1)

                def finish(t, s):
                    wait(dve, u_turned, t - 1)
                    mish.finish(dve, nc.vector, u[s % 2][:, :], t, s % 2)

                over_tiles(dve, NT, 4, (2, rest_of_xa), (5, rest_of_u), (4, make_z), (7, make_y), (8, norm_sums),
                           (4, lambda t, s: mish.product(dve, t, s % 2)), (7, scale_y), (8, scale_x),
                           (4, lambda t, s: mish.share(dve, t, s % 2)), (4, finish), (9, count))

            @block.scalar
            def _(act):
                def copy_turned(t, s):
                    wait(act, turned, t + 1)
                    wait(act, u_product, t - 1)
                    for n, bank in enumerate((p_x, p_agg)):
                        copy_blocks(nc, xaT.hi[s % 2][:, n * KC:(n + 1) * KC, :], bank).then_inc(xaT.hi_made, 1)

                def copy_u(t, s):
                    wait(act, u_turned, t + 1)
                    wait(act, out_product, t - 1)
                    copy_blocks(nc, uT.hi[s % 2][:, :, :], p_uT).then_inc(uT.hi_made, 1)

                over_tiles(act, NT, 4, (2, copy_turned), (5, copy_u), (4, lambda t, s: mish.exp(act, t, s % 2)),
                           (7, lambda t, s: norm_y.root(act, t, s % 2)),
                           (8, lambda t, s: norm_x.root(act, t, s % 2)),
                           (4, lambda t, s: mish.log(act, t, s % 2)), (4, lambda t, s: mish.inverse(act, t, s % 2)))

            @block.tensor
            def _(pe):
                pe.wait_ge(w3_halves.made, 2 * KC)
                pe.wait_ge(w4_halves.made, KC)

                def turn(t, s):
                    wait(pe, x_in[s % 2], landed(t, s % 2, 2))
                    wait(pe, agg.landed[s], landed(t, s, 4))
                    wait(pe, xaT.made, t)
                    turn_blocks(nc, c, p_x, xt[s % 2])
                    turn_blocks(nc, c, p_agg, agg.rows[s]).then_inc(turned, 1)

                def multiply_in(t, s):
                    wait(pe, xaT.made, t + 1)
                    wait(pe, mish.z_made, t - 1)
                    multiply_halves(nc, p_u[s % 2][:, :], xaT, s % 2, range(2 * KC), w3_halves, range(2 * KC))\
                        .then_inc(u_product, 1)

                def turn_u(t, s):
                    wait(pe, mish.made, t + 1)
                    wait(pe, uT.made, t)
                    turn_blocks(nc, c, p_uT, u[s % 2]).then_inc(u_turned, 1)

                def multiply_out(t, s):
                    wait(pe, uT.made, t + 1)
                    wait(pe, y_step, 2 * t - 3)
                    multiply_halves(nc, p_out[s % 2][:, :], uT, s % 2, range(KC), w4_halves, range(KC))\
                        .then_inc(out_product, 1)

                def turn_res(t, s):
                    wait(pe, norm_x.made, t + 1)
                    wait(pe, counted, t)
                    turn_blocks(nc, c, p_res, res[s % 2]).then_inc(res_turned, 1)

                over_tiles(pe, NT, 4, (2, turn), (9, turn_res), (5, turn_u), (3, multiply_in), (6, multiply_out))


TOKENS = 64
M = 256
KEPS = 1e-6


def attention(nc, c, x1, Wq, Wk, Wv, Wo, proj, first_rows, other_rows):
    T, CH = TOKENS, M // P
    with Stage(nc, "attention") as st:
        w = [st.sb(f"w{n}", [P, KC, D]) for n in range(4)]
        pr = st.sb("pr", [P, CH, DH])
        xt = st.sb("xt", [T, D])
        xT, oT = st.sb("xT", [P, KC, T]), st.sb("oT", [P, KC, T])
        prT = st.sb("prT", [DH, M])
        qk = st.sb("qk", [T, 2, D])
        v1 = st.sb("v1", [T, HEADS, DH + 1])
        sq = st.sb("sq", [T, D])
        qkT = st.sb("qkT", [DH, 2, HEADS, T])
        half = st.sb("half", [T, 2, HEADS])
        top = st.sb("top", [T, 2, HEADS])
        bias = st.sb("bias", [T, 2, HEADS])
        topT, top_all = st.sb("topT", [HEADS, 1]), st.sb("top_all", [HEADS, HEADS])
        feat = st.sb("feat", [T, 2, HEADS, M])
        qfT = st.sb("qfT", [P, CH, HEADS, T])
        kv = st.sb("kv", [P, CH, HEADS, DH + 1])
        zr, zi = st.sb("zr", [T, HEADS]), st.sb("zi", [T, HEADS])
        o = st.sb("o", [T, D])
        out = st.sb("out", [T, D])
        pick = st.sb("pick", [T, P])
        bank = [st.ps(f"bank{i}") for i in range(8)]
        loaded, proj_in = st.sem("loaded"), st.sem("proj_in")
        names = ("x_turned", "xT_made", "projected", "qkv_made", "squared", "halved", "turned", "qkT_made", "u_made",
                 "top_made", "top_turned", "topT_made", "top_spread", "bias_made", "exp_made", "features", "qf_turned",
                 "qfT_made", "kv_made", "kv_copied", "num_made", "z_step", "o_made", "o_turned", "oT_made",
                 "out_made", "out_copied", "picked", "spread")
        s = {n: st.sem(n) for n in names}
        HB = HEADS // 2

        with nc.Block() as block:
            @block.sync
            def _(sp):
                sp.dma_start(xt[:, :], x1[0:T, :]).then_inc(loaded, 16)
                load_weights(sp, loaded, [(w[n][:, :, :], m) for n, m in enumerate((Wq, Wk, Wv, Wo))])
                sp.dma_start(pr[:, :, :], proj.rearrange("(c p) d -> p c d", p=P)).then_inc(loaded, 16)

            @block.tensor
            def _(pe):
                pe.wait_ge(loaded, 96)
                for k in range(KC):
                    nc.tensor.transpose(bank[0][:, k * T:(k + 1) * T], xt[:, k * P:(k + 1) * P], c["ident"][0:T, 0:T])
                for h in range(CH):
                    ins = nc.tensor.transpose(bank[0][0:DH, 256 + h * P:256 + (h + 1) * P], pr[:, h, :],
                                              c["ident"][:, :])
                ins.then_inc(s["x_turned"], 1)
                pe.wait_ge(s["xT_made"], 2)
                for n in range(3):
                    for k in range(KC):
                        ins = nc.tensor.matmul(bank[1 + n][0:T, :], xT[:, k, :], w[n][:, k, :],
                                               start=k == 0, stop=k == KC - 1)
                ins.then_inc(s["projected"], 1)
                pe.wait_ge(s["qkv_made"], 3)
                for n in range(2):
                    for h in range(HEADS):
                        ins = nc.tensor.transpose(bank[4 + n][0:DH, h * T:(h + 1) * T], qk[:, n, h * DH:(h + 1) * DH],
                                                  c["ident"][0:T, 0:T])
                ins.then_inc(s["turned"], 1)
                for n in range(2):
                    pe.wait_ge(s["qkT_made"], 2)
                    for h in range(HEADS):
                        if n == 1 and h == 0:
                            pe.wait_ge(s["exp_made"], HEADS)
                        b = bank[h // 2 + 4 * (n == 1)] if n == 0 else bank[h // 2]
                        ins = nc.tensor.matmul(b[0:T, (h % 2) * M:(h % 2 + 1) * M], qkT[:, n, h, :], prT[:, :],
                                               start=True, stop=True)
                    ins.then_inc(s["u_made"], 1)
                pe.wait_ge(s["top_made"], 2)
                nc.tensor.transpose(bank[4][0:HEADS, 0:T], top[:, 1, :], c["ident"][0:T, 0:T]).then_inc(s["top_turned"], 1)
                pe.wait_ge(s["topT_made"], 2)
                nc.tensor.matmul(bank[4][0:T, 0:HEADS], c["ones"][0:HEADS, 0:T], top_all[:, :],
                                 start=True, stop=True).then_inc(s["top_spread"], 1)
                pe.wait_ge(s["features"], 1)
                for ch in range(CH):
                    for h in range(HEADS):
                        ins = nc.tensor.transpose(bank[5 + ch][:, h * T:(h + 1) * T],
                                                  feat[:, 0, h, ch * P:(ch + 1) * P], c["ident"][0:T, 0:T])
                ins.then_inc(s["qf_turned"], 1)
                pe.wait_ge(s["features"], 2)
                for ch in range(CH):
                    for h in range(HEADS):
                        j = (h % HB) * (DH + 1)
                        ins = nc.tensor.matmul(bank[2 * ch + h // HB][:, j:j + DH + 1],
                                               feat[:, 1, h, ch * P:(ch + 1) * P], v1[:, h, :], start=True, stop=True)
                ins.then_inc(s["kv_made"], 1)
                pe.wait_ge(s["kv_copied"], 2)
                pe.wait_ge(s["qfT_made"], 1)
                for h in range(HEADS):
                    j = (h % HB) * (DH + 1)
                    for ch in range(CH):
                        ins = nc.tensor.matmul(bank[5 + h // HB][0:T, j:j + DH + 1], qfT[:, ch, h, :], kv[:, ch, h, :],
                                               start=ch == 0, stop=ch == CH - 1)
                ins.then_inc(s["num_made"], 1)
                pe.wait_ge(s["o_made"], 2)
                for k in range(KC):
                    ins = nc.tensor.transpose(bank[7][:, k * T:(k + 1) * T], o[:, k * P:(k + 1) * P], c["ident"][0:T, 0:T])
                ins.then_inc(s["o_turned"], 1)
                pe.wait_ge(s["oT_made"], 1)
                for k in range(KC):
                    ins = nc.tensor.matmul(bank[0][0:T, :], oT[:, k, :], w[3][:, k, :], start=k == 0, stop=k == KC - 1)
                ins.then_inc(s["out_made"], 1)
                pe.wait_ge(s["out_copied"], 1)
                pe.wait_ge(s["picked"], 1)
                nc.tensor.matmul(bank[1][:, :], pick[:, :], out[:, :], start=True, stop=True).then_inc(s["spread"], 1)

            @block.vector
            def _(dve):
                dve.wait_ge(s["x_turned"], 1)
                nc.vector.tensor_copy(xT[:, :, :], bank[0][:, 0:KC * T].rearrange("p (k m) -> p k m", k=KC))\
                    .then_inc(s["xT_made"], 1)
                nc.vector.tensor_copy(prT[:, :], bank[0][0:DH, 256:256 + M]).then_inc(s["xT_made"], 1)
                nc.vector.tensor_copy(v1[:, :, DH:DH + 1], c["ones"][0:T, 0:HEADS].unsqueeze(2)).then_inc(s["qkv_made"], 1)
                nc.vector.tensor_copy(pick[:, :], c["ident"][0:T, T - 1:T].to_broadcast([T, P])).then_inc(s["picked"], 1)
                dve.wait_ge(s["projected"], 1)
                for n in range(2):
                    ins = nc.vector.tensor_scalar(qk[:, n, :], bank[1 + n][0:T, :], float(DH) ** -0.25, None, ALU.mult)
                ins.then_inc(s["qkv_made"], 1)
                nc.vector.tensor_copy(v1[:, :, 0:DH], bank[3][0:T, :].rearrange("p (h d) -> p h d", h=HEADS))\
                    .then_inc(s["qkv_made"], 1)
                dve.wait_ge(s["qkv_made"], 3)
                for n in range(2):
                    nc.vector.tensor_tensor(sq[:, :], qk[:, n, :], qk[:, n, :], ALU.mult).then_inc(s["squared"], 1)
                    dve.wait_ge(s["squared"], n + 1)
                    nc.vector.tensor_reduce(half[:, n, :], sq[:, :].rearrange("p (h d) -> p h d", h=HEADS),
                                            mybir.AxisListType.X, ALU.add).then_inc(s["halved"], 1)
                    dve.wait_ge(s["halved"], 2 * n + 1)
                    nc.vector.tensor_scalar(half[:, n, :], half[:, n, :], 0.5, None, ALU.mult).then_inc(s["halved"], 1)
                dve.wait_ge(s["turned"], 1)
                for n in range(2):
                    nc.vector.tensor_copy(qkT[:, n, :, :], bank[4 + n][0:DH, :].rearrange("p (h m) -> p h m", h=HEADS))\
                        .then_inc(s["qkT_made"], 1)
                dve.wait_ge(s["u_made"], 1)
                for b in range(HB):
                    ins = nc.vector.tensor_reduce(top[:, 0, 2 * b:2 * b + 2],
                                                  bank[b][0:T, :].rearrange("p (h m) -> p h m", h=2),
                                                  mybir.AxisListType.X, ALU.max)
                ins.then_inc(s["top_made"], 1)
                dve.wait_ge(s["top_made"], 1)
                dve.wait_ge(s["halved"], 4)
                nc.vector.scalar_tensor_tensor(bias[:, 0, :], top[:, 0, :], -1.0, half[:, 0, :],
                                               ALU.mult, ALU.subtract).then_inc(s["bias_made"], 1)
                dve.wait_ge(s["u_made"], 2)
                for b in range(HB):
                    ins = nc.vector.tensor_reduce(top[:, 1, 2 * b:2 * b + 2],
                                                  bank[b][0:T, :].rearrange("p (h m) -> p h m", h=2),
                                                  mybir.AxisListType.X, ALU.max)
                ins.then_inc(s["top_made"], 1)
                dve.wait_ge(s["top_turned"], 1)
                nc.vector.tensor_reduce(topT[:, :], bank[4][0:HEADS, 0:T], mybir.AxisListType.X, ALU.max)\
                    .then_inc(s["topT_made"], 1)
                dve.wait_ge(s["topT_made"], 1)
                nc.vector.tensor_scalar(top_all[:, :], c["ident"][0:HEADS, 0:HEADS], topT[:, 0:1], None, ALU.mult)\
                    .then_inc(s["topT_made"], 1)
                dve.wait_ge(s["top_spread"], 1)
                nc.vector.scalar_tensor_tensor(bias[:, 1, :], bank[4][0:T, 0:HEADS], -1.0, half[:, 1, :],
                                               ALU.mult, ALU.subtract).then_inc(s["bias_made"], 1)
                for n in range(2):
                    dve.wait_ge(s["exp_made"], HEADS * (n + 1))
                    nc.vector.tensor_scalar(feat[:, n, :, :], feat[:, n, :, :], float(M) ** -0.5, KEPS,
                                            ALU.mult, ALU.add).then_inc(s["features"], 1)
                dve.wait_ge(s["qf_turned"], 1)
                for ch in range(CH):
                    ins = nc.vector.tensor_copy(qfT[:, ch, :, :], bank[5 + ch][:, :].rearrange("p (h m) -> p h m", h=HEADS))
                ins.then_inc(s["qfT_made"], 1)
                dve.wait_ge(s["kv_made"], 1)
                for ch in range(CH):
                    for g in range(2):
                        ins = nc.vector.tensor_copy(kv[:, ch, g * HB:(g + 1) * HB, :],
                                                    bank[2 * ch + g][:, 0:HB * (DH + 1)]
                                                    .rearrange("p (h d) -> p h d", h=HB))
                    ins.then_inc(s["kv_copied"], 1)
                dve.wait_ge(s["num_made"], 1)
                for g in range(2):
                    num = bank[5 + g][0:T, 0:HB * (DH + 1)].rearrange("p (h d) -> p h d", h=HB)
                    ins = nc.vector.tensor_scalar(zr[:, g * HB:(g + 1) * HB].unsqueeze(2), num[:, :, DH:DH + 1], KEPS, None,
                                                  ALU.add)
                ins.then_inc(s["z_step"], 1)
                dve.wait_ge(s["z_step"], 1)
                nc.vector.reciprocal(zi[:, :], zr[:, :]).then_inc(s["z_step"], 1)
                dve.wait_ge(s["z_step"], 2)
                for g in range(2):
                    num = bank[5 + g][0:T, 0:HB * (DH + 1)].rearrange("p (h d) -> p h d", h=HB)
                    nc.vector.tensor_tensor(o[:, g * HB * DH:(g + 1) * HB * DH].rearrange("p (h d) -> p h d", h=HB),
                                            num[:, :, 0:DH],
                                            zi[:, g * HB:(g + 1) * HB].unsqueeze(2).to_broadcast([T, HB, DH]),
                                            ALU.mult).then_inc(s["o_made"], 1)
                dve.wait_ge(s["o_turned"], 1)
                nc.vector.tensor_copy(oT[:, :, :], bank[7][:, 0:KC * T].rearrange("p (k m) -> p k m", k=KC))\
                    .then_inc(s["oT_made"], 1)
                dve.wait_ge(s["out_made"], 1)
                nc.vector.tensor_copy(out[:, :], bank[0][0:T, :]).then_inc(s["out_copied"], 1)
                dve.wait_ge(s["spread"], 1)
                nc.vector.tensor_copy(other_rows, bank[1][:, :])
                nc.vector.tensor_copy(first_rows[T:P, :], bank[1][T:P, :])
                nc.vector.tensor_copy(first_rows[0:T, :], out[:, :])

            @block.scalar
            def _(act):
                for n in range(2):
                    act.wait_ge(s["bias_made"], n + 1)
                    for h in range(HEADS):
                        nc.scalar.activation(feat[:, n, h, :], bank[h // 2][0:T, (h % 2) * M:(h % 2 + 1) * M], ACT.Exp,
                                             bias=bias[:, n, h:h + 1]).then_inc(s["exp_made"], 1)


def conv_nodes(nc, c, x1, sums, W, b, g1, b1, stats1, first_rows, other_rows, y, stats2):
    with Stage(nc, "conv") as st:
        w, wa = st.sb("w", [P, KC, D]), st.sb("wa", [P, KC, D])
        bias, shift_w = st.sb("bias", [P, D]), st.sb("shift_w", [P, D])
        gb = st.sb("gb", [P, 2, KC])
        scale, shift, tmp = st.sb("scale", [P, KC]), st.sb("shift", [P, KC]), st.sb("tmp", [P, KC])
        mom = st.sb("mom", [P, KC, 2])
        shift_all = st.sb("shift_all", [P, KC, P])
        xt = st.slots(st.sb, "xt", 4, [P, D])
        aT = Halves(st, "aT", [P, KC, P])
        wa_halves, fill_wa = split_weights(nc, st, "wa", wa)
        v, yt = st.slots(st.sb, "v", 2, [P, D]), st.slots(st.sb, "yt", 2, [P, D])
        p_agg, p_out, p_y = (st.slots(st.ps, n, 2) for n in ("p_agg", "p_out", "p_y"))
        p_shift = st.ps("p_shift")
        weights, moments, step, shifted_w, params = (st.sem(n) for n in
                                                     ("weights", "moments", "step", "shifted_w", "params"))
        x_in, stored = st.slots(st.sem, "x_in", 4), st.slots(st.sem, "stored", 2)
        turned, product, v_step, summed, y_turned, counted = (
            st.sem(n) for n in ("turned", "product", "v_step", "summed", "y_turned", "counted"))
        wa_made = st.sem("wa_made")
        attended = st.sem("attended")
        agg = NodeGather(nc, st, c, sums, turned)

        with nc.Block() as block:
            @block.sync
            def _(sp):
                load_weights(sp, weights, [(w[:, :, :], W)])
                sp.dma_start(bias[:, :], row_of_all(b)).then_inc(weights, 16)
                sp.dma_start(gb[:, 0, :], g1.rearrange("(k p) -> p k", p=P), allow_slow_non_contiguous=True)\
                    .then_inc(weights, 16)
                sp.dma_start(gb[:, 1, :], b1.rearrange("(k p) -> p k", p=P), allow_slow_non_contiguous=True)\
                    .then_inc(weights, 16)

                def load(t, s):
                    wait(sp, attended, t - 3)
                    sp.dma_start(xt[s][:, :], rows(x1, t)).then_inc(x_in[s], 16)

                def store(t, s):
                    wait(sp, attended, t + 1)
                    sp.dma_start(rows(y, t), yt[s % 2][:, :]).then_inc(stored[s % 2], 16)

                over_tiles(sp, NT, 4, (2, load), (5, store))
                for s in range(2):
                    sp.wait_ge(stored[s], 16 * len(range(s, NT, 2)))

            @block.gpsimd
            def _(pool):
                def attend(t, s):
                    wait(pool, summed, t + 1)
                    wait(pool, y_turned, t - 1)
                    wait(pool, stored[s % 2], landed(t, s % 2, 2) - 16)
                    given = first_rows if isinstance(t, int) and t == 0 else other_rows
                    nc.gpsimd.tensor_tensor(yt[s % 2][:, :], v[s % 2][:, :], given, ALU.add).then_inc(attended, 1)

                over_tiles(pool, NT, 4, (0, lambda t, s: agg.stage_and_gather(pool, t, s)), (5, attend))

            @block.vector
            def _(dve):
                dve.wait_ge(weights, 64)
                for k in range(KC):
                    nc.vector.bn_aggr(mom[:, k, :], stats1[:, k, :, :].rearrange("p t f -> p (t f)"))\
                        .then_inc(moments, 1)
                dve.wait_ge(step, 2)
                nc.vector.tensor_tensor(scale[:, :], tmp[:, :], gb[:, 0, :], ALU.mult).then_inc(step, 1)
                dve.wait_ge(step, 3)
                nc.vector.tensor_tensor(shift[:, :], mom[:, :, 0], scale[:, :], ALU.mult).then_inc(step, 1)
                dve.wait_ge(step, 4)
                nc.vector.tensor_tensor(shift[:, :], gb[:, 1, :], shift[:, :], ALU.subtract).then_inc(step, 1)
                dve.wait_ge(step, 5)
                for k in range(KC):
                    nc.vector.tensor_scalar(wa[:, k, :], w[:, k, :], scale[:, k:k + 1], None, ALU.mult)\
                        .then_inc(wa_made, 1)
                    ins = nc.vector.tensor_scalar(shift_all[:, k, :], c["ones"][:, :], shift[:, k:k + 1], None, ALU.mult)
                ins.then_inc(params, 1)
                dve.wait_ge(shifted_w, 1)
                nc.vector.tensor_copy(shift_w[:, :], p_shift[:, :]).then_inc(params, 1)
                dve.wait_ge(params, 2)
                dve.wait_ge(wa_made, KC)
                fill_wa(dve)

                def rest(t, s):
                    wait(dve, aT.hi_made, t + 1)
                    wait(dve, product, t - 1)
                    rest_of_blocks(nc, aT.lo[s % 2][:, :, :], p_agg[s % 2], aT.hi[s % 2][:, :, :]).then_inc(aT.made, 1)

                def activate(t, s):
                    wait(dve, product, t + 1)
                    wait(dve, x_in[s], landed(t, s, 4))
                    wait(dve, summed, t - 1)
                    wait(dve, attended, t - 1)
                    nc.vector.scalar_tensor_tensor(v[s % 2][:, :], p_out[s % 2][:, :], c["inv_deg"][:, bass.ds(t, 1)],
                                                   bias[:, :], ALU.mult, ALU.add).then_inc(v_step, 1)
                    wait(dve, v_step, 2 * t + 1)
                    nc.vector.scalar_tensor_tensor(v[s % 2][:, :], shift_w[:, :], c["has_edges"][:, bass.ds(t, 1)],
                                                   v[s % 2][:, :], ALU.mult, ALU.add).then_inc(v_step, 1)
                    wait(dve, v_step, 2 * t + 2)
                    nc.vector.scalar_tensor_tensor(v[s % 2][:, :], v[s % 2][:, :], 0.0, xt[s][:, :],
                                                   ALU.max, ALU.add).then_inc(summed, 1)

                def count(t, s):
                    wait(dve, y_turned, t + 1)
                    column_stats(nc, c, stats2, p_y[s % 2], t).then_inc(counted, 1)

                over_tiles(dve, NT, 4, (3, rest), (5, activate), (6, count))

            @block.scalar
            def _(act):
                act.wait_ge(moments, KC)
                nc.scalar.activation(tmp[:, :], mom[:, :, 1], ACT.Ln, bias=c["eps"][:, 0:1]).then_inc(step, 1)
                act.wait_ge(step, 1)
                nc.scalar.activation(tmp[:, :], tmp[:, :], ACT.Exp, scale=-0.5).then_inc(step, 1)

                def copy_turned(t, s):
                    wait(act, turned, t + 1)
                    wait(act, product, t - 1)
                    copy_blocks(nc, aT.hi[s % 2][:, :, :], p_agg[s % 2]).then_inc(aT.hi_made, 1)

                over_tiles(act, NT, 4, (3, copy_turned))

            @block.tensor
            def _(pe):
                pe.wait_ge(weights, 64)
                pe.wait_ge(params, 1)
                for k in range(KC):
                    ins = nc.tensor.matmul(p_shift[:, :], shift_all[:, k, :], w[:, k, :], start=k == 0, stop=k == KC - 1)
                ins.then_inc(shifted_w, 1)
                pe.wait_ge(wa_halves.made, KC)

                def turn(t, s):
                    wait(pe, agg.landed[s], landed(t, s, 4))
                    wait(pe, aT.made, t - 1)
                    turn_blocks(nc, c, p_agg[s % 2], agg.rows[s]).then_inc(turned, 1)

                def multiply(t, s):
                    wait(pe, aT.made, t + 1)
                    wait(pe, v_step, 2 * t - 3)
                    multiply_halves(nc, p_out[s % 2][:, :], aT, s % 2, range(KC), wa_halves, range(KC))\
                        .then_inc(product, 1)

                def turn_y(t, s):
                    wait(pe, attended, t + 1)
                    wait(pe, counted, t - 1)
                    turn_blocks(nc, c, p_y[s % 2], yt[s % 2]).then_inc(y_turned, 1)

                over_tiles(pe, NT, 4, (3, turn), (6, turn_y), (4, multiply))


def head_products(nc, c, x1, y, g2, b2, stats2, Ws, Wb, a_w, a_b, x2, wx, uv):
    with Stage(nc, "heads") as st:
        w, wa = st.sb("w", [P, KC, D]), st.sb("wa", [P, KC, 2 * HEADS])
        bias, bias_uv = st.sb("bias", [P, D]), st.sb("bias_uv", [P, 2 * HEADS])
        a_src, a_dst = st.sb("a_src", [P, D]), st.sb("a_dst", [P, D])
        ab = st.sb("ab", [P, HEADS])
        prod = st.sb("prod", [P, D])
        gb, mom = st.sb("gb", [P, 2, KC]), st.sb("mom", [P, KC, 2])
        scale, shift, tmp = st.sb("scale", [P, KC]), st.sb("shift", [P, KC]), st.sb("tmp", [P, KC])
        diag = st.sb("diag", [P, 2, KC, P])
        scale_row, shift_row = st.sb("scale_row", [P, D]), st.sb("shift_row", [P, D])
        xt, yt = st.slots(st.sb, "xt", 4, [P, D]), st.slots(st.sb, "yt", 4, [P, D])
        res, xT = st.slots(st.sb, "res", 2, [P, D]), Halves(st, "xT", [P, KC, P])
        w_halves, fill_w = split_weights(nc, st, "w", w)
        wa_halves, fill_wa = split_weights(nc, st, "wa", wa)
        out, out_uv = st.slots(st.sb, "out", 2, [P, D]), st.slots(st.sb, "out_uv", 2, [P, 2 * HEADS])
        p_row = st.slots(st.ps, "p_row", 2)
        p_turn, p_out, p_uv = st.slots(st.ps, "p_turn", 2), st.slots(st.ps, "p_out", 2), st.slots(st.ps, "p_uv", 2)
        weights, moments, step, prep, spread = (st.sem(n) for n in ("weights", "moments", "step", "prep", "spread"))
        x_in, y_in = st.slots(st.sem, "x_in", 4), st.slots(st.sem, "y_in", 4)
        stored = [st.slots(st.sem, f"stored{n}_", 2) for n in range(3)]
        scaled, shifted, summed, turned, product, out_made = (
            st.sem(n) for n in ("scaled", "shifted", "summed", "turned", "product", "out_made"))
        norm = LayerNorm(nc, st, c, "norm")

        with nc.Block() as block:
            @block.sync
            def _(sp):
                for h in range(HEADS):
                    sp.dma_start(w[:, :, h * DH:(h + 1) * DH], Ws[h].rearrange("(k p) d -> p k d", p=P))\
                        .then_inc(weights, 16)
                for h in range(HEADS):
                    sp.dma_start(a_dst[:, h * DH:(h + 1) * DH], row_of_all(a_w[h, 0:DH])).then_inc(weights, 16)
                sp.dma_start(bias[:, :], row_of_all(Wb.rearrange("h d -> (h d)"))).then_inc(weights, 16)
                for h in range(0, HEADS, 4):
                    sp.dma_start(a_src[:, h * DH:(h + 4) * DH].rearrange("p (h d) -> p h d", h=4),
                                 bass.AP(tensor=a_w.tensor, offset=a_w.offset + (2 * h + 1) * DH,
                                         ap=[[0, P], [2 * DH, 4], [1, DH]])).then_inc(weights, 16)
                sp.dma_start(ab[:, :], row_of_all(a_b)).then_inc(weights, 16)
                sp.dma_start(gb[:, 0, :], g2.rearrange("(k p) -> p k", p=P), allow_slow_non_contiguous=True)\
                    .then_inc(weights, 16)
                sp.dma_start(gb[:, 1, :], b2.rearrange("(k p) -> p k", p=P), allow_slow_non_contiguous=True)\
                    .then_inc(weights, 16)

                def load(t, s):
                    wait(sp, summed, t - 3)
                    sp.dma_start(xt[s][:, :], rows(x1, t)).then_inc(x_in[s], 16)
                    wait(sp, norm.made, t - 3)
                    sp.dma_start(yt[s][:, :], rows(y, t)).then_inc(y_in[s], 16)

                def store_x(t, s):
                    wait(sp, norm.made, t + 1)
                    sp.dma_start(rows(x2, t), res[s % 2][:, :]).then_inc(stored[0][s % 2], 16)

                def store(t, s):
                    wait(sp, out_made, 2 * t + 2)
                    sp.dma_start(rows(wx, t), out[s % 2][:, :]).then_inc(stored[1][s % 2], 16)
                    sp.dma_start(rows(uv, t), out_uv[s % 2][:, :]).then_inc(stored[2][s % 2], 16)

                over_tiles(sp, NT, 4, (0, load), (3, store_x), (6, store))
                for n in range(3):
                    for s in range(2):
                        sp.wait_ge(stored[n][s], 16 * len(range(s, NT, 2)))

            @block.gpsimd
            def _(pool):
                pool.wait_ge(prep, 4)

                def shift_and_add(t, s):
                    wait(pool, scaled, t + 1)
                    nc.gpsimd.tensor_tensor(yt[s][:, :], yt[s][:, :], shift_row[:, :], ALU.add).then_inc(shifted, 1)
                    wait(pool, shifted, t + 1)
                    nc.gpsimd.tensor_tensor(yt[s][:, :], yt[s][:, :], xt[s][:, :], ALU.add).then_inc(summed, 1)

                over_tiles(pool, NT, 4, (1, shift_and_add))

            @block.vector
            def _(dve):
                dve.wait_ge(weights, 16 * (2 * HEADS + 6))
                for k in range(KC):
                    nc.vector.bn_aggr(mom[:, k, :], stats2[:, k, :, :].rearrange("p t f -> p (t f)"))\
                        .then_inc(moments, 1)
                dve.wait_ge(step, 2)
                nc.vector.tensor_tensor(scale[:, :], tmp[:, :], gb[:, 0, :], ALU.mult).then_inc(step, 1)
                dve.wait_ge(step, 3)
                nc.vector.tensor_tensor(shift[:, :], mom[:, :, 0], scale[:, :], ALU.mult).then_inc(step, 1)
                dve.wait_ge(step, 4)
                nc.vector.tensor_tensor(shift[:, :], gb[:, 1, :], shift[:, :], ALU.subtract).then_inc(step, 1)
                dve.wait_ge(step, 5)
                for k in range(KC):
                    nc.vector.tensor_scalar(diag[:, 0, k, :], c["ident"][:, :], scale[:, k:k + 1], None, ALU.mult)
                    ins = nc.vector.tensor_scalar(diag[:, 1, k, :], c["ident"][:, :], shift[:, k:k + 1], None, ALU.mult)
                ins.then_inc(prep, 1)
                n = 0
                for k in range(KC + 1):
                    for j, a in enumerate((a_src, a_dst)):
                        source = w[:, k, :] if k < KC else bias[:, :]
                        dest = wa[:, k, j * HEADS:(j + 1) * HEADS] if k < KC else bias_uv[:, j * HEADS:(j + 1) * HEADS]
                        nc.vector.tensor_tensor(prod[:, :], source, a[:, :], ALU.mult).then_inc(step, 1)
                        n += 1
                        dve.wait_ge(step, 5 + n)
                        nc.vector.tensor_reduce(dest, prod[:, :].rearrange("p (h d) -> p h d", h=HEADS),
                                                mybir.AxisListType.X, ALU.add).then_inc(step, 1)
                        n += 1
                        dve.wait_ge(step, 5 + n)
                nc.vector.tensor_tensor(bias_uv[:, HEADS:], bias_uv[:, HEADS:], ab[:, :], ALU.add).then_inc(prep, 1)
                dve.wait_ge(spread, 2)
                nc.vector.tensor_copy(scale_row[:, :], p_row[0][:, :]).then_inc(prep, 1)
                nc.vector.tensor_copy(shift_row[:, :], p_row[1][:, :]).then_inc(prep, 1)
                dve.wait_ge(prep, 4)
                fill_w(dve)
                fill_wa(dve)

                def rest(t, s):
                    wait(dve, xT.hi_made, t + 1)
                    wait(dve, product, t - 1)
                    rest_of_blocks(nc, xT.lo[s % 2][:, :, :], p_turn[s % 2], xT.hi[s % 2][:, :, :]).then_inc(xT.made, 1)

                def scale_y(t, s):
                    wait(dve, y_in[s], landed(t, s, 4))
                    wait(dve, x_in[s], landed(t, s, 4))
                    nc.vector.tensor_tensor(yt[s][:, :], yt[s][:, :], scale_row[:, :], ALU.mult).then_inc(scaled, 1)

                def norm_sums(t, s):
                    wait(dve, summed, t + 1)
                    norm.sums(dve, yt[s][:, :], t, s % 2)

                def norm_scale(t, s):
                    wait(dve, turned, t - 1)
                    wait(dve, stored[0][s % 2], landed(t, s % 2, 2) - 16)
                    norm.scale(dve, res[s % 2][:, :], yt[s][:, :], t, s % 2)

                def evacuate(t, s):
                    wait(dve, product, t + 1)
                    for n in (1, 2):
                        wait(dve, stored[n][s % 2], landed(t, s % 2, 2) - 16)
                    nc.vector.tensor_tensor(out[s % 2][:, :], p_out[s % 2][:, :], bias[:, :], ALU.add).then_inc(out_made, 1)
                    nc.vector.tensor_tensor(out_uv[s % 2][:, :], p_uv[s % 2][:, 0:2 * HEADS], bias_uv[:, :], ALU.add)\
                        .then_inc(out_made, 1)

                over_tiles(dve, NT, 4, (3, rest), (1, scale_y), (2, norm_sums), (5, evacuate), (2, norm_scale))

            @block.scalar
            def _(act):
                act.wait_ge(moments, KC)
                nc.scalar.activation(tmp[:, :], mom[:, :, 1], ACT.Ln, bias=c["eps"][:, 0:1]).then_inc(step, 1)
                act.wait_ge(step, 1)
                nc.scalar.activation(tmp[:, :], tmp[:, :], ACT.Exp, scale=-0.5).then_inc(step, 1)

                def copy_turned(t, s):
                    wait(act, turned, t + 1)
                    wait(act, product, t - 1)
                    copy_blocks(nc, xT.hi[s % 2][:, :, :], p_turn[s % 2]).then_inc(xT.hi_made, 1)

                over_tiles(act, NT, 4, (3, copy_turned), (2, lambda t, s: norm.root(act, t, s % 2)))

            @block.tensor
            def _(pe):
                pe.wait_ge(prep, 1)
                for n in range(2):
                    for k in range(KC):
                        ins = nc.tensor.matmul(p_row[n][:, k * P:(k + 1) * P], c["ones"][:, :], diag[:, n, k, :],
                                               start=True, stop=True)
                    ins.then_inc(spread, 1)
                pe.wait_ge(prep, 4)
                pe.wait_ge(w_halves.made, KC)
                pe.wait_ge(wa_halves.made, KC)

                def turn(t, s):
                    wait(pe, norm.made, t + 1)
                    wait(pe, xT.made, t - 1)
                    turn_blocks(nc, c, p_turn[s % 2], res[s % 2]).then_inc(turned, 1)

                def multiply(t, s):
                    wait(pe, xT.made, t + 1)
                    wait(pe, out_made, 2 * t - 2)
                    multiply_halves(nc, p_out[s % 2][:, :], xT, s % 2, range(KC), w_halves, range(KC))
                    multiply_halves(nc, p_uv[s % 2][:, 0:2 * HEADS], xT, s % 2, range(KC), wa_halves, range(KC))\
                        .then_inc(product, 1)

                over_tiles(pe, NT, 4, (3, turn), (4, multiply))


def edge_softmax(nc, c, uv, weights):
    with Stage(nc, "scores") as st:
        idx = [st.slots(st.sb, f"idx{n}_", 4, [P, 1], I32) for n in range(2)]
        part = [st.slots(st.sb, f"part{n}_", 4, [P, 2 * HEADS]) for n in range(2)]
        raw = st.slots(st.sb, "raw", 4, [P, HEADS])
        scores = st.sb("scores", [P, GROUPS * GT, HEADS])
        staged, raw_made, scored = st.sem("staged"), st.sem("raw_made"), st.sem("scored")
        gathered = [st.slots(st.dma_sem, f"gathered{n}_", 4) for n in range(2)]
        cleared = st.sem("cleared")

        with nc.Block() as block:
            @block.gpsimd
            def _(pool):
                def gather(t, s):
                    for n in range(2):
                        nc.gpsimd.indirect_dma_start(out=part[n][s][:, :], in_=uv[:, :], out_offset=None,
                                                     in_offset=bass.IndirectOffsetOnAxis(ap=idx[n][s][:, 0:1], axis=0))\
                            .then_inc(gathered[n][s], 16)

                def stage_and_gather(t, s):
                    wait(pool, staged, 2 * t)
                    wait(pool, raw_made, t - 4)
                    for n, lst in enumerate(("src_list", "dst_list")):
                        wait(pool, gathered[n][s], landed(t, s, 4) - 16)
                        nc.gpsimd.tensor_copy(idx[n][s][:, :], c[lst][:, bass.ds(t, 1)]).then_inc(staged, 1)
                    if not isinstance(t, int) or t > 0:
                        gather(t - 1, (s - 1) % 4)

                over_tiles(pool, NET, 4, (0, stage_and_gather))
                pool.wait_ge(staged, 2 * NET)
                pool.wait_ge(raw_made, NET - 4)
                gather(NET - 1, (NET - 1) % 4)

            @block.vector
            def _(dve):
                nc.vector.memset(scores[:, NET:, :], 0.0).then_inc(cleared, 1)

                def score(t, s):
                    for n in range(2):
                        wait(dve, gathered[n][s], landed(t, s, 4))
                    nc.vector.tensor_tensor(raw[s][:, :], part[0][s][:, 0:HEADS], part[1][s][:, HEADS:],
                                            ALU.add).then_inc(raw_made, 1)
                    wait(dve, raw_made, t + 1)
                    nc.vector.scalar_tensor_tensor(scores[:, bass.ds(t, 1), :].rearrange("p o h -> p (o h)"),
                                                   raw[s][:, :], 0.2, raw[s][:, :], ALU.mult, ALU.max).then_inc(scored, 1)

                over_tiles(dve, NET, 4, (0, score))
                dve.wait_ge(scored, NET)

        key, same_p, same_n = (st.sb(n, [P, GE]) for n in ("key", "same_p", "same_n"))
        with_p, with_n = st.sb("with_p", [P, GE]), st.sb("with_n", [P, GE])
        sT, fwd, bwd, ex, tmp = (st.sb(n, [P, GE]) for n in ("sT", "fwd", "bwd", "ex", "tmp"))
        alpha = st.sb("alpha", [P, GE + 1])
        key_in = st.sb("key_in", [P, GT, P])
        row, row2 = st.sb("row", [1, 4, P]), st.sb("row2", [1, 4, P])
        link = st.sb("link", [1, 2, P])
        ends, nears = st.sb("ends", [P, 4]), st.sb("nears", [P, 4])
        p_s = [st.ps(f"p_s{i}") for i in range(GT)]
        p_row, p_col = st.ps("p_row"), st.ps("p_col")
        ready, keys_turned, keys_read, turned = (st.sem(n) for n in ("ready", "keys_turned", "keys_read", "turned"))
        step, rows_made, rows_read, cols_made = (st.sem(n) for n in ("step", "rows_made", "rows_read", "cols_made"))
        less_max, summed = st.sem("less_max"), st.sem("summed")
        exp_made, log_made, inv_made, alpha_made, alpha_turned = (
            st.sem(n) for n in ("exp_made", "log_made", "inv_made", "alpha_made", "alpha_turned"))

        def of_tile(v, j):
            return v[:, j * ET:(j + 1) * ET]

        with nc.Block() as block:
            @block.tensor
            def _(pe):
                pe.wait_ge(ready, 1)
                for j in range(GT):
                    ins = nc.tensor.transpose(p_s[j][:, 0:P], key_in[:, j, :], c["ident"][:, :])
                ins.then_inc(keys_turned, 1)
                pe.wait_ge(keys_read, 1)
                pe.wait_ge(ready, 2)
                for j in range(GT):
                    ins = nc.tensor.transpose(p_s[j][:, 0:P], key_in[:, j, :], c["ident"][:, :])
                ins.then_inc(turned, 1)
                for turn in range(2):
                    pe.wait_ge(rows_made, 2 * turn + 1)
                    for n in range(4):
                        ins = nc.tensor.transpose(p_row[0:1, n * P:(n + 1) * P], ends[:, n:n + 1], c["ident"][:, :])
                    ins.then_inc(rows_read, 1)
                    pe.wait_ge(rows_made, 2 * turn + 2)
                    for n in range(4):
                        ins = nc.tensor.transpose(p_col[:, n:n + 1], row2[:, n, :], c["ident"][0:1, 0:1])
                    ins.then_inc(cols_made, 1)
                pe.wait_ge(alpha_made, 1)
                for j in range(GT):
                    ins = nc.tensor.transpose(p_s[j][:, 0:P], alpha[:, j * ET:j * ET + P], c["ident"][:, :])
                ins.then_inc(alpha_turned, 1)

            @block.scalar
            def _(act):
                act.wait_ge(less_max, 1)
                nc.scalar.activation(ex[:, :], sT[:, :], ACT.Exp).then_inc(exp_made, 1)
                act.wait_ge(summed, 1)
                nc.scalar.activation(fwd[:, :], fwd[:, :], ACT.Ln).then_inc(log_made, 1)
                act.wait_ge(log_made, 1)
                nc.scalar.activation(fwd[:, :], fwd[:, :], ACT.Exp, scale=-1.0).then_inc(inv_made, 1)

            @block.vector
            def _(dve):
                done = [0]

                def then(ins):
                    done[0] += 1
                    ins.then_inc(step, 1)
                    dve.wait_ge(step, done[0])

                V = nc.vector
                for j in range(GT):
                    ins = V.tensor_copy(key_in[:, j, :].rearrange("p (g h) -> p g h", h=HEADS),
                                        c["keys"][:, j::GT].unsqueeze(2).to_broadcast([P, GROUPS, HEADS]))
                ins.then_inc(ready, 1)
                dve.wait_ge(keys_turned, 1)
                for j in range(GT):
                    ins = V.tensor_copy(of_tile(key, j), p_s[j][:, 1:P])
                ins.then_inc(keys_read, 1)
                for j in range(GT):
                    ins = V.tensor_copy(key_in[:, j, :].rearrange("p (g h) -> p g h", h=HEADS), scores[:, j::GT, :])
                ins.then_inc(ready, 1)
                V.memset(same_p[:, 0:1], 0.0)
                V.memset(same_n[:, GE - 1:GE], 0.0)
                V.memset(alpha[:, 0:1], 0.0)
                dve.wait_ge(keys_read, 1)
                V.tensor_tensor(same_p[:, 1:GE], key[:, 1:GE], key[:, 0:GE - 1], ALU.is_equal)
                then(V.tensor_tensor(same_n[:, 0:GE - 1], key[:, 1:GE], key[:, 0:GE - 1], ALU.is_equal))
                dve.wait_ge(turned, 1)
                for j in range(GT):
                    ins = V.tensor_copy(of_tile(sT, j), p_s[j][:, 1:P])
                then(ins)

                def ends_of_groups(first):
                    V.tensor_copy(ends[:, 0:1], fwd[:, GE - 1:GE])
                    V.tensor_copy(ends[:, 1:2], key[:, GE - 1:GE])
                    V.tensor_copy(ends[:, 2:3], bwd[:, 0:1])
                    V.tensor_copy(ends[:, 3:4], key[:, 0:1]).then_inc(rows_made, 1)
                    dve.wait_ge(rows_read, 1 if first else 2)
                    for n in range(4):
                        ins = V.tensor_copy(row[:, n, :].rearrange("o (h g) -> o h g", h=HEADS),
                                            p_row[0:1, n * P:(n + 1) * P].rearrange("o (g h) -> o h g", h=HEADS))
                    then(ins)
                    V.tensor_tensor(link[:, 0, 1:P], row[:, 1, 1:P], row[:, 1, 0:P - 1], ALU.is_equal)
                    then(V.tensor_tensor(link[:, 1, 0:P - 1], row[:, 3, 1:P], row[:, 3, 0:P - 1], ALU.is_equal))
                    V.memset(link[:, 0, 0:P:GROUPS], 0.0)
                    then(V.memset(link[:, 1, GROUPS - 1:P:GROUPS], 0.0))
                    if first:
                        then(V.tensor_scalar(link[:, :, :], link[:, :, :], -1.0, BIG, ALU.add, ALU.mult))
                    ops = (ALU.add, ALU.max) if first else (ALU.mult, ALU.add)
                    none = -BIG if first else 0.0
                    V.tensor_tensor_scan(row[:, 0, :], link[:, 0, :], row[:, 0, :], none, *ops)
                    then(V.tensor_tensor_scan(row[:, 2, ::-1], link[:, 1, ::-1], row[:, 2, ::-1], none, *ops))
                    for n, fill in ((0, none), (1, -1.0), (2, none), (3, -1.0)):
                        back = row2[:, n, :].rearrange("o (g h) -> o h g", h=HEADS)
                        mine = row[:, n, :].rearrange("o (h g) -> o h g", h=HEADS)
                        if n < 2:
                            V.tensor_copy(back[:, :, 1:GROUPS], mine[:, :, 0:GROUPS - 1])
                            V.memset(row2[:, n, 0:HEADS], fill)
                        else:
                            V.tensor_copy(back[:, :, 0:GROUPS - 1], mine[:, :, 1:GROUPS])
                            ins = V.memset(row2[:, n, P - HEADS:P], fill)
                    ins.then_inc(rows_made, 1)
                    dve.wait_ge(cols_made, 1 if first else 2)
                    then(V.tensor_copy(nears[:, :], p_col[:, 0:4]))

                V.tensor_scalar(with_p[:, :], same_p[:, :], -1.0, BIG, ALU.add, ALU.mult)
                then(V.tensor_scalar(with_n[:, :], same_n[:, :], -1.0, BIG, ALU.add, ALU.mult))
                V.tensor_tensor_scan(fwd[:, :], with_p[:, :], sT[:, :], -BIG, ALU.add, ALU.max)
                then(V.tensor_tensor_scan(bwd[:, ::-1], with_n[:, ::-1], sT[:, ::-1], -BIG, ALU.add, ALU.max))
                ends_of_groups(True)
                V.tensor_scalar(with_p[:, :], key[:, :], nears[:, 1:2], None, ALU.is_equal)
                then(V.tensor_scalar(with_n[:, :], key[:, :], nears[:, 3:4], None, ALU.is_equal))
                then(V.tensor_tensor(fwd[:, :], fwd[:, :], bwd[:, :], ALU.max))
                for near, at in ((with_p, 0), (with_n, 2)):
                    then(V.tensor_scalar(tmp[:, :], near[:, :], -1.0, BIG, ALU.add, ALU.mult))
                    then(V.scalar_tensor_tensor(fwd[:, :], tmp[:, :], nears[:, at:at + 1], fwd[:, :], ALU.add, ALU.max))
                V.tensor_tensor(sT[:, :], sT[:, :], fwd[:, :], ALU.subtract).then_inc(less_max, 1)
                dve.wait_ge(exp_made, 1)
                V.tensor_tensor_scan(fwd[:, :], same_p[:, :], ex[:, :], 0.0, ALU.mult, ALU.add)
                then(V.tensor_tensor_scan(bwd[:, ::-1], same_n[:, ::-1], ex[:, ::-1], 0.0, ALU.mult, ALU.add))
                ends_of_groups(False)
                then(V.tensor_tensor(fwd[:, :], fwd[:, :], bwd[:, :], ALU.add))
                then(V.tensor_tensor(fwd[:, :], fwd[:, :], ex[:, :], ALU.subtract))
                then(V.scalar_tensor_tensor(fwd[:, :], with_p[:, :], nears[:, 0:1], fwd[:, :], ALU.mult, ALU.add))
                V.scalar_tensor_tensor(fwd[:, :], with_n[:, :], nears[:, 2:3], fwd[:, :],
                                       ALU.mult, ALU.add).then_inc(summed, 1)
                dve.wait_ge(inv_made, 1)
                V.tensor_tensor(alpha[:, 1:], ex[:, :], fwd[:, :], ALU.mult).then_inc(alpha_made, 1)
                dve.wait_ge(alpha_turned, 1)
                for j in range(GT):
                    V.tensor_copy(weights[:, j::GT, :], p_s[j][:, 0:P].rearrange("p (g h) -> p g h", h=HEADS))


def add_and_norm(nc, c, x2, sums, x3):
    with Stage(nc, "combine") as st:
        xt, res = st.slots(st.sb, "xt", 4, [P, D]), st.slots(st.sb, "res", 4, [P, D])
        x_in, stored = st.slots(st.sem, "x_in", 4), st.slots(st.sem, "stored", 4)
        summed = st.sem("summed")
        agg = NodeGather(nc, st, c, sums, summed)
        norm = LayerNorm(nc, st, c, "norm", 4)

        with nc.Block() as block:
            @block.sync
            def _(sp):
                def load(t, s):
                    wait(sp, norm.made, t - 3)
                    sp.dma_start(xt[s][:, :], rows(x2, t)).then_inc(x_in[s], 16)

                def store(t, s):
                    wait(sp, norm.made, t + 1)
                    sp.dma_start(rows(x3, t), res[s][:, :]).then_inc(stored[s], 16)

                over_tiles(sp, NT, 4, (0, load), (3, store))
                for s in range(4):
                    sp.wait_ge(stored[s], 16 * len(range(s, NT, 4)))

            @block.gpsimd
            def _(pool):
                over_tiles(pool, NT, 4, (0, lambda t, s: agg.stage_and_gather(pool, t, s)))

            @block.vector
            def _(dve):
                def add(t, s):
                    wait(dve, x_in[s], landed(t, s, 4))
                    wait(dve, agg.landed[s], landed(t, s, 4))
                    nc.vector.tensor_tensor(xt[s][:, :], xt[s][:, :], agg.rows[s][:, :], ALU.add).then_inc(summed, 1)
                    wait(dve, summed, t + 1)
                    norm.sums(dve, xt[s][:, :], t, s)

                def scale(t, s):
                    wait(dve, stored[s], landed(t, s, 4) - 16)
                    norm.scale(dve, res[s][:, :], xt[s][:, :], t, s)

                over_tiles(dve, NT, 4, (0, add), (1, scale))

            @block.scalar
            def _(act):
                over_tiles(act, NT, 4, (0, lambda t, s: norm.root(act, t, s)))


def last_layer(nc, c, x3, sums, W_self, W_neigh, b, out):
    with Stage(nc, "last") as st:
        w_in = [st.sb(f"w_in{n}", [P, KC, D]) for n in range(2)]
        w = Halves(st, "w", [P, 2 * KC, D], 1)
        bias = st.sb("bias", [P, D])
        xt, again = st.slots(st.sb, "xt", 2, [P, D]), st.slots(st.sb, "again", 4, [P, D])
        mean = st.slots(st.sb, "mean", 2, [P, D])
        xaT = Halves(st, "xaT", [P, 2 * KC, P])
        v, res = st.slots(st.sb, "v", 2, [P, D]), st.slots(st.sb, "res", 2, [P, D])
        p_x, p_agg, p_out = (st.slots(st.ps, n, 2) for n in ("p_x", "p_agg", "p_out"))
        p_w = st.slots(st.ps, "p_w", 2)
        weights, w_turned = st.sem("weights"), st.sem("w_turned")
        x_in, again_in, stored = (st.slots(st.sem, "x_in", 2), st.slots(st.sem, "again_in", 4),
                                  st.slots(st.sem, "stored", 2))
        averaged, turned, product, v_step, summed = (
            st.sem(n) for n in ("averaged", "turned", "product", "v_step", "summed"))
        agg = NodeGather(nc, st, c, sums, averaged)
        norm = LayerNorm(nc, st, c, "norm")

        with nc.Block() as block:
            @block.sync
            def _(sp):
                for n, m in enumerate((W_self, W_neigh)):
                    sp.dma_start(w_in[n][:, :, :], m.rearrange("(k p) n -> p k n", p=P)).then_inc(weights, 16)
                sp.dma_start(bias[:, :], row_of_all(b)).then_inc(weights, 16)

                def load(t, s):
                    wait(sp, turned, t - 1)
                    sp.dma_start(xt[s % 2][:, :], rows(x3, t)).then_inc(x_in[s % 2], 16)

                def load_again(t, s):
                    wait(sp, summed, t - 3)
                    sp.dma_start(again[s][:, :], rows(x3, t)).then_inc(again_in[s], 16)

                def store(t, s):
                    wait(sp, norm.made, t + 1)
                    if isinstance(t, int) and t == NT - 1:
                        sp.dma_start(out[t * P:N, :], res[s % 2][0:LAST, :]).then_inc(stored[s % 2], 16)
                    else:
                        sp.dma_start(rows(out, t), res[s % 2][:, :]).then_inc(stored[s % 2], 16)

                over_tiles(sp, NT, 4, (1, load), (3, load_again), (6, store))
                for s in range(2):
                    sp.wait_ge(stored[s], 16 * len(range(s, NT, 2)))

            @block.gpsimd
            def _(pool):
                over_tiles(pool, NT, 4, (0, lambda t, s: agg.stage_and_gather(pool, t, s)))

            @block.vector
            def _(dve):
                dve.wait_ge(weights, 48)
                for i in range(2 * KC):
                    dve.wait_ge(w.hi_made, i + 1)
                    nc.vector.tensor_tensor(w.lo[0][:, i, :], p_w[i % 2][:, :], w.hi[0][:, i, :], ALU.subtract)\
                        .then_inc(w.made, 1)

                def rest(t, s):
                    wait(dve, xaT.hi_made, 2 * t + 2)
                    wait(dve, product, t - 1)
                    for n, bank in enumerate((p_x[s % 2], p_agg[s % 2])):
                        ins = rest_of_blocks(nc, xaT.lo[s % 2][:, n * KC:(n + 1) * KC, :], bank,
                                             xaT.hi[s % 2][:, n * KC:(n + 1) * KC, :])
                    ins.then_inc(xaT.made, 1)

                def average(t, s):
                    wait(dve, agg.landed[s], landed(t, s, 4))
                    wait(dve, turned, t - 1)
                    nc.vector.tensor_scalar(mean[s % 2][:, :], agg.rows[s][:, :], c["inv_deg"][:, bass.ds(t, 1)], None,
                                            ALU.mult).then_inc(averaged, 1)

                def activate(t, s):
                    wait(dve, product, t + 1)
                    wait(dve, again_in[s], landed(t, s, 4))
                    nc.vector.tensor_tensor(v[s % 2][:, :], p_out[s % 2][:, :], bias[:, :], ALU.add).then_inc(v_step, 1)
                    wait(dve, v_step, t + 1)
                    nc.vector.scalar_tensor_tensor(v[s % 2][:, :], v[s % 2][:, :], 0.0, again[s][:, :],
                                                   ALU.max, ALU.add).then_inc(summed, 1)
                    wait(dve, summed, t + 1)
                    norm.sums(dve, v[s % 2][:, :], t, s % 2)

                def scale(t, s):
                    wait(dve, stored[s % 2], landed(t, s % 2, 2) - 16)
                    norm.scale(dve, res[s % 2][:, :], v[s % 2][:, :], t, s % 2)

                over_tiles(dve, NT, 4, (2, average), (3, rest), (5, activate), (5, scale))

            @block.scalar
            def _(act):
                for n in range(2):
                    for k in range(KC):
                        i = n * KC + k
                        act.wait_ge(w_turned, i + 1)
                        nc.scalar.copy(w.hi[0][:, i, :], p_w[i % 2][:, :]).then_inc(w.hi_made, 1)

                def copy_turned(t, s):
                    wait(act, turned, t + 1)
                    wait(act, product, t - 1)
                    for n, bank in enumerate((p_x[s % 2], p_agg[s % 2])):
                        copy_blocks(nc, xaT.hi[s % 2][:, n * KC:(n + 1) * KC, :], bank).then_inc(xaT.hi_made, 1)

                over_tiles(act, NT, 4, (3, copy_turned), (5, lambda t, s: norm.root(act, t, s % 2)))

            @block.tensor
            def _(pe):
                pe.wait_ge(weights, 48)
                for n in range(2):
                    for k in range(KC):
                        i = n * KC + k
                        if i >= 2:
                            pe.wait_ge(w.made, i - 1)
                        for m in range(KC):
                            ins = nc.tensor.transpose(p_w[i % 2][:, m * P:(m + 1) * P],
                                                      w_in[n][:, m, k * P:(k + 1) * P], c["ident"][:, :])
                        ins.then_inc(w_turned, 1)
                pe.wait_ge(w.made, 2 * KC)

                def turn(t, s):
                    wait(pe, x_in[s % 2], landed(t, s % 2, 2))
                    wait(pe, averaged, t + 1)
                    wait(pe, xaT.made, t - 1)
                    turn_blocks(nc, c, p_x[s % 2], xt[s % 2])
                    turn_blocks(nc, c, p_agg[s % 2], mean[s % 2]).then_inc(turned, 1)

                def multiply(t, s):
                    wait(pe, xaT.made, t + 1)
                    wait(pe, v_step, t - 1)
                    multiply_halves(nc, p_out[s % 2][:, :], xaT, s % 2, range(2 * KC), w, range(2 * KC))\
                        .then_inc(product, 1)

                over_tiles(pe, NT, 4, (3, turn), (4, multiply))


def build(nc, ins, out):
    with ExitStack() as ctx:
        def sb(name, shape, dt=F32):
            return ctx.enter_context(nc.sbuf_tensor("all_" + name, shape, dt))

        def dram(name, shape, dt=F32):
            return nc.dram_tensor(name, shape, dt).ap()

        SEMS[:] = [ctx.enter_context(nc.semaphore(f"signal{i}")) for i in range(DMA_SIGNALS + SIGNALS)]
        ids = [s.num for s in SEMS]
        assert max(ids) - min(ids) == len(ids) - 1 and sorted(ids) in (ids, ids[::-1])
        DMA_SEMS[:], SEMS[:] = SEMS[:DMA_SIGNALS], SEMS[DMA_SIGNALS:]

        c = {n: sb(n, [P, P]) for n in ("ident", "ones", "below", "upto", "count")}
        for n in ("has_edges", "inv_deg", "sum_row"):
            c[n] = sb(n, [P, NT])
        c["sum_row_i"] = sb("sum_row_i", [P, NT], I32)
        for n in ("src_list", "dst_list", "edge_list"):
            c[n] = sb(n, [P, NET], I32)
        c["keys"] = sb("keys", [P, GROUPS * GT])
        c["same"] = sb("same", [P, NET, P], BF16)
        c["two"], c["eps"] = sb("two", [P, 1]), sb("eps", [P, 1])
        sorted_edges, edge_keys = dram("sorted_edges", [NSORT, 3], I32), dram("edge_keys", [NET, P])
        from_src, from_dst = dram("from_src", [NP, D]), dram("from_dst", [NP, D])
        sums = [dram(f"sums{n}", [ZROW + 1, D]) for n in range(4)]
        x1, x2, x3, y, wx = (dram(n, [NP, D]) for n in ("x1", "x2", "x3", "y", "wx"))
        uv = dram("uv", [NP, 2 * HEADS])
        x = ins["x"]

        make_constants(nc, c)
        sort_edges(nc, c, ins["src"], ins["dst"], sorted_edges, edge_keys)
        with nc.sbuf_tensor("attrT", [DE, NET, P], F32) as attrT:
            node_products(nc, c, x, ins["edge_attr_64"], ins["L0_gnn_W1"], ins["L0_gnn_b1"], from_src, from_dst, attrT)
            edge_messages(nc, c, from_src, from_dst, attrT, ins["L0_gnn_W1"], ins["L0_gnn_W2"], ins["L0_gnn_b2"], sums[0])
        with nc.sbuf_tensor("stats", [P, KC, NT, 6], F32) as stats, \
                nc.sbuf_tensor("first_rows", [P, D], F32) as first_rows, \
                nc.sbuf_tensor("other_rows", [P, D], F32) as other_rows:
            update_nodes(nc, c, x, sums[0], *(ins["L0_gnn_" + n] for n in ("W3", "b3", "W4", "b4", "gamma", "beta")),
                         x1, stats)
            attention(nc, c, x1, *(ins["L1_gnn_" + n] for n in ("Wq", "Wk", "Wv", "Wo", "proj")),
                      first_rows[:, :], other_rows[:, :])
            segment_sums(nc, c, "sums1", x1, sums[1])
            with nc.sbuf_tensor("stats2", [P, KC, NT, 6], F32) as stats2:
                conv_nodes(nc, c, x1, sums[1], *(ins["L1_gnn_" + n] for n in ("W_conv", "b_conv", "norm1_g", "norm1_b")),
                           stats, first_rows[:, :], other_rows[:, :], y, stats2)
                head_products(nc, c, x1, y, ins["L1_gnn_norm2_g"], ins["L1_gnn_norm2_b"], stats2,
                              *(ins["L2_gnn_" + n] for n in ("Ws", "Wb", "a_w", "a_b")), x2, wx, uv)
        with nc.sbuf_tensor("weights", [P, GROUPS * GT, HEADS], F32) as weights:
            edge_softmax(nc, c, uv, weights)
            segment_sums(nc, c, "sums2", wx, sums[2], weights)
        add_and_norm(nc, c, x2, sums[2], x3)
        segment_sums(nc, c, "sums3", x3, sums[3])
        last_layer(nc, c, x3, sums[3], ins["L3_gnn_W_self"], ins["L3_gnn_W_neigh"], ins["L3_gnn_b"], out)


def kernel(**inputs):
    import numpy as _np
    import concourse.bacc as _bacc
    from concourse import mybir as _mybir
    from concourse.bass_utils import run_bass_kernel_spmd as _run

    nc = _bacc.Bacc("TRN2", target_bir_lowering=False, num_devices=1)
    arrays, args = {}, {}
    for name in inputs:
        a = _np.ascontiguousarray(inputs[name])
        arrays[f"in_{name}_dram"] = a
        args[name] = nc.dram_tensor(f"in_{name}_dram", a.shape, _mybir.dt.from_np(a.dtype), kind="ExternalInput").ap()
    out = nc.dram_tensor("out_0_dram", (N, D), F32, kind="ExternalOutput").ap()
    build(nc, args, out)
    r = _run(nc, [arrays], core_ids=[0])
    return r.results[0]["out_0_dram"]
```

```python
from contextlib import ExitStack

import concourse.bass as bass
from concourse import mybir

F32 = mybir.dt.float32
BF16 = mybir.dt.bfloat16
F32R = mybir.dt.float32r
I32 = mybir.dt.int32
ALU = mybir.AluOpType
ACT = mybir.ActivationFunctionType

P = 128
N = 10000
E = 10000
D = 512
KC = D // P
DE = 64
REC = 2 + DE
NPROD = 3
NT = -(-N // P)
LAST = N - (NT - 1) * P
NP = NT * P
NET = -(-E // P)
NSORT = NET * P
NOKEY = NP - 1
ZROW = NET * P
SC = 80
SR = E // SC
HEADS = 8
DH = D // HEADS
GROUPS = P // HEADS
GT = -(-NET // GROUPS)
GE = GT * P
EPS = 1e-5
EXP_AND_LN = 6
BIG = 1e30


def wait(eng, signal, value):
    if isinstance(value, int) and value <= 0:
        return
    eng.wait_ge(signal, value)


def over_tiles(eng, tiles, unroll, *stages):
    depth = max(lag for lag, _ in stages)
    first = min(-(-(depth + unroll + 1) // unroll) * unroll, tiles)
    last = first + max(tiles - 1 - first, 0) // unroll * unroll

    def peeled(t):
        for lag, fn in stages:
            if 0 <= t - lag < tiles:
                fn(t - lag, (t - lag) % unroll)

    for t in range(first):
        peeled(t)
    if last > first:
        with eng.Fori(0, (last - first) // unroll, 1) as turn:
            step = turn * unroll + first
            for u in range(unroll):
                for lag, fn in stages:
                    fn(step + (u - lag), (u - lag) % unroll)
    for t in range(last, tiles + depth):
        peeled(t)


def first_tiles(n, fn):
    return lambda t, slot: None if isinstance(t, int) and t >= n else fn(t, slot)


def landed(t, slot, slots):
    if isinstance(t, int):
        return 16 * (t // slots + 1)
    return (t - slot) * (16 // slots) + 16


DMA_SIGNALS, SIGNALS = 8, 80


class Stage:

    def __init__(self, nc, name):
        self.nc, self.name, self.used, self.dmas = nc, name, 0, 0

    def __enter__(self):
        self.ctx = ExitStack()
        self.ctx.__enter__()
        return self

    def sb(self, name, shape, dt=F32):
        return self.ctx.enter_context(self.nc.sbuf_tensor(f"{self.name}_{name}", shape, dt))

    def ps(self, name, shape=(P, D), dt=F32):
        return self.ctx.enter_context(self.nc.psum_tensor(f"{self.name}_{name}", list(shape), dt))

    def sem(self, name):
        self.used += 1
        return SEMS[self.used - 1]

    def dma_sem(self, name):
        self.dmas += 1
        return DMA_SEMS[self.dmas - 1]

    def slots(self, make, name, n, *a):
        return [make(f"{name}{i}", *a) for i in range(n)]

    def __exit__(self, *exc):
        if exc[0] is None:
            ids = [s.num for s in DMA_SEMS[:self.dmas] + SEMS[:self.used]]
            if self.dmas:
                first = min(s.num for s in DMA_SEMS[:self.dmas])
                self.nc.gpsimd.dma_reset(range(first, first + self.dmas))
            self.nc.all_engine_barrier(sems_to_clear=range(min(ids), max(ids) + 1))
        return self.ctx.__exit__(*exc)


DMA_SEMS, SEMS = [], []


def row_of_all(v, parts=P):
    return bass.AP(tensor=v.tensor, offset=v.offset, ap=[[0, parts], [1, v.shape[-1]]])


def make_constants(nc, c):
    with Stage(nc, "constants") as st:
        done, copied = st.sem("const_made"), st.sem("const_copied")
        counts = st.sb("counts_i", [P, P], I32)
        with nc.Block() as block:
            @block.scalar
            def _(act):
                nc.scalar.add_instruction(mybir.InstLoadActFuncSet(name=nc.get_next_instruction_name(),
                                                                   act_func_set_id=EXP_AND_LN))

            @block.gpsimd
            def _(pool):
                nc.gpsimd.memset(c["ident"][:, :], 0.0).then_inc(done, 1)
                nc.gpsimd.memset(c["ones"][:, :], 1.0).then_inc(done, 1)
                nc.gpsimd.memset(c["below"][:, :], 1.0).then_inc(done, 1)
                nc.gpsimd.memset(c["upto"][:, :], 1.0).then_inc(done, 1)
                nc.gpsimd.memset(c["two"][:, :], 2.0)
                nc.gpsimd.memset(c["eps"][:, :], EPS)
                nc.gpsimd.iota(counts[:, :], [[1, P]], base=0, channel_multiplier=0).then_inc(done, 1)
                pool.wait_ge(done, 5)
                nc.gpsimd.affine_select(out=c["ident"][:, :], in_=c["ident"][:, :], compare_op=ALU.not_equal,
                                        fill=1.0, base=0, pattern=[[-1, P]], channel_multiplier=1)
                nc.gpsimd.affine_select(out=c["below"][:, :], in_=c["below"][:, :], compare_op=ALU.is_gt,
                                        fill=0.0, base=0, pattern=[[-1, P]], channel_multiplier=1)
                nc.gpsimd.affine_select(out=c["upto"][:, :], in_=c["upto"][:, :], compare_op=ALU.is_ge,
                                        fill=0.0, base=0, pattern=[[1, P]], channel_multiplier=-1)

            @block.vector
            def _(dve):
                dve.wait_ge(done, 5)
                nc.vector.tensor_copy(c["count"][:, :], counts[:, :]).then_inc(copied, 1)


def load_weights(eng, sem, pairs):
    for tile, w in pairs:
        eng.dma_start(tile, w.rearrange("(k p) n -> p k n", p=P)).then_inc(sem, 16)


class Halves:

    def __init__(self, st, name, shape, slots=2):
        self.hi = st.slots(st.sb, name + "_hi", slots, shape, F32R)
        self.lo = st.slots(st.sb, name + "_lo", slots, shape, F32R)
        self.hi_made, self.made = st.sem(name + "_hi_made"), st.sem(name + "_made")


def split_weights(nc, st, name, w):
    halves = Halves(st, name, w.shape, 1)

    def fill(dve):
        for k in range(w.shape[1]):
            nc.vector.tensor_copy(halves.hi[0][:, k, :], w[:, k, :]).then_inc(halves.hi_made, 1)
            dve.wait_ge(halves.hi_made, k + 1)
            nc.vector.tensor_tensor(halves.lo[0][:, k, :], w[:, k, :], halves.hi[0][:, k, :], ALU.subtract)\
                .then_inc(halves.made, 1)

    return halves, fill


def multiply_halves(nc, out, x, s, x_blocks, w, w_blocks):
    pairs = list(zip(x_blocks, w_blocks))
    products = [(x.lo[s], w.hi[0], pair) for pair in pairs]
    products += [(x.hi[s], half, pair) for pair in pairs for half in (w.lo[0], w.hi[0])]
    for n, (x_half, w_half, (i, j)) in enumerate(products):
        ins = nc.tensor.matmul(out, x_half[:, i, :], w_half[:, j, :], start=n == 0, stop=n == len(products) - 1)
    return ins


def copy_blocks(nc, dest, bank):
    return nc.scalar.copy(dest, bank[:, :].rearrange("p (k m) -> p k m", k=KC))


def rest_of_blocks(nc, lo, bank, hi):
    return nc.vector.tensor_tensor(lo, bank[:, :].rearrange("p (k m) -> p k m", k=KC), hi, ALU.subtract)


def turn_blocks(nc, c, p_turn, v):
    for k in range(KC):
        ins = nc.tensor.transpose(p_turn[:, k * P:(k + 1) * P], v[:, k * P:(k + 1) * P], c["ident"][:, :])
    return ins


def rows(dram, t):
    return dram[bass.ds(t * P, P), :]


def sort_and_multiply(nc, c, src, dst, attr, sorted_edges, x, W1, b1, W3, b3, products):
    with Stage(nc, "sort") as st:
        dst_i, src_i = st.sb("dst_i", [SR, SC], I32), st.sb("src_i", [SR, SC], I32)
        hi_i, lo_i = st.sb("hi_i", [SR, SC], I32), st.sb("lo_i", [SR, SC], I32)
        dst_f, hi_f, lo_f = (st.sb(n, [SR, SC]) for n in ("dst_f", "hi_f", "lo_f"))
        rec = st.sb("rec", [SR, SC, REC])
        hi_all = st.sb("hi_all", [SR, SC, NT], BF16)
        lo_all = st.sb("lo_all", [SR, SC, P], BF16)
        deg, ends, excl = st.sb("deg", [P, NT]), st.sb("ends", [P, NT]), st.sb("excl", [P, NT])
        first_pos = st.sb("first_pos", [P, NT])
        tmp = [st.sb(f"tmp{i}", [P, NT]) for i in range(3)]
        count = [st.sb(f"count{i}", [NT, P]) for i in range(2)]
        oh = [st.sb(f"oh{i}", [SR, NT]) for i in range(2)]
        ol = [st.sb(f"ol{i}", [SR, P]) for i in range(2)]
        dg = [st.sb(f"dg{i}", [SR, SR]) for i in range(2)]
        oht = [st.sb(f"oht{i}", [NT, SR]) for i in range(2)]
        junk = [st.sb(f"junk{i}", [SR, P]) for i in range(2)]
        before = [st.sb(f"before{i}", [SR, 2]) for i in range(2)]
        rank = st.sb("rank", [SR, SC])
        pos_i = [st.sb(f"pos_i{i}", [SR, 1], I32) for i in range(4)]
        rec_s = [st.sb(f"rec_s{i}", [SR, REC]) for i in range(4)]
        padding = st.sb("padding", [NSORT - E, REC])
        p_turned, p_tile, p_look = st.ps("p_turned"), st.ps("p_tile"), st.ps("p_look")
        loaded, attr_in, split, hot, hist, prefix = (st.sem(n) for n in
                                                     ("loaded", "attr_in", "split", "hot", "hist", "prefix"))
        end_sum, based, first_t = (st.sem(n) for n in ("end_sum", "based", "first_t"))
        hots, tile_hist, oht_made, g_done = (st.sem(n) for n in ("hots", "tile_hist", "oht_made", "g_done"))
        counted, picked, ranked = (st.sem(n) for n in ("counted", "picked", "ranked"))
        packed, staged = st.sem("packed"), st.sem("staged")
        scattered = [st.dma_sem(f"scattered{i}") for i in range(4)]
        padded = st.sem("padded")
        assert NT <= P and SR * SC == E
        w = st.sb("w", [P, NPROD * KC, D])
        w_halves, fill_w = split_weights(nc, st, "w", w)
        bias = {0: st.sb("bias1", [P, D]), 2: st.sb("bias3", [P, D])}
        xt = st.slots(st.sb, "xt", 2, [P, D])
        xT = Halves(st, "xT", [P, KC, P])
        res = [st.slots(st.sb, f"res{n}_", 2, [P, D]) for n in range(NPROD)]
        p_x = st.slots(st.ps, "p_x", 2)
        p_out = [st.ps(f"p_out{n}") for n in range(NPROD)]
        weights, zeroed, turned = st.sem("weights"), st.sem("zeroed"), st.sem("turned")
        x_in = st.slots(st.sem, "x_in", 2)
        product, evacuated = st.slots(st.sem, "product", NPROD), st.slots(st.sem, "evacuated", NPROD)
        stored = [st.slots(st.sem, f"stored{n}_", 2) for n in range(NPROD)]

        with nc.Block() as block:
            @block.sync
            def _(sp):
                sp.dma_start(dst_i[:, :], dst.rearrange("(p t) -> p t", t=SC)).then_inc(loaded, 16)
                sp.dma_start(src_i[:, :], src.rearrange("(p t) -> p t", t=SC)).then_inc(loaded, 16)
                load_weights(sp, weights, [(w[:, 0:2 * KC, :], W1[0:2 * D, :]), (w[:, 2 * KC:, :], W3[0:D, :])])
                sp.dma_start(bias[0][:, :], row_of_all(b1)).then_inc(weights, 16)
                sp.dma_start(bias[2][:, :], row_of_all(b3)).then_inc(weights, 16)
                sp.dma_start(rec[:, :, 2:], attr.rearrange("(p t) d -> p t d", t=SC)).then_inc(attr_in, 16)
                sp.wait_ge(packed, 2)
                sp.dma_start(sorted_edges[E:NSORT, :], padding[:, :]).then_inc(padded, 16)
                sp.wait_ge(zeroed, 2)

                def load(t, s):
                    wait(sp, turned, t - 1)
                    if isinstance(t, int) and t == NT - 1:
                        sp.dma_start(xt[s % 2][0:LAST, :], x[t * P:N, :]).then_inc(x_in[s % 2], 16)
                    else:
                        sp.dma_start(xt[s % 2][:, :], rows(x, t)).then_inc(x_in[s % 2], 16)

                def store(t, s):
                    for n, dram in enumerate(products):
                        wait(sp, evacuated[n], t + 1)
                        sp.dma_start(rows(dram, t), res[n][s % 2][:, :]).then_inc(stored[n][s % 2], 16)

                over_tiles(sp, NT, 4, (0, load), (2, store))
                for s in range(2):
                    for n in range(NPROD):
                        sp.wait_ge(stored[n][s], 16 * len(range(s, NT, 2)))
                sp.wait_ge(padded, 16)

            @block.vector
            def _(dve):
                dve.wait_ge(loaded, 32)
                nc.vector.tensor_scalar(hi_i[:, :], dst_i[:, :], 7, None, ALU.logical_shift_right).then_inc(split, 1)
                nc.vector.tensor_scalar(lo_i[:, :], dst_i[:, :], P - 1, None, ALU.bitwise_and).then_inc(split, 1)
                nc.vector.tensor_copy(dst_f[:, :], dst_i[:, :]).then_inc(split, 1)
                dve.wait_ge(split, 2)
                nc.vector.tensor_copy(hi_f[:, :], hi_i[:, :]).then_inc(split, 1)
                nc.vector.tensor_copy(lo_f[:, :], lo_i[:, :]).then_inc(split, 1)
                dve.wait_ge(split, 5)
                nc.vector.tensor_tensor(hi_all[:, :, :], hi_f[:, :].unsqueeze(2).to_broadcast([SR, SC, NT]),
                                        c["count"][0:SR, 0:NT].unsqueeze(1).to_broadcast([SR, SC, NT]),
                                        ALU.is_equal).then_inc(hot, 1)
                nc.vector.tensor_tensor(lo_all[:, :, :], lo_f[:, :].unsqueeze(2).to_broadcast([SR, SC, P]),
                                        c["count"][0:SR, :].unsqueeze(1).to_broadcast([SR, SC, P]),
                                        ALU.is_equal).then_inc(hot, 1)
                dve.wait_ge(weights, 64)
                fill_w(dve)
                dve.wait_ge(hist, 1)
                nc.vector.tensor_copy(deg[:, :], p_tile[:, 0:NT]).then_inc(prefix, 1)
                dve.wait_ge(prefix, 1)
                nc.vector.tensor_tensor_scan(tmp[0][:, :], c["ones"][:, 0:NT], deg[:, :], 0.0,
                                             ALU.mult, ALU.add).then_inc(prefix, 1)
                dve.wait_ge(prefix, 2)
                nc.vector.tensor_tensor(excl[:, :], tmp[0][:, :], deg[:, :], ALU.subtract).then_inc(prefix, 1)
                dve.wait_ge(end_sum, 1)
                nc.vector.tensor_copy(ends[:, :], p_look[:, 0:NT]).then_inc(based, 1)
                dve.wait_ge(based, 1)
                nc.vector.tensor_tensor(first_pos[:, :], ends[:, :], deg[:, :], ALU.subtract).then_inc(based, 1)
                nc.vector.tensor_scalar(tmp[2][:, :], ends[:, :], float(-1 - ZROW), None, ALU.add).then_inc(based, 1)
                nc.vector.tensor_scalar(c["has_edges"][:, :], deg[:, :], 0.0, None, ALU.is_gt).then_inc(based, 1)
                nc.vector.tensor_scalar(tmp[0][:, :], deg[:, :], 1.0, None, ALU.max).then_inc(based, 1)
                dve.wait_ge(based, 5)
                nc.vector.reciprocal(c["inv_deg"][:, :], tmp[0][:, :]).then_inc(based, 1)
                nc.vector.tensor_tensor(tmp[1][:, :], tmp[2][:, :], c["has_edges"][:, :], ALU.mult).then_inc(based, 1)
                dve.wait_ge(based, 7)
                nc.vector.tensor_scalar(c["sum_row"][:, :], tmp[1][:, :], float(ZROW), None, ALU.add).then_inc(based, 1)
                dve.wait_ge(first_t, 1)
                nc.vector.tensor_copy(count[0][:, :], p_tile[0:NT, P:2 * P]).then_inc(counted, 1)

                def one_hots(t, s):
                    wait(dve, tile_hist, t - 1)
                    s = s % 2
                    nc.vector.tensor_scalar(oh[s][:, :], c["count"][0:SR, 0:NT], hi_f[:, bass.ds(t, 1)], None,
                                            ALU.is_equal).then_inc(hots, 1)
                    nc.vector.tensor_scalar(ol[s][:, :], c["count"][0:SR, :], lo_f[:, bass.ds(t, 1)], None,
                                            ALU.is_equal).then_inc(hots, 1)
                    nc.vector.tensor_scalar(dg[s][:, :], c["ident"][0:SR, 0:SR], dst_f[:, bass.ds(t, 1)], None,
                                            ALU.mult).then_inc(hots, 1)

                def ranks(t, s):
                    s = s % 2
                    wait(dve, g_done, t + 1)
                    wait(dve, counted, t + 1)
                    nc.vector.tensor_tensor(count[1 - s][:, :], count[s][:, :], p_tile[0:NT, P:2 * P],
                                            ALU.add).then_inc(counted, 1)
                    nc.vector.tensor_tensor_reduce(out=junk[0][:, :], in0=p_look[0:SR, 0:P], in1=ol[s][:, :],
                                                   scale=1.0, scalar=0.0, op0=ALU.mult, op1=ALU.add,
                                                   accum_out=before[s][:, 0:1]).then_inc(picked, 1)
                    nc.vector.scalar_tensor_tensor(junk[1][:, 0:SR], p_tile[0:SR, 2 * P:2 * P + SR],
                                                   dst_f[:, bass.ds(t, 1)], c["below"][0:SR, 0:SR],
                                                   ALU.is_equal, ALU.mult,
                                                   accum_out=before[s][:, 1:2]).then_inc(picked, 1)
                    wait(dve, picked, 2 * t + 2)
                    nc.vector.tensor_tensor(rank[:, bass.ds(t, 1)], before[s][:, 0:1], before[s][:, 1:2],
                                            ALU.add).then_inc(ranked, 1)

                def rest(t, s):
                    wait(dve, xT.hi_made, t + 1)
                    wait(dve, product[NPROD - 1], t - 1)
                    rest_of_blocks(nc, xT.lo[s % 2][:, :, :], p_x[s % 2], xT.hi[s % 2][:, :, :]).then_inc(xT.made, 1)

                def evacuate(n, t, s):
                    wait(dve, product[n], t + 1)
                    wait(dve, stored[n][s % 2], landed(t, s % 2, 2) - 16)
                    nc.vector.tensor_tensor(res[n][s % 2][:, :], p_out[n][:, :], bias[n][:, :], ALU.add)\
                        .then_inc(evacuated[n], 1)

                over_tiles(dve, SC, 4, (1, first_tiles(NT, rest)), (2, first_tiles(NT, lambda t, s: evacuate(0, t, s))),
                           (1, ranks), (0, one_hots), (2, first_tiles(NT, lambda t, s: evacuate(2, t, s))))

            @block.tensor
            def _(pe):
                pe.wait_ge(hot, 2)
                nc.tensor.matmul(p_tile[:, 0:NT], lo_all[:, 0, :], hi_all[:, 0, :], start=True, stop=False)
                with pe.Fori(1, SC - 1, 1) as t:
                    nc.tensor.matmul(p_tile[:, 0:NT], lo_all[:, bass.ds(t, 1), :].rearrange("p o l -> p (o l)"),
                                     hi_all[:, bass.ds(t, 1), :].rearrange("p o l -> p (o l)"), start=False, stop=False)
                nc.tensor.matmul(p_tile[:, 0:NT], lo_all[:, SC - 1, :], hi_all[:, SC - 1, :],
                                 start=False, stop=True).then_inc(hist, 1)
                pe.wait_ge(prefix, 3)
                nc.tensor.matmul(p_look[:, 0:NT], c["upto"][:, :], deg[:, :], start=True, stop=False)
                nc.tensor.matmul(p_look[:, 0:NT], c["ones"][:, :], excl[:, :], start=False, stop=True).then_inc(end_sum, 1)
                pe.wait_ge(based, 2)
                nc.tensor.transpose(p_tile[0:NT, P:2 * P], first_pos[:, :], c["ident"][:, :]).then_inc(first_t, 1)
                pe.wait_ge(w_halves.made, NPROD * KC)

                def tile_histogram(t, s):
                    s = s % 2
                    wait(pe, hots, 3 * t + 3)
                    if isinstance(t, int) and t == 0:
                        pe.wait_ge(counted, 1)
                    wait(pe, ranked, t)
                    wait(pe, oht_made, t)
                    nc.tensor.transpose(p_turned[0:NT, 0:SR], oh[s][:, :], c["ident"][0:SR, 0:SR])
                    nc.tensor.matmul(p_tile[0:NT, P:2 * P], oh[s][:, :], ol[s][:, :], start=True, stop=True)
                    nc.tensor.matmul(p_tile[0:SR, 2 * P:2 * P + SR], c["ones"][0:SR, 0:SR], dg[s][:, :],
                                     start=True, stop=True).then_inc(tile_hist, 1)

                def look_up(t, s):
                    wait(pe, oht_made, t + 1)
                    wait(pe, counted, t + 1)
                    nc.tensor.matmul(p_look[0:SR, 0:P], oht[s % 2][:, :], count[s % 2][:, :],
                                     start=True, stop=True).then_inc(g_done, 1)

                def turn(t, s):
                    wait(pe, x_in[s % 2], landed(t, s % 2, 2))
                    wait(pe, xT.made, t - 1)
                    turn_blocks(nc, c, p_x[s % 2], xt[s % 2]).then_inc(turned, 1)

                def multiply(n, t, s):
                    wait(pe, xT.made, t + 1)
                    wait(pe, evacuated[n], t)
                    multiply_halves(nc, p_out[n][:, :], xT, s % 2, range(KC), w_halves,
                                    range(n * KC, (n + 1) * KC)).then_inc(product[n], 1)

                over_tiles(pe, SC, 4, (1, tile_histogram), (1, first_tiles(NT, turn)),
                           (2, first_tiles(NT, lambda t, s: multiply(0, t, s))), (1, look_up),
                           (2, first_tiles(NT, lambda t, s: multiply(1, t, s))),
                           (2, first_tiles(NT, lambda t, s: multiply(2, t, s))))

            @block.scalar
            def _(act):
                def copy_turned(t, s):
                    wait(act, tile_hist, t + 1)
                    wait(act, g_done, t - 1)
                    nc.scalar.copy(oht[s % 2][:, :], p_turned[0:NT, 0:SR]).then_inc(oht_made, 1)

                def copy_x(t, s):
                    wait(act, turned, t + 1)
                    wait(act, product[NPROD - 1], t - 1)
                    copy_blocks(nc, xT.hi[s % 2][:, :, :], p_x[s % 2]).then_inc(xT.hi_made, 1)

                def evacuate(t, s):
                    wait(act, product[1], t + 1)
                    wait(act, stored[1][s % 2], landed(t, s % 2, 2) - 16)
                    nc.scalar.copy(res[1][s % 2][:, :], p_out[1][:, :]).then_inc(evacuated[1], 1)

                over_tiles(act, SC, 4, (1, copy_turned), (1, first_tiles(NT, copy_x)), (2, first_tiles(NT, evacuate)))

            @block.gpsimd
            def _(pool):
                nc.gpsimd.memset(padding[:, :], 0.0).then_inc(packed, 1)
                pool.wait_ge(packed, 1)
                nc.gpsimd.memset(padding[:, 1:2], float(NOKEY)).then_inc(packed, 1)
                for s in range(2):
                    nc.gpsimd.memset(xt[s][:, :], 0.0).then_inc(zeroed, 1)
                pool.wait_ge(loaded, 32)
                nc.gpsimd.tensor_copy(rec[:, :, 0], src_i[:, :]).then_inc(packed, 1)
                nc.gpsimd.tensor_copy(rec[:, :, 1], dst_i[:, :]).then_inc(packed, 1)
                pool.wait_ge(based, 8)
                nc.gpsimd.tensor_copy(c["sum_row_i"][:, :], c["sum_row"][:, :]).then_inc(packed, 1)
                pool.wait_ge(packed, 5)
                pool.wait_ge(attr_in, 16)

                def send(t, s):
                    nc.gpsimd.indirect_dma_start(out=sorted_edges[:, :], in_=rec_s[s][:, :],
                                                 out_offset=bass.IndirectOffsetOnAxis(ap=pos_i[s][:, 0:1], axis=0),
                                                 in_offset=None).then_inc(scattered[s], 16)

                def stage_and_scatter(t, s):
                    wait(pool, staged, 2 * t)
                    wait(pool, ranked, t + 1)
                    wait(pool, scattered[s], landed(t, s, 4) - 16)
                    nc.gpsimd.tensor_copy(pos_i[s][:, :], rank[:, bass.ds(t, 1)]).then_inc(staged, 1)
                    nc.gpsimd.tensor_copy(rec_s[s][:, :], rec[:, bass.ds(t, 1), :].rearrange("p o c -> p (o c)"))\
                        .then_inc(staged, 1)
                    if not isinstance(t, int) or t > 0:
                        send(t - 1, (s - 1) % 4)

                over_tiles(pool, SC, 4, (0, stage_and_scatter))
                pool.wait_ge(staged, 2 * SC)
                send(SC - 1, (SC - 1) % 4)
                for s in range(4):
                    pool.wait_ge(scattered[s], 16 * SC // 4)


def list_edges(nc, c, sorted_edges, edge_keys):
    with Stage(nc, "list") as st:
        lst = st.sb("lst", [P, NET, 2])
        keys = c["keys"][:, 0:NET]
        key_rows = st.sb("key_rows", [NET, P])
        key_all = st.sb("key_all", [P, NET, P])
        p_key = st.ps("p_key")
        read, keyed, turned, rows, stored, spread = (st.sem(n) for n in
                                                     ("read", "keyed", "turned", "rows", "stored", "spread"))
        same = st.sem("same")
        tile_base, base_f = st.sb("tile_base", [NET, 1], I32), st.sb("base_f", [NET, 1])
        first_key, in_first = st.sb("first_key", [NET, P]), st.sb("in_first", [NET, 1])
        earlier = st.sb("earlier", [NET, NET])
        based, join = st.sem("based"), st.sem("join")

        with nc.Block() as block:
            @block.sync
            def _(sp):
                sp.dma_start(lst[:, :, :], sorted_edges[:, 0:2].rearrange("(t p) c -> p t c", p=P),
                             allow_slow_non_contiguous=True).then_inc(read, 16)
                sp.wait_ge(rows, 1)
                sp.dma_start(edge_keys, key_rows[:, :]).then_inc(stored, 16)
                sp.wait_ge(stored, 16)
                sp.dma_start(key_all[:, :, :], bass.AP(tensor=edge_keys.tensor, offset=edge_keys.offset,
                                                       ap=[[0, P], [P, NET], [1, P]])).then_inc(spread, 16)
                sp.wait_ge(spread, 16)

            @block.vector
            def _(dve):
                dve.wait_ge(read, 16)
                for n, name in enumerate(("src_list", "dst_list")):
                    nc.vector.tensor_copy(c[name][:, :], lst[:, :, n])
                nc.vector.memset(c["keys"][:, NET:], float(NOKEY))
                nc.vector.tensor_copy(keys, lst[:, :, 1]).then_inc(keyed, 1)
                dve.wait_ge(turned, 1)
                nc.vector.tensor_copy(key_rows[:, :], p_key[0:NET, 0:P]).then_inc(rows, 1)
                dve.wait_ge(rows, 1)
                nc.vector.tensor_scalar(first_key[:, :], key_rows[:, :], key_rows[:, 0:1], None, ALU.is_equal)\
                    .then_inc(join, 1)
                nc.vector.tensor_tensor(earlier[:, :], c["upto"][0:NET, 0:NET], c["ident"][0:NET, 0:NET], ALU.subtract)\
                    .then_inc(join, 1)
                dve.wait_ge(based, 1)
                nc.vector.tensor_copy(base_f[:, :], tile_base[:, :]).then_inc(join, 1)
                dve.wait_ge(join, 3)
                nc.vector.tensor_reduce(in_first[:, :], first_key[:, :], mybir.AxisListType.X, ALU.add).then_inc(join, 1)
                dve.wait_ge(join, 4)
                nc.vector.tensor_tensor(c["join_row"][:, :], in_first[:, :], base_f[:, :], ALU.add).then_inc(join, 1)
                dve.wait_ge(spread, 16)
                nc.vector.scalar_tensor_tensor(c["join"][:, :], key_all[0:NET, :, 0], key_rows[:, P - 1:P],
                                               earlier[:, :], ALU.is_equal, ALU.mult).then_inc(join, 1)
                nc.vector.tensor_tensor(c["same"][:, :, :], key_all[:, :, :],
                                        keys.unsqueeze(2).to_broadcast([P, NET, P]),
                                        ALU.is_equal).then_inc(same, 1)

            @block.gpsimd
            def _(pool):
                nc.gpsimd.iota(tile_base[:, :], [[0, 1]], base=-1, channel_multiplier=P).then_inc(based, 1)
                pool.wait_ge(join, 5)
                nc.gpsimd.tensor_copy(c["join_row_i"][:, :], c["join_row"][:, :])

            @block.tensor
            def _(pe):
                pe.wait_ge(keyed, 1)
                nc.tensor.transpose(p_key[0:NET, 0:P], keys, c["ident"][:, :]).then_inc(turned, 1)


class Mish:

    def __init__(self, nc, st, name, slots=2):
        self.nc, self.n = nc, slots
        self.z = st.slots(st.sb, name + "_z", slots, [P, D])
        self.w = st.slots(st.sb, name + "_w", slots, [P, D])
        self.z_made, self.exp_made, self.d_made = (st.sem(f"{name}_{n}") for n in ("z_made", "exp_made", "d_made"))
        self.log_made, self.inv_made = (st.sem(f"{name}_{n}") for n in ("log_made", "inv_made"))
        self.made = st.sem(name + "_made")

    def exp(self, act, t, s):
        wait(act, self.z_made, t + 1)
        wait(act, self.made, t - self.n + 1)
        self.nc.scalar.activation(self.w[s][:, :], self.z[s][:, :], ACT.Exp).then_inc(self.exp_made, 1)

    def product(self, dve, t, s):
        wait(dve, self.exp_made, t + 1)
        self.nc.vector.scalar_tensor_tensor(self.w[s][:, :], self.w[s][:, :], 2.0, self.w[s][:, :],
                                            ALU.add, ALU.mult).then_inc(self.d_made, 1)

    def log(self, act, t, s):
        wait(act, self.d_made, t + 1)
        self.nc.scalar.activation(self.w[s][:, :], self.w[s][:, :], ACT.Ln, bias=self.two[:, 0:1])\
            .then_inc(self.log_made, 1)

    def inverse(self, act, t, s):
        wait(act, self.log_made, t + 1)
        self.nc.scalar.activation(self.w[s][:, :], self.w[s][:, :], ACT.Exp, scale=-1.0).then_inc(self.inv_made, 1)

    def finish(self, dve, out, t, s):
        wait(dve, self.inv_made, t + 1)
        self.nc.vector.scalar_tensor_tensor(out, self.w[s][:, :], 0.5, self.z[s][:, :],
                                            ALU.subtract, ALU.mult).then_inc(self.made, 1)


def edge_messages(nc, c, from_src, from_dst, sorted_edges, W1, W2, b2, sums):
    with Stage(nc, "messages") as st:
        w1 = st.sb("w1", [DE, D])
        w2 = st.sb("w2", [P, KC, D])
        bias = st.sb("bias", [P, D])
        idx = [st.slots(st.sb, f"idx{n}_", 4, [P, 1], I32) for n in range(2)]
        part = [st.slots(st.sb, f"part{n}_", 4, [P, D]) for n in range(2)]
        at_rows, at = st.slots(st.sb, "at_rows", 4, [P, DE]), st.slots(st.sb, "at", 2, [DE, P])
        at_in, at_turned = st.slots(st.sem, "at_in", 4), st.sem("at_turned")
        first, second = Mish(nc, st, "first", 4), Mish(nc, st, "second", 4)
        first.two = second.two = c["two"]
        h = st.slots(st.sb, "h", 2, [P, D])
        hT = Halves(st, "hT", [P, KC, P])
        w2_halves, fill_w2 = split_weights(nc, st, "w2", w2)
        msg = st.slots(st.sb, "msg", 2, [P, D])
        same = st.slots(st.sb, "same", 2, [P, P])
        res = st.slots(st.sb, "res", 2, [P, D])
        zeros = st.sb("zeros", [1, D])
        p_z, p_turn = st.slots(st.ps, "p_z", 2), st.slots(st.ps, "p_turn", 2)
        p_m, p_sum = st.slots(st.ps, "p_m", 2), st.slots(st.ps, "p_sum", 2)
        weights, zeroed, zero_row = st.sem("weights"), st.sem("zeroed"), st.sem("zero_row")
        staged, at_made, z_product, parts_added = (st.sem(n) for n in
                                                   ("staged", "at_made", "z_product", "parts_added"))
        gathered = [st.slots(st.dma_sem, f"gathered{n}_", 4) for n in range(2)]
        turned, m_product, same_made = (st.sem(n) for n in ("turned", "m_product", "same_made"))
        summed, evacuated = st.sem("summed"), st.sem("evacuated")
        stored = st.slots(st.sem, "stored", 2)

        with nc.Block() as block:
            @block.sync
            def _(sp):
                sp.dma_start(w1[:, :], W1[2 * D:2 * D + DE, :]).then_inc(weights, 16)
                load_weights(sp, weights, [(w2[:, :, :], W2)])
                sp.dma_start(bias[:, :], row_of_all(b2)).then_inc(weights, 16)
                sp.wait_ge(zeroed, 1)
                sp.dma_start(sums[ZROW:ZROW + 1, :], zeros[:, :]).then_inc(zero_row, 16)
                sp.wait_ge(zero_row, 16)

                def load(t, s):
                    wait(sp, at_turned, t - 3)
                    sp.dma_start(at_rows[s][:, :], sorted_edges[bass.ds(t * P, P), 2:]).then_inc(at_in[s], 16)

                def store(t, s):
                    wait(sp, evacuated, t + 1)
                    sp.dma_start(rows(sums, t), res[s % 2][:, :]).then_inc(stored[s % 2], 16)

                over_tiles(sp, NET, 4, (0, load), (12, store))
                for s in range(2):
                    sp.wait_ge(stored[s], 16 * len(range(s, NET, 2)))

            @block.gpsimd
            def _(pool):
                nc.gpsimd.memset(zeros[:, :], 0.0).then_inc(zeroed, 1)

                def gather(t, s):
                    for n, table in enumerate((from_src, from_dst)):
                        nc.gpsimd.indirect_dma_start(out=part[n][s][:, :], in_=table[:, :], out_offset=None,
                                                     in_offset=bass.IndirectOffsetOnAxis(ap=idx[n][s][:, 0:1], axis=0))\
                            .then_inc(gathered[n][s], 16)

                def stage_and_gather(t, s):
                    wait(pool, staged, 2 * t)
                    wait(pool, first.z_made, t - 4)
                    for n, lst in enumerate(("src_list", "dst_list")):
                        wait(pool, gathered[n][s], landed(t, s, 4) - 16)
                        nc.gpsimd.tensor_copy(idx[n][s][:, :], c[lst][:, bass.ds(t, 1)]).then_inc(staged, 1)
                    if not isinstance(t, int) or t > 0:
                        gather(t - 1, (s - 1) % 4)

                def last_gather():
                    pool.wait_ge(staged, 2 * NET)
                    pool.wait_ge(first.z_made, NET - 4)
                    gather(NET - 1, (NET - 1) % 4)

                def add_parts(t, s):
                    if isinstance(t, int) and t == NET - 3:
                        last_gather()
                    for n in range(2):
                        wait(pool, gathered[n][s], landed(t, s, 4))
                    nc.gpsimd.tensor_tensor(part[0][s][:, :], part[0][s][:, :], part[1][s][:, :], ALU.add)\
                        .then_inc(parts_added, 1)

                over_tiles(pool, NET, 4, (0, stage_and_gather), (3, add_parts))

            @block.vector
            def _(dve):
                dve.wait_ge(weights, 48)
                fill_w2(dve)

                def rest_of_h(t, s):
                    wait(dve, hT.hi_made, t + 1)
                    wait(dve, m_product, t - 1)
                    rest_of_blocks(nc, hT.lo[s % 2][:, :, :], p_turn[s % 2], hT.hi[s % 2][:, :, :]).then_inc(hT.made, 1)

                def first_z(t, s):
                    wait(dve, z_product, t + 1)
                    wait(dve, parts_added, t + 1)
                    wait(dve, first.made, t - 3)
                    nc.vector.tensor_tensor(first.z[s][:, :], p_z[s % 2][:, :], part[0][s][:, :], ALU.add)\
                        .then_inc(first.z_made, 1)

                def second_z(t, s):
                    wait(dve, m_product, t + 1)
                    wait(dve, second.made, t - 3)
                    nc.vector.scalar_tensor_tensor(second.z[s][:, :], p_m[s % 2][:, :], -2.0, bias[:, :],
                                                   ALU.mult, ALU.add).then_inc(second.z_made, 1)

                def finish_first(t, s):
                    wait(dve, turned, t - 1)
                    first.finish(dve, h[s % 2][:, :], t, s)

                def finish_second(t, s):
                    wait(dve, summed, t - 1)
                    second.finish(dve, msg[s % 2][:, :], t, s)

                over_tiles(dve, NET, 4, (5, lambda t, s: first.product(dve, t, s)),
                           (9, lambda t, s: second.product(dve, t, s)), (6, finish_first), (10, finish_second),
                           (4, first_z), (8, second_z), (6, rest_of_h))

            @block.scalar
            def _(act):
                def copy_turned(t, s):
                    wait(act, turned, t + 1)
                    wait(act, m_product, t - 1)
                    copy_blocks(nc, hT.hi[s % 2][:, :, :], p_turn[s % 2]).then_inc(hT.hi_made, 1)

                def evacuate(t, s):
                    wait(act, summed, t + 1)
                    wait(act, stored[s % 2], landed(t, s % 2, 2) - 16)
                    nc.scalar.activation(res[s % 2][:, :], p_sum[s % 2][:, :], ACT.Identity, scale=-2.0)\
                        .then_inc(evacuated, 1)

                def copy_attr(t, s):
                    wait(act, at_turned, t + 1)
                    wait(act, z_product, t - 1)
                    nc.scalar.copy(at[s % 2][:, :], p_z[s % 2][0:DE, 0:P]).then_inc(at_made, 1)

                def spread_same(t, s):
                    wait(act, summed, t - 1)
                    nc.scalar.copy(same[s % 2][:, :], c["same"][:, bass.ds(t, 1), :].rearrange("p o m -> p (o m)"))\
                        .then_inc(same_made, 1)

                over_tiles(act, NET, 4, (3, copy_attr),
                           (5, lambda t, s: first.log(act, t, s)), (9, lambda t, s: second.log(act, t, s)),
                           (5, lambda t, s: first.inverse(act, t, s)), (9, lambda t, s: second.inverse(act, t, s)),
                           (9, spread_same), (6, copy_turned), (12, evacuate),
                           (4, lambda t, s: first.exp(act, t, s)), (8, lambda t, s: second.exp(act, t, s)))

            @block.tensor
            def _(pe):
                pe.wait_ge(weights, 48)
                pe.wait_ge(w2_halves.made, KC)

                def turn_attr(t, s):
                    wait(pe, at_in[s], landed(t, s, 4))
                    wait(pe, first.z_made, t - 1)
                    nc.tensor.matmul(p_z[s % 2][0:DE, 0:P], at_rows[s][:, :], c["ident"][:, :],
                                     start=True, stop=True).then_inc(at_turned, 1)

                def attr_product(t, s):
                    wait(pe, at_made, t + 1)
                    nc.tensor.matmul(p_z[s % 2][:, :], at[s % 2][:, :], w1[:, :], start=True, stop=True)\
                        .then_inc(z_product, 1)

                def turn(t, s):
                    wait(pe, first.made, t + 1)
                    wait(pe, hT.made, t - 1)
                    for k in range(KC):
                        ins = nc.tensor.transpose(p_turn[s % 2][:, k * P:(k + 1) * P], h[s % 2][:, k * P:(k + 1) * P],
                                                  c["ident"][:, :])
                    ins.then_inc(turned, 1)

                def multiply(t, s):
                    wait(pe, hT.made, t + 1)
                    wait(pe, second.z_made, t - 1)
                    multiply_halves(nc, p_m[s % 2][:, :], hT, s % 2, range(KC), w2_halves, range(KC))\
                        .then_inc(m_product, 1)

                def add_up(t, s):
                    wait(pe, same_made, t + 1)
                    wait(pe, second.made, t + 1)
                    wait(pe, evacuated, t - 1)
                    nc.tensor.matmul(p_sum[s % 2][:, :], same[s % 2][:, :], msg[s % 2][:, :], start=True, stop=True)\
                        .then_inc(summed, 1)

                over_tiles(pe, NET, 4, (3, turn_attr), (11, add_up), (3, attr_product), (6, turn), (7, multiply))
    join_tiles(nc, c, "messages_join", sums)


def segment_sums(nc, c, name, table, sums, weights=None):
    with Stage(nc, name) as st:
        U = 4
        idx = st.slots(st.sb, "idx", U, [P, 1], I32)
        msg = st.slots(st.sb, "msg", U, [P, D])
        same = st.slots(st.sb, "same", U, [P, P])
        res = st.slots(st.sb, "res", U, [P, D])
        p_sum = st.slots(st.ps, "p_sum", U)
        zeros = st.sb("zeros", [1, D])
        staged, same_made, summed = st.sem("staged"), st.sem("same_made"), st.sem("summed")
        evacuated, weighted, zeroed, zero_row = (st.sem(n) for n in ("evacuated", "weighted", "zeroed", "zero_row"))
        gathered, stored = st.slots(st.dma_sem, "gathered", U), st.slots(st.sem, "stored", U)
        if weights is not None:
            msg_in = st.slots(st.sb, "msg_in", U, [P, D])

        with nc.Block() as block:
            @block.gpsimd
            def _(pool):
                dest = msg if weights is None else msg_in
                nc.gpsimd.memset(zeros[:, :], 0.0).then_inc(zeroed, 1)

                def gather(t, s):
                    nc.gpsimd.indirect_dma_start(out=dest[s][:, :], in_=table[:, :], out_offset=None,
                                                 in_offset=bass.IndirectOffsetOnAxis(ap=idx[s][:, 0:1], axis=0))\
                        .then_inc(gathered[s], 16)

                def stage_and_gather(t, s):
                    wait(pool, staged, t)
                    wait(pool, summed if weights is None else weighted, t - U)
                    wait(pool, gathered[s], landed(t, s, U) - 16)
                    nc.gpsimd.tensor_copy(idx[s][:, :], c["src_list"][:, bass.ds(t, 1)]).then_inc(staged, 1)
                    if not isinstance(t, int) or t > 0:
                        gather(t - 1, (s - 1) % U)

                over_tiles(pool, NET, U, (0, stage_and_gather))
                pool.wait_ge(staged, NET)
                wait(pool, summed if weights is None else weighted, NET - U)
                gather(NET - 1, (NET - 1) % U)

            @block.scalar
            def _(act):
                def spread_same(t, s):
                    wait(act, summed, t - U + 1)
                    nc.scalar.copy(same[s][:, :], c["same"][:, bass.ds(t, 1), :].rearrange("p o m -> p (o m)"))\
                        .then_inc(same_made, 1)

                over_tiles(act, NET, U, (0, spread_same))

            @block.vector
            def _(dve):
                def evacuate(t, s):
                    wait(dve, summed, t + 1)
                    wait(dve, stored[s], landed(t, s, U) - 16)
                    nc.vector.tensor_copy(res[s][:, :], p_sum[s][:, :]).then_inc(evacuated, 1)

                def weigh(t, s):
                    wait(dve, gathered[s], landed(t, s, U))
                    wait(dve, summed, t - U + 1)
                    nc.vector.tensor_tensor(msg[s][:, :].rearrange("p (h d) -> p h d", h=HEADS),
                                            msg_in[s][:, :].rearrange("p (h d) -> p h d", h=HEADS),
                                            weights[:, bass.ds(t, 1), :].rearrange("p o h -> p (o h)")
                                            .unsqueeze(2).to_broadcast([P, HEADS, DH]),
                                            ALU.mult).then_inc(weighted, 1)

                if weights is None:
                    over_tiles(dve, NET, U, (0, evacuate))
                else:
                    over_tiles(dve, NET, U, (0, weigh), (1, evacuate))

            @block.tensor
            def _(pe):
                def add_up(t, s):
                    wait(pe, same_made, t + 1)
                    if weights is None:
                        wait(pe, gathered[s], landed(t, s, U))
                    else:
                        wait(pe, weighted, t + 1)
                    wait(pe, evacuated, t - U + 1)
                    nc.tensor.matmul(p_sum[s][:, :], same[s][:, :], msg[s][:, :], start=True, stop=True)\
                        .then_inc(summed, 1)

                over_tiles(pe, NET, U, (0, add_up))

            @block.sync
            def _(sp):
                sp.wait_ge(zeroed, 1)
                sp.dma_start(sums[ZROW:ZROW + 1, :], zeros[:, :]).then_inc(zero_row, 16)
                sp.wait_ge(zero_row, 16)

                def store(t, s):
                    wait(sp, evacuated, t + 1)
                    sp.dma_start(rows(sums, t), res[s][:, :]).then_inc(stored[s], 16)

                over_tiles(sp, NET, U, (0, store))
                for s in range(U):
                    sp.wait_ge(stored[s], 16 * len(range(s, NET, U)))
    join_tiles(nc, c, name + "_join", sums)


def join_tiles(nc, c, name, sums):
    with Stage(nc, name) as st:
        tails, joined = st.sb("tails", [NET, D]), st.sb("joined", [NET, D])
        p_add = st.ps("p_add")
        tails_in, summed, added = st.sem("tails_in"), st.sem("summed"), st.sem("added")
        gathered, scattered = st.dma_sem("gathered"), st.dma_sem("scattered")
        where = c["join_row_i"][:, 0:1]

        with nc.Block() as block:
            @block.sync
            def _(sp):
                sp.dma_start(tails[:, :], bass.AP(tensor=sums.tensor, offset=sums.offset + (P - 1) * D,
                                                  ap=[[P * D, NET], [1, D]])).then_inc(tails_in, 16)

            @block.gpsimd
            def _(pool):
                nc.gpsimd.indirect_dma_start(out=joined[:, :], in_=sums[:, :], out_offset=None,
                                             in_offset=bass.IndirectOffsetOnAxis(ap=where, axis=0))\
                    .then_inc(gathered, 16)
                pool.wait_ge(added, 1)
                nc.gpsimd.indirect_dma_start(out=sums[:, :], in_=joined[:, :], in_offset=None,
                                             out_offset=bass.IndirectOffsetOnAxis(ap=where, axis=0))\
                    .then_inc(scattered, 16)
                pool.wait_ge(scattered, 16)

            @block.tensor
            def _(pe):
                pe.wait_ge(tails_in, 16)
                nc.tensor.matmul(p_add[0:NET, :], c["join"][:, :], tails[:, :], start=True, stop=True)\
                    .then_inc(summed, 1)

            @block.vector
            def _(dve):
                dve.wait_ge(gathered, 16)
                dve.wait_ge(summed, 1)
                nc.vector.tensor_tensor(joined[:, :], joined[:, :], p_add[0:NET, :], ALU.add).then_inc(added, 1)


class LayerNorm:

    def __init__(self, nc, st, c, name, slots=2):
        self.nc, self.n, self.eps = nc, slots, c["eps"]
        self.spare = st.sb(name + "_spare", [P, 1])
        self.stats = st.slots(st.sb, name + "_stats", slots, [P, 6])
        self.moments = st.slots(st.sb, name + "_moments", slots, [P, 2])
        self.inv = st.slots(st.sb, name + "_inv", slots, [P, 1])
        self.stats_made, self.moments_made, self.log_made = (st.sem(f"{name}_{n}") for n in
                                                             ("stats_made", "moments_made", "log_made"))
        self.inv_made, self.made = st.sem(name + "_inv_made"), st.sem(name + "_made")

    def sums(self, dve, v, t, s):
        self.nc.vector.bn_stats(self.stats[s][:, :], v).then_inc(self.stats_made, 1)
        wait(dve, self.stats_made, t + 1)
        self.nc.vector.memset(self.spare[:, :], 0.0)
        self.nc.vector.bn_aggr(self.moments[s][:, :], self.stats[s][:, :]).then_inc(self.moments_made, 1)

    def root(self, act, t, s):
        wait(act, self.moments_made, t + 1)
        wait(act, self.made, t - self.n + 1)
        self.nc.scalar.activation(self.inv[s][:, :], self.moments[s][:, 1:2], ACT.Ln, bias=self.eps[:, 0:1])\
            .then_inc(self.log_made, 1)
        wait(act, self.log_made, t + 1)
        self.nc.scalar.activation(self.inv[s][:, :], self.inv[s][:, :], ACT.Exp, scale=-0.5).then_inc(self.inv_made, 1)

    def scale(self, dve, out, v, t, s):
        wait(dve, self.inv_made, t + 1)
        self.nc.vector.tensor_scalar(out, v, self.moments[s][:, 0:1], self.inv[s][:, 0:1],
                                     ALU.subtract, ALU.mult).then_inc(self.made, 1)


class NodeGather:

    def __init__(self, nc, st, c, sums, used, name="agg"):
        self.nc, self.c, self.sums, self.used = nc, c, sums, used
        self.idx = st.slots(st.sb, name + "_idx", 4, [P, 1], I32)
        self.rows = st.slots(st.sb, name, 4, [P, D])
        self.staged = st.sem(name + "_staged")
        self.landed = st.slots(st.dma_sem, name + "_landed", 4)

    def _gather(self, t, s):
        self.nc.gpsimd.indirect_dma_start(out=self.rows[s][:, :], in_=self.sums[:, :], out_offset=None,
                                          in_offset=bass.IndirectOffsetOnAxis(ap=self.idx[s][:, 0:1], axis=0))\
            .then_inc(self.landed[s], 16)

    def stage_and_gather(self, pool, t, s):
        wait(pool, self.staged, t)
        wait(pool, self.used, t - 4)
        wait(pool, self.landed[s], landed(t, s, 4) - 16)
        self.nc.gpsimd.tensor_copy(self.idx[s][:, :], self.c["sum_row_i"][:, bass.ds(t, 1)]).then_inc(self.staged, 1)
        if not isinstance(t, int) or t > 0:
            self._gather(t - 1, (s - 1) % 4)
        if isinstance(t, int) and t == NT - 1:
            pool.wait_ge(self.staged, NT)
            pool.wait_ge(self.used, NT - 4)
            self._gather(t, s)


def column_stats(nc, c, stats, p_turn, t):
    count = LAST if isinstance(t, int) and t == NT - 1 else P
    for k in range(KC):
        ins = nc.vector.bn_stats(stats[:, k, bass.ds(t, 1), :].rearrange("p o f -> p (o f)"),
                                 p_turn[:, k * P:k * P + count])
    return ins


def update_nodes(nc, c, x, from_x, sums, W3, W4, b4, gamma, beta, x1, stats):
    with Stage(nc, "update") as st:
        w3, w4 = st.sb("w3", [P, KC, D]), st.sb("w4", [P, KC, D])
        vecs = {n: st.sb(n, [P, D]) for n in ("b4", "gamma", "beta")}
        fx, xt = st.slots(st.sb, "fx", 4, [P, D]), st.slots(st.sb, "xt", 4, [P, D])
        xb = st.slots(st.sb, "xb", 4, [P, D])
        aT = Halves(st, "aT", [P, KC, P])
        w3_halves, fill_w3 = split_weights(nc, st, "w3", w3)
        w4_halves, fill_w4 = split_weights(nc, st, "w4", w4)
        mish = Mish(nc, st, "mish", 4)
        mish.two = c["two"]
        u, uT = st.slots(st.sb, "u", 2, [P, D]), Halves(st, "uT", [P, KC, P])
        y, y_norm = st.slots(st.sb, "y", 2, [P, D]), st.slots(st.sb, "y_norm", 4, [P, D])
        res = st.slots(st.sb, "res", 2, [P, D])
        p_agg, p_uT, p_res = (st.ps(n) for n in ("p_agg", "p_uT", "p_res"))
        p_u, p_out = st.slots(st.ps, "p_u", 2), st.slots(st.ps, "p_out", 2)
        weights, zeroed = st.sem("weights"), st.sem("zeroed")
        fx_in, x_in, biased = st.slots(st.sem, "fx_in", 4), st.slots(st.sem, "x_in", 4), st.sem("biased")
        stored = st.slots(st.sem, "stored", 2)
        turned, u_product, u_turned, out_product = (
            st.sem(n) for n in ("turned", "u_product", "u_turned", "out_product"))
        y_step, scaled, shifted, summed = (st.sem(n) for n in ("y_step", "scaled", "shifted", "summed"))
        res_turned, counted = st.sem("res_turned"), st.sem("counted")
        agg = NodeGather(nc, st, c, sums, turned)
        norm_y, norm_x = LayerNorm(nc, st, c, "norm_y"), LayerNorm(nc, st, c, "norm_x")

        with nc.Block() as block:
            @block.sync
            def _(sp):
                load_weights(sp, weights, [(w3[:, :, :], W3[D:2 * D, :]), (w4[:, :, :], W4)])
                for n, v in (("b4", b4), ("gamma", gamma), ("beta", beta)):
                    sp.dma_start(vecs[n][:, :], row_of_all(v)).then_inc(weights, 16)
                sp.wait_ge(zeroed, 4)

                def load(t, s):
                    wait(sp, mish.z_made, t - 3)
                    sp.dma_start(fx[s][:, :], rows(from_x, t)).then_inc(fx_in[s], 16)

                def load_x(t, s):
                    wait(sp, summed, t - 3)
                    if isinstance(t, int) and t == NT - 1:
                        sp.dma_start(xt[s][0:LAST, :], x[t * P:N, :]).then_inc(x_in[s], 16)
                    else:
                        sp.dma_start(xt[s][:, :], rows(x, t)).then_inc(x_in[s], 16)

                def store(t, s):
                    wait(sp, norm_x.made, t + 1)
                    sp.dma_start(rows(x1, t), res[s % 2][:, :]).then_inc(stored[s % 2], 16)

                over_tiles(sp, NT, 4, (1, load), (6, load_x), (12, store))
                for s in range(2):
                    sp.wait_ge(stored[s], 16 * len(range(s, NT, 2)))

            @block.gpsimd
            def _(pool):
                for v in xt:
                    nc.gpsimd.memset(v[:, :], 0.0).then_inc(zeroed, 1)
                pool.wait_ge(weights, 80)

                def add_bias(t, s):
                    wait(pool, x_in[s], landed(t, s, 4))
                    wait(pool, norm_y.stats_made, t - 3)
                    nc.gpsimd.tensor_tensor(xb[s][:, :], xt[s][:, :], vecs["b4"][:, :], ALU.add).then_inc(biased, 1)

                def scale_and_shift(t, s):
                    wait(pool, norm_y.made, t + 1)
                    nc.gpsimd.tensor_tensor(y_norm[s][:, :], y_norm[s][:, :], vecs["gamma"][:, :], ALU.mult)\
                        .then_inc(scaled, 1)
                    wait(pool, scaled, t + 1)
                    nc.gpsimd.tensor_tensor(y_norm[s][:, :], y_norm[s][:, :], vecs["beta"][:, :], ALU.add)\
                        .then_inc(shifted, 1)
                    wait(pool, shifted, t + 1)
                    nc.gpsimd.tensor_tensor(y_norm[s][:, :], y_norm[s][:, :], xt[s][:, :], ALU.add)\
                        .then_inc(summed, 1)

                over_tiles(pool, NT, 4, (0, lambda t, s: agg.stage_and_gather(pool, t, s)), (8, add_bias),
                           (10, scale_and_shift))

            @block.vector
            def _(dve):
                dve.wait_ge(weights, 80)
                fill_w3(dve)
                fill_w4(dve)

                def rest_of_agg(t, s):
                    wait(dve, aT.hi_made, t + 1)
                    wait(dve, u_product, t - 1)
                    rest_of_blocks(nc, aT.lo[s % 2][:, :, :], p_agg, aT.hi[s % 2][:, :, :]).then_inc(aT.made, 1)

                def rest_of_u(t, s):
                    wait(dve, uT.hi_made, t + 1)
                    wait(dve, out_product, t - 1)
                    rest_of_blocks(nc, uT.lo[s % 2][:, :, :], p_uT, uT.hi[s % 2][:, :, :]).then_inc(uT.made, 1)

                def make_z(t, s):
                    wait(dve, u_product, t + 1)
                    wait(dve, mish.made, t - 3)
                    wait(dve, fx_in[s], landed(t, s, 4))
                    nc.vector.tensor_tensor(mish.z[s][:, :], p_u[s % 2][:, :], fx[s][:, :], ALU.add)\
                        .then_inc(mish.z_made, 1)

                def make_y(t, s):
                    wait(dve, out_product, t + 1)
                    wait(dve, biased, t + 1)
                    nc.vector.scalar_tensor_tensor(y[s % 2][:, :], p_out[s % 2][:, :], -2.0, xb[s][:, :],
                                                   ALU.mult, ALU.add).then_inc(y_step, 1)
                    wait(dve, y_step, t + 1)
                    norm_y.sums(dve, y[s % 2][:, :], t, s % 2)

                def scale_y(t, s):
                    wait(dve, summed, t - 3)
                    norm_y.scale(dve, y_norm[s][:, :], y[s % 2][:, :], t, s % 2)

                def norm_sums(t, s):
                    wait(dve, summed, t + 1)
                    norm_x.sums(dve, y_norm[s][:, :], t, s % 2)

                def scale_x(t, s):
                    wait(dve, res_turned, t - 1)
                    wait(dve, stored[s % 2], landed(t, s % 2, 2) - 16)
                    norm_x.scale(dve, res[s % 2][:, :], y_norm[s][:, :], t, s % 2)

                def count(t, s):
                    wait(dve, res_turned, t + 1)
                    column_stats(nc, c, stats, p_res, t).then_inc(counted, 1)

                def finish(t, s):
                    wait(dve, u_turned, t - 1)
                    mish.finish(dve, u[s % 2][:, :], t, s)

                over_tiles(dve, NT, 4, (6, lambda t, s: mish.product(dve, t, s)), (10, scale_y), (13, count),
                           (7, finish), (3, rest_of_agg), (12, scale_x), (5, make_z), (9, make_y), (11, norm_sums),
                           (7, rest_of_u))

            @block.scalar
            def _(act):
                def copy_turned(t, s):
                    wait(act, turned, t + 1)
                    wait(act, u_product, t - 1)
                    copy_blocks(nc, aT.hi[s % 2][:, :, :], p_agg).then_inc(aT.hi_made, 1)

                def copy_u(t, s):
                    wait(act, u_turned, t + 1)
                    wait(act, out_product, t - 1)
                    copy_blocks(nc, uT.hi[s % 2][:, :, :], p_uT).then_inc(uT.hi_made, 1)

                over_tiles(act, NT, 4, (3, copy_turned), (6, lambda t, s: mish.log(act, t, s)),
                           (6, lambda t, s: mish.inverse(act, t, s)), (7, copy_u),
                           (5, lambda t, s: mish.exp(act, t, s)), (9, lambda t, s: norm_y.root(act, t, s % 2)),
                           (11, lambda t, s: norm_x.root(act, t, s % 2)))

            @block.tensor
            def _(pe):
                pe.wait_ge(w3_halves.made, KC)
                pe.wait_ge(w4_halves.made, KC)

                def turn(t, s):
                    wait(pe, agg.landed[s], landed(t, s, 4))
                    wait(pe, aT.made, t)
                    turn_blocks(nc, c, p_agg, agg.rows[s]).then_inc(turned, 1)

                def multiply_in(t, s):
                    wait(pe, aT.made, t + 1)
                    wait(pe, mish.z_made, t - 1)
                    multiply_halves(nc, p_u[s % 2][:, :], aT, s % 2, range(KC), w3_halves, range(KC))\
                        .then_inc(u_product, 1)

                def turn_u(t, s):
                    wait(pe, mish.made, t + 1)
                    wait(pe, uT.made, t)
                    turn_blocks(nc, c, p_uT, u[s % 2]).then_inc(u_turned, 1)

                def multiply_out(t, s):
                    wait(pe, uT.made, t + 1)
                    wait(pe, y_step, t - 1)
                    multiply_halves(nc, p_out[s % 2][:, :], uT, s % 2, range(KC), w4_halves, range(KC))\
                        .then_inc(out_product, 1)

                def turn_res(t, s):
                    wait(pe, norm_x.made, t + 1)
                    wait(pe, counted, t)
                    turn_blocks(nc, c, p_res, res[s % 2]).then_inc(res_turned, 1)

                over_tiles(pe, NT, 4, (3, turn), (4, multiply_in), (7, turn_u), (8, multiply_out), (12, turn_res))


TOKENS = 64
M = 256
KEPS = 1e-6


def attention(nc, c, x1, Wq, Wk, Wv, Wo, proj, first_rows, other_rows):
    T, CH = TOKENS, M // P
    with Stage(nc, "attention") as st:
        w = [st.sb(f"w{n}", [P, KC, D]) for n in range(4)]
        pr = st.sb("pr", [P, CH, DH])
        xt = st.sb("xt", [T, D])
        xT, oT = st.sb("xT", [P, KC, T]), st.sb("oT", [P, KC, T])
        prT = st.sb("prT", [DH, M])
        qk = st.sb("qk", [T, 2, D])
        v1 = st.sb("v1", [T, HEADS, DH + 1])
        sq = st.sb("sq", [T, D])
        qkT = st.sb("qkT", [DH, 2, HEADS, T])
        half = st.sb("half", [T, 2, HEADS])
        top = st.sb("top", [T, 2, HEADS])
        bias = st.sb("bias", [T, 2, HEADS])
        topT, top_all = st.sb("topT", [HEADS, 1]), st.sb("top_all", [HEADS, HEADS])
        feat = st.sb("feat", [T, 2, HEADS, M])
        qfT = st.sb("qfT", [P, CH, HEADS, T])
        kv = st.sb("kv", [P, CH, HEADS, DH + 1])
        zr, zi = st.sb("zr", [T, HEADS]), st.sb("zi", [T, HEADS])
        o = st.sb("o", [T, D])
        out = st.sb("out", [T, D])
        pick = st.sb("pick", [T, P])
        bank = [st.ps(f"bank{i}") for i in range(8)]
        loaded, proj_in = st.sem("loaded"), st.sem("proj_in")
        names = ("x_turned", "xT_made", "projected", "qkv_made", "squared", "halved", "turned", "qkT_made", "u_made",
                 "top_made", "top_turned", "topT_made", "top_spread", "bias_made", "exp_made", "features", "qf_turned",
                 "qfT_made", "kv_made", "kv_copied", "num_made", "z_step", "o_made", "o_turned", "oT_made",
                 "out_made", "out_copied", "picked", "spread")
        s = {n: st.sem(n) for n in names}
        HB = HEADS // 2

        with nc.Block() as block:
            @block.sync
            def _(sp):
                sp.dma_start(xt[:, :], x1[0:T, :]).then_inc(loaded, 16)
                load_weights(sp, loaded, [(w[n][:, :, :], m) for n, m in enumerate((Wq, Wk, Wv, Wo))])
                sp.dma_start(pr[:, :, :], proj.rearrange("(c p) d -> p c d", p=P)).then_inc(loaded, 16)

            @block.tensor
            def _(pe):
                pe.wait_ge(loaded, 96)
                for k in range(KC):
                    nc.tensor.transpose(bank[0][:, k * T:(k + 1) * T], xt[:, k * P:(k + 1) * P], c["ident"][0:T, 0:T])
                for h in range(CH):
                    ins = nc.tensor.transpose(bank[0][0:DH, 256 + h * P:256 + (h + 1) * P], pr[:, h, :],
                                              c["ident"][:, :])
                ins.then_inc(s["x_turned"], 1)
                pe.wait_ge(s["xT_made"], 2)
                for n in range(3):
                    for k in range(KC):
                        ins = nc.tensor.matmul(bank[1 + n][0:T, :], xT[:, k, :], w[n][:, k, :],
                                               start=k == 0, stop=k == KC - 1)
                ins.then_inc(s["projected"], 1)
                pe.wait_ge(s["qkv_made"], 3)
                for n in range(2):
                    for h in range(HEADS):
                        ins = nc.tensor.transpose(bank[4 + n][0:DH, h * T:(h + 1) * T], qk[:, n, h * DH:(h + 1) * DH],
                                                  c["ident"][0:T, 0:T])
                ins.then_inc(s["turned"], 1)
                for n in range(2):
                    pe.wait_ge(s["qkT_made"], 2)
                    for h in range(HEADS):
                        if n == 1 and h == 0:
                            pe.wait_ge(s["exp_made"], HEADS)
                        b = bank[h // 2 + 4 * (n == 1)] if n == 0 else bank[h // 2]
                        ins = nc.tensor.matmul(b[0:T, (h % 2) * M:(h % 2 + 1) * M], qkT[:, n, h, :], prT[:, :],
                                               start=True, stop=True)
                    ins.then_inc(s["u_made"], 1)
                pe.wait_ge(s["top_made"], 2)
                nc.tensor.transpose(bank[4][0:HEADS, 0:T], top[:, 1, :], c["ident"][0:T, 0:T]).then_inc(s["top_turned"], 1)
                pe.wait_ge(s["topT_made"], 2)
                nc.tensor.matmul(bank[4][0:T, 0:HEADS], c["ones"][0:HEADS, 0:T], top_all[:, :],
                                 start=True, stop=True).then_inc(s["top_spread"], 1)
                pe.wait_ge(s["features"], 1)
                for ch in range(CH):
                    for h in range(HEADS):
                        ins = nc.tensor.transpose(bank[5 + ch][:, h * T:(h + 1) * T],
                                                  feat[:, 0, h, ch * P:(ch + 1) * P], c["ident"][0:T, 0:T])
                ins.then_inc(s["qf_turned"], 1)
                pe.wait_ge(s["features"], 2)
                for ch in range(CH):
                    for h in range(HEADS):
                        j = (h % HB) * (DH + 1)
                        ins = nc.tensor.matmul(bank[2 * ch + h // HB][:, j:j + DH + 1],
                                               feat[:, 1, h, ch * P:(ch + 1) * P], v1[:, h, :], start=True, stop=True)
                ins.then_inc(s["kv_made"], 1)
                pe.wait_ge(s["kv_copied"], 2)
                pe.wait_ge(s["qfT_made"], 1)
                for h in range(HEADS):
                    j = (h % HB) * (DH + 1)
                    for ch in range(CH):
                        ins = nc.tensor.matmul(bank[5 + h // HB][0:T, j:j + DH + 1], qfT[:, ch, h, :], kv[:, ch, h, :],
                                               start=ch == 0, stop=ch == CH - 1)
                ins.then_inc(s["num_made"], 1)
                pe.wait_ge(s["o_made"], 2)
                for k in range(KC):
                    ins = nc.tensor.transpose(bank[7][:, k * T:(k + 1) * T], o[:, k * P:(k + 1) * P], c["ident"][0:T, 0:T])
                ins.then_inc(s["o_turned"], 1)
                pe.wait_ge(s["oT_made"], 1)
                for k in range(KC):
                    ins = nc.tensor.matmul(bank[0][0:T, :], oT[:, k, :], w[3][:, k, :], start=k == 0, stop=k == KC - 1)
                ins.then_inc(s["out_made"], 1)
                pe.wait_ge(s["out_copied"], 1)
                pe.wait_ge(s["picked"], 1)
                nc.tensor.matmul(bank[1][:, :], pick[:, :], out[:, :], start=True, stop=True).then_inc(s["spread"], 1)

            @block.vector
            def _(dve):
                dve.wait_ge(s["x_turned"], 1)
                nc.vector.tensor_copy(xT[:, :, :], bank[0][:, 0:KC * T].rearrange("p (k m) -> p k m", k=KC))\
                    .then_inc(s["xT_made"], 1)
                nc.vector.tensor_copy(prT[:, :], bank[0][0:DH, 256:256 + M]).then_inc(s["xT_made"], 1)
                nc.vector.tensor_copy(v1[:, :, DH:DH + 1], c["ones"][0:T, 0:HEADS].unsqueeze(2)).then_inc(s["qkv_made"], 1)
                nc.vector.tensor_copy(pick[:, :], c["ident"][0:T, T - 1:T].to_broadcast([T, P])).then_inc(s["picked"], 1)
                dve.wait_ge(s["projected"], 1)
                for n in range(2):
                    ins = nc.vector.tensor_scalar(qk[:, n, :], bank[1 + n][0:T, :], float(DH) ** -0.25, None, ALU.mult)
                ins.then_inc(s["qkv_made"], 1)
                nc.vector.tensor_copy(v1[:, :, 0:DH], bank[3][0:T, :].rearrange("p (h d) -> p h d", h=HEADS))\
                    .then_inc(s["qkv_made"], 1)
                dve.wait_ge(s["qkv_made"], 3)
                for n in range(2):
                    nc.vector.tensor_tensor(sq[:, :], qk[:, n, :], qk[:, n, :], ALU.mult).then_inc(s["squared"], 1)
                    dve.wait_ge(s["squared"], n + 1)
                    nc.vector.tensor_reduce(half[:, n, :], sq[:, :].rearrange("p (h d) -> p h d", h=HEADS),
                                            mybir.AxisListType.X, ALU.add).then_inc(s["halved"], 1)
                    dve.wait_ge(s["halved"], 2 * n + 1)
                    nc.vector.tensor_scalar(half[:, n, :], half[:, n, :], 0.5, None, ALU.mult).then_inc(s["halved"], 1)
                dve.wait_ge(s["turned"], 1)
                for n in range(2):
                    nc.vector.tensor_copy(qkT[:, n, :, :], bank[4 + n][0:DH, :].rearrange("p (h m) -> p h m", h=HEADS))\
                        .then_inc(s["qkT_made"], 1)
                dve.wait_ge(s["u_made"], 1)
                for b in range(HB):
                    ins = nc.vector.tensor_reduce(top[:, 0, 2 * b:2 * b + 2],
                                                  bank[b][0:T, :].rearrange("p (h m) -> p h m", h=2),
                                                  mybir.AxisListType.X, ALU.max)
                ins.then_inc(s["top_made"], 1)
                dve.wait_ge(s["top_made"], 1)
                dve.wait_ge(s["halved"], 4)
                nc.vector.scalar_tensor_tensor(bias[:, 0, :], top[:, 0, :], -1.0, half[:, 0, :],
                                               ALU.mult, ALU.subtract).then_inc(s["bias_made"], 1)
                dve.wait_ge(s["u_made"], 2)
                for b in range(HB):
                    ins = nc.vector.tensor_reduce(top[:, 1, 2 * b:2 * b + 2],
                                                  bank[b][0:T, :].rearrange("p (h m) -> p h m", h=2),
                                                  mybir.AxisListType.X, ALU.max)
                ins.then_inc(s["top_made"], 1)
                dve.wait_ge(s["top_turned"], 1)
                nc.vector.tensor_reduce(topT[:, :], bank[4][0:HEADS, 0:T], mybir.AxisListType.X, ALU.max)\
                    .then_inc(s["topT_made"], 1)
                dve.wait_ge(s["topT_made"], 1)
                nc.vector.tensor_scalar(top_all[:, :], c["ident"][0:HEADS, 0:HEADS], topT[:, 0:1], None, ALU.mult)\
                    .then_inc(s["topT_made"], 1)
                dve.wait_ge(s["top_spread"], 1)
                nc.vector.scalar_tensor_tensor(bias[:, 1, :], bank[4][0:T, 0:HEADS], -1.0, half[:, 1, :],
                                               ALU.mult, ALU.subtract).then_inc(s["bias_made"], 1)
                for n in range(2):
                    dve.wait_ge(s["exp_made"], HEADS * (n + 1))
                    nc.vector.tensor_scalar(feat[:, n, :, :], feat[:, n, :, :], float(M) ** -0.5, KEPS,
                                            ALU.mult, ALU.add).then_inc(s["features"], 1)
                dve.wait_ge(s["qf_turned"], 1)
                for ch in range(CH):
                    ins = nc.vector.tensor_copy(qfT[:, ch, :, :], bank[5 + ch][:, :].rearrange("p (h m) -> p h m", h=HEADS))
                ins.then_inc(s["qfT_made"], 1)
                dve.wait_ge(s["kv_made"], 1)
                for ch in range(CH):
                    for g in range(2):
                        ins = nc.vector.tensor_copy(kv[:, ch, g * HB:(g + 1) * HB, :],
                                                    bank[2 * ch + g][:, 0:HB * (DH + 1)]
                                                    .rearrange("p (h d) -> p h d", h=HB))
                    ins.then_inc(s["kv_copied"], 1)
                dve.wait_ge(s["num_made"], 1)
                for g in range(2):
                    num = bank[5 + g][0:T, 0:HB * (DH + 1)].rearrange("p (h d) -> p h d", h=HB)
                    ins = nc.vector.tensor_scalar(zr[:, g * HB:(g + 1) * HB].unsqueeze(2), num[:, :, DH:DH + 1], KEPS, None,
                                                  ALU.add)
                ins.then_inc(s["z_step"], 1)
                dve.wait_ge(s["z_step"], 1)
                nc.vector.reciprocal(zi[:, :], zr[:, :]).then_inc(s["z_step"], 1)
                dve.wait_ge(s["z_step"], 2)
                for g in range(2):
                    num = bank[5 + g][0:T, 0:HB * (DH + 1)].rearrange("p (h d) -> p h d", h=HB)
                    nc.vector.tensor_tensor(o[:, g * HB * DH:(g + 1) * HB * DH].rearrange("p (h d) -> p h d", h=HB),
                                            num[:, :, 0:DH],
                                            zi[:, g * HB:(g + 1) * HB].unsqueeze(2).to_broadcast([T, HB, DH]),
                                            ALU.mult).then_inc(s["o_made"], 1)
                dve.wait_ge(s["o_turned"], 1)
                nc.vector.tensor_copy(oT[:, :, :], bank[7][:, 0:KC * T].rearrange("p (k m) -> p k m", k=KC))\
                    .then_inc(s["oT_made"], 1)
                dve.wait_ge(s["out_made"], 1)
                nc.vector.tensor_copy(out[:, :], bank[0][0:T, :]).then_inc(s["out_copied"], 1)
                dve.wait_ge(s["spread"], 1)
                nc.vector.tensor_copy(other_rows, bank[1][:, :])
                nc.vector.tensor_copy(first_rows[T:P, :], bank[1][T:P, :])
                nc.vector.tensor_copy(first_rows[0:T, :], out[:, :])

            @block.scalar
            def _(act):
                for n in range(2):
                    act.wait_ge(s["bias_made"], n + 1)
                    for h in range(HEADS):
                        nc.scalar.activation(feat[:, n, h, :], bank[h // 2][0:T, (h % 2) * M:(h % 2 + 1) * M], ACT.Exp,
                                             bias=bias[:, n, h:h + 1]).then_inc(s["exp_made"], 1)


def conv_nodes(nc, c, x1, sums, W, b, g1, b1, stats1, first_rows, other_rows, y, stats2):
    with Stage(nc, "conv") as st:
        w, wa = st.sb("w", [P, KC, D]), st.sb("wa", [P, KC, D])
        bias, shift_w = st.sb("bias", [P, D]), st.sb("shift_w", [P, D])
        gb = st.sb("gb", [P, 2, KC])
        scale, shift, tmp = st.sb("scale", [P, KC]), st.sb("shift", [P, KC]), st.sb("tmp", [P, KC])
        mom = st.sb("mom", [P, KC, 2])
        shift_all = st.sb("shift_all", [P, KC, P])
        xt = st.slots(st.sb, "xt", 4, [P, D])
        aT = Halves(st, "aT", [P, KC, P])
        wa_halves, fill_wa = split_weights(nc, st, "wa", wa)
        v, yt = st.slots(st.sb, "v", 2, [P, D]), st.slots(st.sb, "yt", 4, [P, D])
        p_agg, p_out, p_y = (st.slots(st.ps, n, 2) for n in ("p_agg", "p_out", "p_y"))
        p_shift = st.ps("p_shift")
        weights, moments, step, shifted_w, params = (st.sem(n) for n in
                                                     ("weights", "moments", "step", "shifted_w", "params"))
        x_in, stored = st.slots(st.sem, "x_in", 4), st.slots(st.sem, "stored", 4)
        turned, product, v_step, summed, y_turned, counted = (
            st.sem(n) for n in ("turned", "product", "v_step", "summed", "y_turned", "counted"))
        wa_made = st.sem("wa_made")
        attended = st.sem("attended")
        agg = NodeGather(nc, st, c, sums, turned)

        with nc.Block() as block:
            @block.sync
            def _(sp):
                load_weights(sp, weights, [(w[:, :, :], W)])
                sp.dma_start(bias[:, :], row_of_all(b)).then_inc(weights, 16)
                sp.dma_start(gb[:, 0, :], g1.rearrange("(k p) -> p k", p=P), allow_slow_non_contiguous=True)\
                    .then_inc(weights, 16)
                sp.dma_start(gb[:, 1, :], b1.rearrange("(k p) -> p k", p=P), allow_slow_non_contiguous=True)\
                    .then_inc(weights, 16)

                def load(t, s):
                    wait(sp, attended, t - 3)
                    sp.dma_start(xt[s][:, :], rows(x1, t)).then_inc(x_in[s], 16)

                def store(t, s):
                    wait(sp, attended, t + 1)
                    sp.dma_start(rows(y, t), yt[s][:, :]).then_inc(stored[s], 16)

                over_tiles(sp, NT, 4, (2, load), (7, store))
                for s in range(4):
                    sp.wait_ge(stored[s], 16 * len(range(s, NT, 4)))

            @block.gpsimd
            def _(pool):
                def attend(t, s):
                    wait(pool, summed, t + 1)
                    wait(pool, y_turned, t - 3)
                    wait(pool, stored[s], landed(t, s, 4) - 16)
                    given = first_rows if isinstance(t, int) and t == 0 else other_rows
                    nc.gpsimd.tensor_tensor(yt[s][:, :], v[s % 2][:, :], given, ALU.add).then_inc(attended, 1)

                over_tiles(pool, NT, 4, (0, lambda t, s: agg.stage_and_gather(pool, t, s)), (6, attend))

            @block.vector
            def _(dve):
                dve.wait_ge(weights, 64)
                for k in range(KC):
                    nc.vector.bn_aggr(mom[:, k, :], stats1[:, k, :, :].rearrange("p t f -> p (t f)"))\
                        .then_inc(moments, 1)
                dve.wait_ge(step, 2)
                nc.vector.tensor_tensor(scale[:, :], tmp[:, :], gb[:, 0, :], ALU.mult).then_inc(step, 1)
                dve.wait_ge(step, 3)
                nc.vector.tensor_tensor(shift[:, :], mom[:, :, 0], scale[:, :], ALU.mult).then_inc(step, 1)
                dve.wait_ge(step, 4)
                nc.vector.tensor_tensor(shift[:, :], gb[:, 1, :], shift[:, :], ALU.subtract).then_inc(step, 1)
                dve.wait_ge(step, 5)
                for k in range(KC):
                    nc.vector.tensor_scalar(wa[:, k, :], w[:, k, :], scale[:, k:k + 1], None, ALU.mult)\
                        .then_inc(wa_made, 1)
                    ins = nc.vector.tensor_scalar(shift_all[:, k, :], c["ones"][:, :], shift[:, k:k + 1], None, ALU.mult)
                ins.then_inc(params, 1)
                dve.wait_ge(shifted_w, 1)
                nc.vector.tensor_copy(shift_w[:, :], p_shift[:, :]).then_inc(params, 1)
                dve.wait_ge(params, 2)
                dve.wait_ge(wa_made, KC)
                fill_wa(dve)

                def rest(t, s):
                    wait(dve, aT.hi_made, t + 1)
                    wait(dve, product, t - 1)
                    rest_of_blocks(nc, aT.lo[s % 2][:, :, :], p_agg[s % 2], aT.hi[s % 2][:, :, :]).then_inc(aT.made, 1)

                def average(t, s):
                    wait(dve, product, t + 1)
                    wait(dve, summed, t - 1)
                    wait(dve, attended, t - 1)
                    nc.vector.scalar_tensor_tensor(v[s % 2][:, :], p_out[s % 2][:, :], c["inv_deg"][:, bass.ds(t, 1)],
                                                   bias[:, :], ALU.mult, ALU.add).then_inc(v_step, 1)

                def add_shift(t, s):
                    wait(dve, v_step, 2 * t + 1)
                    nc.vector.scalar_tensor_tensor(v[s % 2][:, :], shift_w[:, :], c["has_edges"][:, bass.ds(t, 1)],
                                                   v[s % 2][:, :], ALU.mult, ALU.add).then_inc(v_step, 1)

                def activate(t, s):
                    wait(dve, x_in[s], landed(t, s, 4))
                    wait(dve, v_step, 2 * t + 2)
                    nc.vector.scalar_tensor_tensor(v[s % 2][:, :], v[s % 2][:, :], 0.0, xt[s][:, :],
                                                   ALU.max, ALU.add).then_inc(summed, 1)

                def count(t, s):
                    wait(dve, y_turned, t + 1)
                    column_stats(nc, c, stats2, p_y[s % 2], t).then_inc(counted, 1)

                over_tiles(dve, NT, 4, (5, average), (8, count), (5, add_shift), (3, rest), (5, activate))

            @block.scalar
            def _(act):
                act.wait_ge(moments, KC)
                nc.scalar.activation(tmp[:, :], mom[:, :, 1], ACT.Ln, bias=c["eps"][:, 0:1]).then_inc(step, 1)
                act.wait_ge(step, 1)
                nc.scalar.activation(tmp[:, :], tmp[:, :], ACT.Exp, scale=-0.5).then_inc(step, 1)

                def copy_turned(t, s):
                    wait(act, turned, t + 1)
                    wait(act, product, t - 1)
                    copy_blocks(nc, aT.hi[s % 2][:, :, :], p_agg[s % 2]).then_inc(aT.hi_made, 1)

                over_tiles(act, NT, 4, (3, copy_turned))

            @block.tensor
            def _(pe):
                pe.wait_ge(weights, 64)
                pe.wait_ge(params, 1)
                for k in range(KC):
                    ins = nc.tensor.matmul(p_shift[:, :], shift_all[:, k, :], w[:, k, :], start=k == 0, stop=k == KC - 1)
                ins.then_inc(shifted_w, 1)
                pe.wait_ge(wa_halves.made, KC)

                def turn(t, s):
                    wait(pe, agg.landed[s], landed(t, s, 4))
                    wait(pe, aT.made, t - 1)
                    turn_blocks(nc, c, p_agg[s % 2], agg.rows[s]).then_inc(turned, 1)

                def multiply(t, s):
                    wait(pe, aT.made, t + 1)
                    wait(pe, v_step, 2 * t - 3)
                    multiply_halves(nc, p_out[s % 2][:, :], aT, s % 2, range(KC), wa_halves, range(KC))\
                        .then_inc(product, 1)

                def turn_y(t, s):
                    wait(pe, attended, t + 1)
                    wait(pe, counted, t - 1)
                    turn_blocks(nc, c, p_y[s % 2], yt[s]).then_inc(y_turned, 1)

                over_tiles(pe, NT, 4, (3, turn), (4, multiply), (7, turn_y))


def head_products(nc, c, x1, y, g2, b2, stats2, Ws, Wb, a_w, a_b, x2, wx, uv):
    with Stage(nc, "heads") as st:
        w, wa = st.sb("w", [P, KC, D]), st.sb("wa", [P, KC, 2 * HEADS])
        bias, bias_uv = st.sb("bias", [P, D]), st.sb("bias_uv", [P, 2 * HEADS])
        a_src, a_dst = st.sb("a_src", [P, D]), st.sb("a_dst", [P, D])
        ab = st.sb("ab", [P, HEADS])
        prod = st.sb("prod", [P, D])
        gb, mom = st.sb("gb", [P, 2, KC]), st.sb("mom", [P, KC, 2])
        scale, shift, tmp = st.sb("scale", [P, KC]), st.sb("shift", [P, KC]), st.sb("tmp", [P, KC])
        diag = st.sb("diag", [P, 2, KC, P])
        scale_row, shift_row = st.sb("scale_row", [P, D]), st.sb("shift_row", [P, D])
        xt, yt = st.slots(st.sb, "xt", 4, [P, D]), st.slots(st.sb, "yt", 4, [P, D])
        res, xT = st.slots(st.sb, "res", 2, [P, D]), Halves(st, "xT", [P, KC, P])
        w_halves, fill_w = split_weights(nc, st, "w", w)
        wa_both, wa_hi_made, wa_made = st.sb("wa_both", [P, KC, 4 * HEADS], F32R), st.sem("wa_hi_made"), st.sem("wa_made")
        uv_step, uv_sum = st.sem("uv_step"), st.slots(st.sb, "uv_sum", 2, [P, 2 * HEADS])
        out, out_uv = st.slots(st.sb, "out", 2, [P, D]), st.slots(st.sb, "out_uv", 2, [P, 2 * HEADS])
        p_row = st.slots(st.ps, "p_row", 2)
        p_turn, p_out, p_uv = st.slots(st.ps, "p_turn", 2), st.slots(st.ps, "p_out", 2), st.slots(st.ps, "p_uv", 2)
        weights, moments, step, prep, spread = (st.sem(n) for n in ("weights", "moments", "step", "prep", "spread"))
        x_in, y_in = st.slots(st.sem, "x_in", 4), st.slots(st.sem, "y_in", 4)
        stored = [st.slots(st.sem, f"stored{n}_", 2) for n in range(3)]
        scaled, shifted, summed, turned, product, out_made = (
            st.sem(n) for n in ("scaled", "shifted", "summed", "turned", "product", "out_made"))
        norm = LayerNorm(nc, st, c, "norm")

        with nc.Block() as block:
            @block.sync
            def _(sp):
                for h in range(HEADS):
                    sp.dma_start(w[:, :, h * DH:(h + 1) * DH], Ws[h].rearrange("(k p) d -> p k d", p=P))\
                        .then_inc(weights, 16)
                for h in range(HEADS):
                    sp.dma_start(a_dst[:, h * DH:(h + 1) * DH], row_of_all(a_w[h, 0:DH])).then_inc(weights, 16)
                sp.dma_start(bias[:, :], row_of_all(Wb.rearrange("h d -> (h d)"))).then_inc(weights, 16)
                for h in range(0, HEADS, 4):
                    sp.dma_start(a_src[:, h * DH:(h + 4) * DH].rearrange("p (h d) -> p h d", h=4),
                                 bass.AP(tensor=a_w.tensor, offset=a_w.offset + (2 * h + 1) * DH,
                                         ap=[[0, P], [2 * DH, 4], [1, DH]])).then_inc(weights, 16)
                sp.dma_start(ab[:, :], row_of_all(a_b)).then_inc(weights, 16)
                sp.dma_start(gb[:, 0, :], g2.rearrange("(k p) -> p k", p=P), allow_slow_non_contiguous=True)\
                    .then_inc(weights, 16)
                sp.dma_start(gb[:, 1, :], b2.rearrange("(k p) -> p k", p=P), allow_slow_non_contiguous=True)\
                    .then_inc(weights, 16)

                def load(t, s):
                    wait(sp, summed, t - 3)
                    sp.dma_start(xt[s][:, :], rows(x1, t)).then_inc(x_in[s], 16)
                    wait(sp, norm.made, t - 3)
                    sp.dma_start(yt[s][:, :], rows(y, t)).then_inc(y_in[s], 16)

                def store_x(t, s):
                    wait(sp, norm.made, t + 1)
                    sp.dma_start(rows(x2, t), res[s % 2][:, :]).then_inc(stored[0][s % 2], 16)

                def store(t, s):
                    wait(sp, out_made, 2 * t + 2)
                    sp.dma_start(rows(wx, t), out[s % 2][:, :]).then_inc(stored[1][s % 2], 16)
                    sp.dma_start(rows(uv, t), out_uv[s % 2][:, :]).then_inc(stored[2][s % 2], 16)

                over_tiles(sp, NT, 4, (0, load), (4, store_x), (7, store))
                for n in range(3):
                    for s in range(2):
                        sp.wait_ge(stored[n][s], 16 * len(range(s, NT, 2)))

            @block.gpsimd
            def _(pool):
                pool.wait_ge(prep, 4)

                def shift(t, s):
                    wait(pool, x_in[s], landed(t, s, 4))
                    nc.gpsimd.tensor_tensor(xt[s][:, :], xt[s][:, :], shift_row[:, :], ALU.add).then_inc(shifted, 1)

                def add(t, s):
                    wait(pool, scaled, t + 1)
                    wait(pool, shifted, t + 1)
                    nc.gpsimd.tensor_tensor(yt[s][:, :], yt[s][:, :], xt[s][:, :], ALU.add).then_inc(summed, 1)

                over_tiles(pool, NT, 4, (0, shift), (1, add))

            @block.vector
            def _(dve):
                dve.wait_ge(weights, 16 * (2 * HEADS + 6))
                for k in range(KC):
                    nc.vector.bn_aggr(mom[:, k, :], stats2[:, k, :, :].rearrange("p t f -> p (t f)"))\
                        .then_inc(moments, 1)
                dve.wait_ge(step, 2)
                nc.vector.tensor_tensor(scale[:, :], tmp[:, :], gb[:, 0, :], ALU.mult).then_inc(step, 1)
                dve.wait_ge(step, 3)
                nc.vector.tensor_tensor(shift[:, :], mom[:, :, 0], scale[:, :], ALU.mult).then_inc(step, 1)
                dve.wait_ge(step, 4)
                nc.vector.tensor_tensor(shift[:, :], gb[:, 1, :], shift[:, :], ALU.subtract).then_inc(step, 1)
                dve.wait_ge(step, 5)
                for k in range(KC):
                    nc.vector.tensor_scalar(diag[:, 0, k, :], c["ident"][:, :], scale[:, k:k + 1], None, ALU.mult)
                    ins = nc.vector.tensor_scalar(diag[:, 1, k, :], c["ident"][:, :], shift[:, k:k + 1], None, ALU.mult)
                ins.then_inc(prep, 1)
                n = 0
                for k in range(KC + 1):
                    for j, a in enumerate((a_src, a_dst)):
                        source = w[:, k, :] if k < KC else bias[:, :]
                        dest = wa[:, k, j * HEADS:(j + 1) * HEADS] if k < KC else bias_uv[:, j * HEADS:(j + 1) * HEADS]
                        nc.vector.tensor_tensor(prod[:, :], source, a[:, :], ALU.mult).then_inc(step, 1)
                        n += 1
                        dve.wait_ge(step, 5 + n)
                        nc.vector.tensor_reduce(dest, prod[:, :].rearrange("p (h d) -> p h d", h=HEADS),
                                                mybir.AxisListType.X, ALU.add).then_inc(step, 1)
                        n += 1
                        dve.wait_ge(step, 5 + n)
                nc.vector.tensor_tensor(bias_uv[:, HEADS:], bias_uv[:, HEADS:], ab[:, :], ALU.add).then_inc(prep, 1)
                dve.wait_ge(spread, 2)
                nc.vector.tensor_copy(scale_row[:, :], p_row[0][:, :]).then_inc(prep, 1)
                nc.vector.tensor_copy(shift_row[:, :], p_row[1][:, :]).then_inc(prep, 1)
                dve.wait_ge(prep, 4)
                fill_w(dve)
                nc.vector.tensor_copy(wa_both[:, :, 0:2 * HEADS], wa[:, :, :]).then_inc(wa_hi_made, 1)
                dve.wait_ge(wa_hi_made, 1)
                nc.vector.tensor_tensor(wa_both[:, :, 2 * HEADS:], wa[:, :, :], wa_both[:, :, 0:2 * HEADS], ALU.subtract)\
                    .then_inc(wa_made, 1)

                def rest(t, s):
                    wait(dve, xT.hi_made, t + 1)
                    wait(dve, product, t - 1)
                    rest_of_blocks(nc, xT.lo[s % 2][:, :, :], p_turn[s % 2], xT.hi[s % 2][:, :, :]).then_inc(xT.made, 1)

                def scale_y(t, s):
                    wait(dve, y_in[s], landed(t, s, 4))
                    nc.vector.tensor_tensor(yt[s][:, :], yt[s][:, :], scale_row[:, :], ALU.mult).then_inc(scaled, 1)

                def norm_sums(t, s):
                    wait(dve, summed, t + 1)
                    norm.sums(dve, yt[s][:, :], t, s % 2)

                def norm_scale(t, s):
                    wait(dve, turned, t - 1)
                    wait(dve, stored[0][s % 2], landed(t, s % 2, 2) - 16)
                    norm.scale(dve, res[s % 2][:, :], yt[s][:, :], t, s % 2)

                def evacuate(t, s):
                    wait(dve, product, t + 1)
                    nc.vector.tensor_tensor(uv_sum[s % 2][:, :], p_uv[s % 2][:, 0:2 * HEADS], bias_uv[:, :], ALU.add)\
                        .then_inc(uv_step, 1)
                    for n in (1, 2):
                        wait(dve, stored[n][s % 2], landed(t, s % 2, 2) - 16)
                    nc.vector.tensor_tensor(out[s % 2][:, :], p_out[s % 2][:, :], bias[:, :], ALU.add).then_inc(out_made, 1)
                    wait(dve, uv_step, t + 1)
                    nc.vector.tensor_tensor(out_uv[s % 2][:, :], p_uv[s % 2][:, 2 * HEADS:4 * HEADS], uv_sum[s % 2][:, :],
                                            ALU.add).then_inc(out_made, 1)

                over_tiles(dve, NT, 4, (1, norm_sums), (0, scale_y), (2, norm_scale), (5, evacuate), (3, rest))

            @block.scalar
            def _(act):
                act.wait_ge(moments, KC)
                nc.scalar.activation(tmp[:, :], mom[:, :, 1], ACT.Ln, bias=c["eps"][:, 0:1]).then_inc(step, 1)
                act.wait_ge(step, 1)
                nc.scalar.activation(tmp[:, :], tmp[:, :], ACT.Exp, scale=-0.5).then_inc(step, 1)

                def copy_turned(t, s):
                    wait(act, turned, t + 1)
                    wait(act, product, t - 1)
                    copy_blocks(nc, xT.hi[s % 2][:, :, :], p_turn[s % 2]).then_inc(xT.hi_made, 1)

                over_tiles(act, NT, 4, (1, lambda t, s: norm.root(act, t, s % 2)), (3, copy_turned))

            @block.tensor
            def _(pe):
                pe.wait_ge(prep, 1)
                for n in range(2):
                    for k in range(KC):
                        ins = nc.tensor.matmul(p_row[n][:, k * P:(k + 1) * P], c["ones"][:, :], diag[:, n, k, :],
                                               start=True, stop=True)
                    ins.then_inc(spread, 1)
                pe.wait_ge(prep, 4)
                pe.wait_ge(w_halves.made, KC)
                pe.wait_ge(wa_made, 1)

                def turn(t, s):
                    wait(pe, norm.made, t + 1)
                    wait(pe, xT.made, t - 1)
                    turn_blocks(nc, c, p_turn[s % 2], res[s % 2]).then_inc(turned, 1)

                def multiply(t, s):
                    wait(pe, xT.made, t + 1)
                    wait(pe, out_made, 2 * t - 2)
                    multiply_halves(nc, p_out[s % 2][:, :], xT, s % 2, range(KC), w_halves, range(KC))
                    for n, half in enumerate((xT.lo[s % 2], xT.hi[s % 2])):
                        for k in range(KC):
                            ins = nc.tensor.matmul(p_uv[s % 2][:, 0:4 * HEADS], half[:, k, :], wa_both[:, k, :],
                                                   start=n == 0 and k == 0, stop=n == 1 and k == KC - 1)
                    ins.then_inc(product, 1)

                over_tiles(pe, NT, 4, (3, turn), (4, multiply))


def edge_softmax(nc, c, uv, weights):
    with Stage(nc, "scores") as st:
        idx = [st.slots(st.sb, f"idx{n}_", 4, [P, 1], I32) for n in range(2)]
        part = [st.slots(st.sb, f"part{n}_", 4, [P, 2 * HEADS]) for n in range(2)]
        raw = st.slots(st.sb, "raw", 4, [P, HEADS])
        scores = st.sb("scores", [P, GROUPS * GT, HEADS])
        staged, raw_made, scored = st.sem("staged"), st.sem("raw_made"), st.sem("scored")
        gathered = [st.slots(st.dma_sem, f"gathered{n}_", 4) for n in range(2)]
        cleared = st.sem("cleared")

        with nc.Block() as block:
            @block.gpsimd
            def _(pool):
                def gather(t, s):
                    for n in range(2):
                        nc.gpsimd.indirect_dma_start(out=part[n][s][:, :], in_=uv[:, :], out_offset=None,
                                                     in_offset=bass.IndirectOffsetOnAxis(ap=idx[n][s][:, 0:1], axis=0))\
                            .then_inc(gathered[n][s], 16)

                def stage_and_gather(t, s):
                    wait(pool, staged, 2 * t)
                    wait(pool, raw_made, t - 4)
                    for n, lst in enumerate(("src_list", "dst_list")):
                        wait(pool, gathered[n][s], landed(t, s, 4) - 16)
                        nc.gpsimd.tensor_copy(idx[n][s][:, :], c[lst][:, bass.ds(t, 1)]).then_inc(staged, 1)
                    if not isinstance(t, int) or t > 0:
                        gather(t - 1, (s - 1) % 4)

                over_tiles(pool, NET, 4, (0, stage_and_gather))
                pool.wait_ge(staged, 2 * NET)
                pool.wait_ge(raw_made, NET - 4)
                gather(NET - 1, (NET - 1) % 4)

            @block.vector
            def _(dve):
                nc.vector.memset(scores[:, NET:, :], 0.0).then_inc(cleared, 1)

                def score(t, s):
                    for n in range(2):
                        wait(dve, gathered[n][s], landed(t, s, 4))
                    nc.vector.tensor_tensor(raw[s][:, :], part[0][s][:, 0:HEADS], part[1][s][:, HEADS:],
                                            ALU.add).then_inc(raw_made, 1)
                    wait(dve, raw_made, t + 1)
                    nc.vector.scalar_tensor_tensor(scores[:, bass.ds(t, 1), :].rearrange("p o h -> p (o h)"),
                                                   raw[s][:, :], 0.2, raw[s][:, :], ALU.mult, ALU.max).then_inc(scored, 1)

                over_tiles(dve, NET, 4, (0, score))
                dve.wait_ge(scored, NET)

        key, same_p, same_n = (st.sb(n, [P, GE]) for n in ("key", "same_p", "same_n"))
        with_p, with_n = st.sb("with_p", [P, GE]), st.sb("with_n", [P, GE])
        sT, fwd, bwd, ex, tmp = (st.sb(n, [P, GE]) for n in ("sT", "fwd", "bwd", "ex", "tmp"))
        alpha = st.sb("alpha", [P, GE])
        key_in = st.sb("key_in", [P, GT, P])
        row, row2 = st.sb("row", [1, 4, P]), st.sb("row2", [1, 4, P])
        link = st.sb("link", [1, 2, P])
        ends, nears = st.sb("ends", [P, 4]), st.sb("nears", [P, 4])
        p_s = [st.ps(f"p_s{i}") for i in range(GT)]
        p_row, p_col = st.ps("p_row"), st.ps("p_col")
        ready, keys_turned, keys_read, turned = (st.sem(n) for n in ("ready", "keys_turned", "keys_read", "turned"))
        step, rows_made, rows_read, cols_made = (st.sem(n) for n in ("step", "rows_made", "rows_read", "cols_made"))
        less_max, summed = st.sem("less_max"), st.sem("summed")
        exp_made, log_made, inv_made, alpha_made, alpha_turned = (
            st.sem(n) for n in ("exp_made", "log_made", "inv_made", "alpha_made", "alpha_turned"))

        def of_tile(v, j):
            return v[:, j * P:(j + 1) * P]

        with nc.Block() as block:
            @block.tensor
            def _(pe):
                pe.wait_ge(ready, 1)
                for j in range(GT):
                    ins = nc.tensor.transpose(p_s[j][:, 0:P], key_in[:, j, :], c["ident"][:, :])
                ins.then_inc(keys_turned, 1)
                pe.wait_ge(keys_read, 1)
                pe.wait_ge(ready, 2)
                for j in range(GT):
                    ins = nc.tensor.transpose(p_s[j][:, 0:P], key_in[:, j, :], c["ident"][:, :])
                ins.then_inc(turned, 1)
                for turn in range(2):
                    pe.wait_ge(rows_made, 2 * turn + 1)
                    for n in range(4):
                        ins = nc.tensor.transpose(p_row[0:1, n * P:(n + 1) * P], ends[:, n:n + 1], c["ident"][:, :])
                    ins.then_inc(rows_read, 1)
                    pe.wait_ge(rows_made, 2 * turn + 2)
                    for n in range(4):
                        ins = nc.tensor.transpose(p_col[:, n:n + 1], row2[:, n, :], c["ident"][0:1, 0:1])
                    ins.then_inc(cols_made, 1)
                pe.wait_ge(alpha_made, 1)
                for j in range(GT):
                    ins = nc.tensor.transpose(p_s[j][:, 0:P], of_tile(alpha, j), c["ident"][:, :])
                ins.then_inc(alpha_turned, 1)

            @block.scalar
            def _(act):
                act.wait_ge(less_max, 1)
                nc.scalar.activation(ex[:, :], sT[:, :], ACT.Exp).then_inc(exp_made, 1)
                act.wait_ge(summed, 1)
                nc.scalar.activation(fwd[:, :], fwd[:, :], ACT.Ln).then_inc(log_made, 1)
                act.wait_ge(log_made, 1)
                nc.scalar.activation(fwd[:, :], fwd[:, :], ACT.Exp, scale=-1.0).then_inc(inv_made, 1)

            @block.vector
            def _(dve):
                done = [0]

                def then(ins):
                    done[0] += 1
                    ins.then_inc(step, 1)
                    dve.wait_ge(step, done[0])

                V = nc.vector
                for j in range(GT):
                    ins = V.tensor_copy(key_in[:, j, :].rearrange("p (g h) -> p g h", h=HEADS),
                                        c["keys"][:, j::GT].unsqueeze(2).to_broadcast([P, GROUPS, HEADS]))
                ins.then_inc(ready, 1)
                dve.wait_ge(keys_turned, 1)
                for j in range(GT):
                    ins = V.tensor_copy(of_tile(key, j), p_s[j][:, 0:P])
                ins.then_inc(keys_read, 1)
                for j in range(GT):
                    ins = V.tensor_copy(key_in[:, j, :].rearrange("p (g h) -> p g h", h=HEADS), scores[:, j::GT, :])
                ins.then_inc(ready, 1)
                V.memset(same_p[:, 0:1], 0.0)
                V.memset(same_n[:, GE - 1:GE], 0.0)
                dve.wait_ge(keys_read, 1)
                V.tensor_tensor(same_p[:, 1:GE], key[:, 1:GE], key[:, 0:GE - 1], ALU.is_equal)
                then(V.tensor_tensor(same_n[:, 0:GE - 1], key[:, 1:GE], key[:, 0:GE - 1], ALU.is_equal))
                dve.wait_ge(turned, 1)
                for j in range(GT):
                    ins = V.tensor_copy(of_tile(sT, j), p_s[j][:, 0:P])
                then(ins)

                def ends_of_groups(first):
                    V.tensor_copy(ends[:, 0:1], fwd[:, GE - 1:GE])
                    V.tensor_copy(ends[:, 1:2], key[:, GE - 1:GE])
                    V.tensor_copy(ends[:, 2:3], bwd[:, 0:1])
                    V.tensor_copy(ends[:, 3:4], key[:, 0:1]).then_inc(rows_made, 1)
                    dve.wait_ge(rows_read, 1 if first else 2)
                    for n in range(4):
                        ins = V.tensor_copy(row[:, n, :].rearrange("o (h g) -> o h g", h=HEADS),
                                            p_row[0:1, n * P:(n + 1) * P].rearrange("o (g h) -> o h g", h=HEADS))
                    then(ins)
                    V.tensor_tensor(link[:, 0, 1:P], row[:, 1, 1:P], row[:, 1, 0:P - 1], ALU.is_equal)
                    then(V.tensor_tensor(link[:, 1, 0:P - 1], row[:, 3, 1:P], row[:, 3, 0:P - 1], ALU.is_equal))
                    V.memset(link[:, 0, 0:P:GROUPS], 0.0)
                    then(V.memset(link[:, 1, GROUPS - 1:P:GROUPS], 0.0))
                    if first:
                        then(V.tensor_scalar(link[:, :, :], link[:, :, :], -1.0, BIG, ALU.add, ALU.mult))
                    ops = (ALU.add, ALU.max) if first else (ALU.mult, ALU.add)
                    none = -BIG if first else 0.0
                    V.tensor_tensor_scan(row[:, 0, :], link[:, 0, :], row[:, 0, :], none, *ops)
                    then(V.tensor_tensor_scan(row[:, 2, ::-1], link[:, 1, ::-1], row[:, 2, ::-1], none, *ops))
                    for n, fill in ((0, none), (1, -1.0), (2, none), (3, -1.0)):
                        back = row2[:, n, :].rearrange("o (g h) -> o h g", h=HEADS)
                        mine = row[:, n, :].rearrange("o (h g) -> o h g", h=HEADS)
                        if n < 2:
                            V.tensor_copy(back[:, :, 1:GROUPS], mine[:, :, 0:GROUPS - 1])
                            V.memset(row2[:, n, 0:HEADS], fill)
                        else:
                            V.tensor_copy(back[:, :, 0:GROUPS - 1], mine[:, :, 1:GROUPS])
                            ins = V.memset(row2[:, n, P - HEADS:P], fill)
                    ins.then_inc(rows_made, 1)
                    dve.wait_ge(cols_made, 1 if first else 2)
                    then(V.tensor_copy(nears[:, :], p_col[:, 0:4]))

                V.tensor_scalar(with_p[:, :], same_p[:, :], -1.0, BIG, ALU.add, ALU.mult)
                then(V.tensor_scalar(with_n[:, :], same_n[:, :], -1.0, BIG, ALU.add, ALU.mult))
                V.tensor_tensor_scan(fwd[:, :], with_p[:, :], sT[:, :], -BIG, ALU.add, ALU.max)
                then(V.tensor_tensor_scan(bwd[:, ::-1], with_n[:, ::-1], sT[:, ::-1], -BIG, ALU.add, ALU.max))
                ends_of_groups(True)
                V.tensor_scalar(with_p[:, :], key[:, :], nears[:, 1:2], None, ALU.is_equal)
                then(V.tensor_scalar(with_n[:, :], key[:, :], nears[:, 3:4], None, ALU.is_equal))
                then(V.tensor_tensor(fwd[:, :], fwd[:, :], bwd[:, :], ALU.max))
                for near, at in ((with_p, 0), (with_n, 2)):
                    then(V.tensor_scalar(tmp[:, :], near[:, :], -1.0, BIG, ALU.add, ALU.mult))
                    then(V.scalar_tensor_tensor(fwd[:, :], tmp[:, :], nears[:, at:at + 1], fwd[:, :], ALU.add, ALU.max))
                V.tensor_tensor(sT[:, :], sT[:, :], fwd[:, :], ALU.subtract).then_inc(less_max, 1)
                dve.wait_ge(exp_made, 1)
                V.tensor_tensor_scan(fwd[:, :], same_p[:, :], ex[:, :], 0.0, ALU.mult, ALU.add)
                then(V.tensor_tensor_scan(bwd[:, ::-1], same_n[:, ::-1], ex[:, ::-1], 0.0, ALU.mult, ALU.add))
                ends_of_groups(False)
                then(V.tensor_tensor(fwd[:, :], fwd[:, :], bwd[:, :], ALU.add))
                then(V.tensor_tensor(fwd[:, :], fwd[:, :], ex[:, :], ALU.subtract))
                then(V.scalar_tensor_tensor(fwd[:, :], with_p[:, :], nears[:, 0:1], fwd[:, :], ALU.mult, ALU.add))
                V.scalar_tensor_tensor(fwd[:, :], with_n[:, :], nears[:, 2:3], fwd[:, :],
                                       ALU.mult, ALU.add).then_inc(summed, 1)
                dve.wait_ge(inv_made, 1)
                V.tensor_tensor(alpha[:, :], ex[:, :], fwd[:, :], ALU.mult).then_inc(alpha_made, 1)
                dve.wait_ge(alpha_turned, 1)
                for j in range(GT):
                    V.tensor_copy(weights[:, j::GT, :], p_s[j][:, 0:P].rearrange("p (g h) -> p g h", h=HEADS))


class TurnedWeights:

    def __init__(self, nc, st, c, name):
        self.nc, self.ident = nc, c["ident"]
        self.w_in = st.sb(name + "_in", [P, KC, D])
        self.halves = Halves(st, name, [P, KC, D], 1)
        self.landed, self.turned = st.sem(name + "_landed"), st.sem(name + "_turned")

    def load(self, sp, W):
        sp.dma_start(self.w_in[:, :, :], W.rearrange("(k p) n -> p k n", p=P)).then_inc(self.landed, 16)

    def turn(self, pe, banks):
        pe.wait_ge(self.landed, 16)
        for k in range(KC):
            wait(pe, self.halves.made, k - 1)
            for m in range(KC):
                ins = self.nc.tensor.transpose(banks[k % 2][:, m * P:(m + 1) * P], self.w_in[:, m, k * P:(k + 1) * P],
                                               self.ident[:, :])
            ins.then_inc(self.turned, 1)
        pe.wait_ge(self.halves.made, KC)

    def copy(self, act, banks):
        for k in range(KC):
            act.wait_ge(self.turned, k + 1)
            self.nc.scalar.copy(self.halves.hi[0][:, k, :], banks[k % 2][:, :]).then_inc(self.halves.hi_made, 1)

    def rest(self, dve, banks):
        for k in range(KC):
            dve.wait_ge(self.halves.hi_made, k + 1)
            self.nc.vector.tensor_tensor(self.halves.lo[0][:, k, :], banks[k % 2][:, :], self.halves.hi[0][:, k, :],
                                         ALU.subtract).then_inc(self.halves.made, 1)


def combine(nc, c, x2, sums, W_self, b, x3, from_x3):
    with Stage(nc, "combine") as st:
        w = TurnedWeights(nc, st, c, "w")
        bias = st.sb("bias", [P, D])
        xt, res = st.slots(st.sb, "xt", 4, [P, D]), st.slots(st.sb, "res", 4, [P, D])
        xT, out = Halves(st, "xT", [P, KC, P]), st.slots(st.sb, "out", 2, [P, D])
        p_turn, p_out = st.slots(st.ps, "p_turn", 2), st.slots(st.ps, "p_out", 2)
        bias_in = st.sem("bias_in")
        x_in, stored = st.slots(st.sem, "x_in", 4), st.slots(st.sem, "stored", 4)
        out_stored = st.slots(st.sem, "out_stored", 2)
        summed, turned, product, out_made = (st.sem(n) for n in ("summed", "turned", "product", "out_made"))
        agg = NodeGather(nc, st, c, sums, summed)
        norm = LayerNorm(nc, st, c, "norm", 4)

        with nc.Block() as block:
            @block.sync
            def _(sp):
                w.load(sp, W_self)
                sp.dma_start(bias[:, :], row_of_all(b)).then_inc(bias_in, 16)

                def load(t, s):
                    wait(sp, norm.made, t - 3)
                    sp.dma_start(xt[s][:, :], rows(x2, t)).then_inc(x_in[s], 16)

                def store(t, s):
                    wait(sp, norm.made, t + 1)
                    sp.dma_start(rows(x3, t), res[s][:, :]).then_inc(stored[s], 16)

                def store_out(t, s):
                    wait(sp, out_made, t + 1)
                    sp.dma_start(rows(from_x3, t), out[s % 2][:, :]).then_inc(out_stored[s % 2], 16)

                over_tiles(sp, NT, 4, (0, load), (4, store), (7, store_out))
                for s in range(4):
                    sp.wait_ge(stored[s], 16 * len(range(s, NT, 4)))
                for s in range(2):
                    sp.wait_ge(out_stored[s], 16 * len(range(s, NT, 2)))

            @block.gpsimd
            def _(pool):
                def add(t, s):
                    wait(pool, x_in[s], landed(t, s, 4))
                    wait(pool, agg.landed[s], landed(t, s, 4))
                    nc.gpsimd.tensor_tensor(xt[s][:, :], xt[s][:, :], agg.rows[s][:, :], ALU.add).then_inc(summed, 1)

                over_tiles(pool, NT, 4, (0, lambda t, s: agg.stage_and_gather(pool, t, s)), (3, add))

            @block.vector
            def _(dve):
                dve.wait_ge(bias_in, 16)
                w.rest(dve, p_out)

                def sums_of(t, s):
                    wait(dve, summed, t + 1)
                    norm.sums(dve, xt[s][:, :], t, s)

                def scale(t, s):
                    wait(dve, turned, t - 3)
                    wait(dve, stored[s], landed(t, s, 4) - 16)
                    norm.scale(dve, res[s][:, :], xt[s][:, :], t, s)

                def rest(t, s):
                    wait(dve, xT.hi_made, t + 1)
                    wait(dve, product, t - 1)
                    rest_of_blocks(nc, xT.lo[s % 2][:, :, :], p_turn[s % 2], xT.hi[s % 2][:, :, :]).then_inc(xT.made, 1)

                def evacuate(t, s):
                    wait(dve, product, t + 1)
                    wait(dve, out_stored[s % 2], landed(t, s % 2, 2) - 16)
                    nc.vector.tensor_tensor(out[s % 2][:, :], p_out[s % 2][:, :], bias[:, :], ALU.add).then_inc(out_made, 1)

                over_tiles(dve, NT, 4, (4, scale), (3, sums_of), (7, evacuate), (5, rest))

            @block.scalar
            def _(act):
                w.copy(act, p_out)

                def copy_turned(t, s):
                    wait(act, turned, t + 1)
                    wait(act, product, t - 1)
                    copy_blocks(nc, xT.hi[s % 2][:, :, :], p_turn[s % 2]).then_inc(xT.hi_made, 1)

                over_tiles(act, NT, 4, (3, lambda t, s: norm.root(act, t, s)), (5, copy_turned))

            @block.tensor
            def _(pe):
                w.turn(pe, p_out)

                def turn(t, s):
                    wait(pe, norm.made, t + 1)
                    wait(pe, xT.made, t - 1)
                    turn_blocks(nc, c, p_turn[s % 2], res[s]).then_inc(turned, 1)

                def multiply(t, s):
                    wait(pe, xT.made, t + 1)
                    wait(pe, out_made, t - 1)
                    multiply_halves(nc, p_out[s % 2][:, :], xT, s % 2, range(KC), w.halves, range(KC)).then_inc(product, 1)

                over_tiles(pe, NT, 4, (5, turn), (6, multiply))


def last_layer(nc, c, x3, from_x3, sums, W_neigh, out):
    with Stage(nc, "last") as st:
        w = TurnedWeights(nc, st, c, "w")
        xt, fx = st.slots(st.sb, "xt", 4, [P, D]), st.slots(st.sb, "fx", 4, [P, D])
        aT = Halves(st, "aT", [P, KC, P])
        v, res = st.slots(st.sb, "v", 4, [P, D]), st.slots(st.sb, "res", 2, [P, D])
        p_agg, p_out = st.slots(st.ps, "p_agg", 2), st.slots(st.ps, "p_out", 2)
        x_in, fx_in, stored = (st.slots(st.sem, "x_in", 4), st.slots(st.sem, "fx_in", 4),
                               st.slots(st.sem, "stored", 2))
        turned, product, v_step, summed = (st.sem(n) for n in ("turned", "product", "v_step", "summed"))
        agg = NodeGather(nc, st, c, sums, turned)
        norm = LayerNorm(nc, st, c, "norm")

        with nc.Block() as block:
            @block.sync
            def _(sp):
                w.load(sp, W_neigh)

                def load(t, s):
                    wait(sp, summed, t - 3)
                    sp.dma_start(fx[s][:, :], rows(from_x3, t)).then_inc(fx_in[s], 16)
                    sp.dma_start(xt[s][:, :], rows(x3, t)).then_inc(x_in[s], 16)

                def store(t, s):
                    wait(sp, norm.made, t + 1)
                    if isinstance(t, int) and t == NT - 1:
                        sp.dma_start(out[t * P:N, :], res[s % 2][0:LAST, :]).then_inc(stored[s % 2], 16)
                    else:
                        sp.dma_start(rows(out, t), res[s % 2][:, :]).then_inc(stored[s % 2], 16)

                over_tiles(sp, NT, 4, (2, load), (7, store))
                for s in range(2):
                    sp.wait_ge(stored[s], 16 * len(range(s, NT, 2)))

            @block.gpsimd
            def _(pool):
                over_tiles(pool, NT, 4, (0, lambda t, s: agg.stage_and_gather(pool, t, s)))

            @block.vector
            def _(dve):
                w.rest(dve, p_out)

                def rest(t, s):
                    wait(dve, aT.hi_made, t + 1)
                    wait(dve, product, t - 1)
                    rest_of_blocks(nc, aT.lo[s % 2][:, :, :], p_agg[s % 2], aT.hi[s % 2][:, :, :]).then_inc(aT.made, 1)

                def add_up(t, s):
                    wait(dve, product, t + 1)
                    wait(dve, fx_in[s], landed(t, s, 4))
                    nc.vector.scalar_tensor_tensor(v[s][:, :], p_out[s % 2][:, :], c["inv_deg"][:, bass.ds(t, 1)],
                                                   fx[s][:, :], ALU.mult, ALU.add).then_inc(v_step, 1)

                def activate(t, s):
                    wait(dve, x_in[s], landed(t, s, 4))
                    wait(dve, v_step, t + 1)
                    nc.vector.scalar_tensor_tensor(v[s][:, :], v[s][:, :], 0.0, xt[s][:, :],
                                                   ALU.max, ALU.add).then_inc(summed, 1)

                def sums_of(t, s):
                    wait(dve, summed, t + 1)
                    norm.sums(dve, v[s][:, :], t, s % 2)

                def scale(t, s):
                    wait(dve, stored[s % 2], landed(t, s % 2, 2) - 16)
                    norm.scale(dve, res[s % 2][:, :], v[s][:, :], t, s % 2)

                over_tiles(dve, NT, 4, (5, add_up), (6, scale), (5, activate), (3, rest), (5, sums_of))

            @block.scalar
            def _(act):
                w.copy(act, p_out)

                def copy_turned(t, s):
                    wait(act, turned, t + 1)
                    wait(act, product, t - 1)
                    copy_blocks(nc, aT.hi[s % 2][:, :, :], p_agg[s % 2]).then_inc(aT.hi_made, 1)

                over_tiles(act, NT, 4, (3, copy_turned), (5, lambda t, s: norm.root(act, t, s % 2)))

            @block.tensor
            def _(pe):
                w.turn(pe, p_out)

                def turn(t, s):
                    wait(pe, agg.landed[s], landed(t, s, 4))
                    wait(pe, aT.made, t - 1)
                    turn_blocks(nc, c, p_agg[s % 2], agg.rows[s]).then_inc(turned, 1)

                def multiply(t, s):
                    wait(pe, aT.made, t + 1)
                    wait(pe, v_step, t - 1)
                    multiply_halves(nc, p_out[s % 2][:, :], aT, s % 2, range(KC), w.halves, range(KC)).then_inc(product, 1)

                over_tiles(pe, NT, 4, (3, turn), (4, multiply))


def build(nc, ins, out):
    with ExitStack() as ctx:
        def sb(name, shape, dt=F32):
            return ctx.enter_context(nc.sbuf_tensor("all_" + name, shape, dt))

        def dram(name, shape, dt=F32):
            return nc.dram_tensor(name, shape, dt).ap()

        SEMS[:] = [ctx.enter_context(nc.semaphore(f"signal{i}")) for i in range(DMA_SIGNALS + SIGNALS)]
        ids = [s.num for s in SEMS]
        assert max(ids) - min(ids) == len(ids) - 1 and sorted(ids) in (ids, ids[::-1])
        DMA_SEMS[:], SEMS[:] = SEMS[:DMA_SIGNALS], SEMS[DMA_SIGNALS:]

        c = {n: sb(n, [P, P]) for n in ("ident", "ones", "below", "upto", "count")}
        for n in ("has_edges", "inv_deg", "sum_row"):
            c[n] = sb(n, [P, NT])
        c["sum_row_i"] = sb("sum_row_i", [P, NT], I32)
        for n in ("src_list", "dst_list"):
            c[n] = sb(n, [P, NET], I32)
        c["join"], c["join_row"] = sb("join", [NET, NET]), sb("join_row", [NET, 1])
        c["join_row_i"] = sb("join_row_i", [NET, 1], I32)
        c["keys"] = sb("keys", [P, GROUPS * GT])
        c["same"] = sb("same", [P, NET, P], BF16)
        c["two"], c["eps"] = sb("two", [P, 1]), sb("eps", [P, 1])
        sorted_edges, edge_keys = dram("sorted_edges", [NSORT, REC]), dram("edge_keys", [NET, P])
        from_src, from_dst, from_x = (dram(n, [NP, D]) for n in ("from_src", "from_dst", "from_x"))
        sums = [dram(f"sums{n}", [ZROW + 1, D]) for n in range(4)]
        x1, x2, x3, from_x3, y, wx = (dram(n, [NP, D]) for n in ("x1", "x2", "x3", "from_x3", "y", "wx"))
        uv = dram("uv", [NP, 2 * HEADS])
        x = ins["x"]

        make_constants(nc, c)
        sort_and_multiply(nc, c, ins["src"], ins["dst"], ins["edge_attr_64"], sorted_edges, x,
                          *(ins["L0_gnn_" + n] for n in ("W1", "b1", "W3", "b3")), (from_src, from_dst, from_x))
        list_edges(nc, c, sorted_edges, edge_keys)
        edge_messages(nc, c, from_src, from_dst, sorted_edges, *(ins["L0_gnn_" + n] for n in ("W1", "W2", "b2")), sums[0])
        with nc.sbuf_tensor("stats", [P, KC, NT, 6], F32) as stats, \
                nc.sbuf_tensor("first_rows", [P, D], F32) as first_rows, \
                nc.sbuf_tensor("other_rows", [P, D], F32) as other_rows:
            update_nodes(nc, c, x, from_x, sums[0], *(ins["L0_gnn_" + n] for n in ("W3", "W4", "b4", "gamma", "beta")),
                         x1, stats)
            attention(nc, c, x1, *(ins["L1_gnn_" + n] for n in ("Wq", "Wk", "Wv", "Wo", "proj")),
                      first_rows[:, :], other_rows[:, :])
            segment_sums(nc, c, "sums1", x1, sums[1])
            with nc.sbuf_tensor("stats2", [P, KC, NT, 6], F32) as stats2:
                conv_nodes(nc, c, x1, sums[1], *(ins["L1_gnn_" + n] for n in ("W_conv", "b_conv", "norm1_g", "norm1_b")),
                           stats, first_rows[:, :], other_rows[:, :], y, stats2)
                head_products(nc, c, x1, y, ins["L1_gnn_norm2_g"], ins["L1_gnn_norm2_b"], stats2,
                              *(ins["L2_gnn_" + n] for n in ("Ws", "Wb", "a_w", "a_b")), x2, wx, uv)
        with nc.sbuf_tensor("weights", [P, GROUPS * GT, HEADS], F32) as weights:
            edge_softmax(nc, c, uv, weights)
            segment_sums(nc, c, "sums2", wx, sums[2], weights)
        combine(nc, c, x2, sums[2], ins["L3_gnn_W_self"], ins["L3_gnn_b"], x3, from_x3)
        segment_sums(nc, c, "sums3", x3, sums[3])
        last_layer(nc, c, x3, from_x3, sums[3], ins["L3_gnn_W_neigh"], out)


def kernel(**inputs):
    import numpy as _np
    import concourse.bacc as _bacc
    from concourse import mybir as _mybir
    from concourse.bass_utils import run_bass_kernel_spmd as _run

    nc = _bacc.Bacc("TRN2", target_bir_lowering=False, num_devices=1)
    arrays, args = {}, {}
    for name in inputs:
        a = _np.ascontiguousarray(inputs[name])
        arrays[f"in_{name}_dram"] = a
        args[name] = nc.dram_tensor(f"in_{name}_dram", a.shape, _mybir.dt.from_np(a.dtype), kind="ExternalInput").ap()
    out = nc.dram_tensor("out_0_dram", (N, D), F32, kind="ExternalOutput").ap()
    build(nc, args, out)
    r = _run(nc, [arrays], core_ids=[0])
    return r.results[0]["out_0_dram"]
```
